# Optimizing a Trainium2 kernel written in Bass

```python
import numpy as np
import jax
import jax.numpy as jnp

def _softmax(x, axis=-1):
    return jax.nn.softmax(x, axis=axis)

def _gelu(x):
    return jax.nn.gelu(x, approximate=True)

def _silu(x):
    return jax.nn.silu(x)

def _sigmoid(x):
    return jax.nn.sigmoid(x)

def _layernorm(x, axis=-1, eps=1e-05):
    m = jnp.mean(x, axis=axis, keepdims=True)
    v = jnp.var(x, axis=axis, keepdims=True)
    return (x - m) / jnp.sqrt(v + eps)

def _scatter_add(tgt, idx, src, axis=0):
    return tgt.at[idx].add(src)

def _segment_sum(src, seg, n):
    return jax.ops.segment_sum(src, seg, n)
kernel_name = 'mk_decoder_preln_d2_seqx_r8_a4a921'

def setup_inputs(seed: int=0):
    np.random.seed(seed)
    _w = jnp.asarray

    def _rec_inputs():
        import jax
        import jax.numpy as jnp
        _rk = jax.random.key(seed)
        x = 7.22e-05 + 1 * jax.random.normal(jax.random.fold_in(_rk, 1), (4, 256, 128), jnp.float32)
        _lenS = 256 - jax.random.randint(jax.random.fold_in(_rk, 7), (4,), 0, max(1, 256 // 4) + 1, jnp.int32)
        _lenS2 = 256 - jax.random.randint(jax.random.fold_in(_rk, 8), (4,), 0, max(1, 256 // 4) + 1, jnp.int32)
        _ctx_1024P = jax.random.normal(jax.random.fold_in(_rk, 11), (4, 16, 128), jnp.float32)
        _ctx_1024c = jax.random.dirichlet(jax.random.fold_in(_rk, 511), 0.3 * jnp.ones((16,), jnp.float32), (4, 256))
        _ctx_1024t = jnp.einsum('bsk,bkd->bsd', _ctx_1024c, _ctx_1024P)
        _ctx_1024t = _ctx_1024t * jax.lax.rsqrt(jnp.mean(jnp.square(_ctx_1024t)) + 1e-12) * 0.953939
        ctx_1024 = 4.13588e-05 + 0.999923 * (_ctx_1024t + 0.3 * jax.random.normal(jax.random.fold_in(_rk, 611), (4, 256, 128), jnp.float32))
        _validS = jnp.arange(256)[None, :] < _lenS[:, None]
        _validS2 = jnp.arange(256)[None, :] < _lenS2[:, None]
        _causal = jnp.tril(jnp.ones((256, 256), dtype=bool))
        mask_BxS_ik0 = jnp.where(jnp.broadcast_to(_validS[:, :], (4, 256)), 0, 1).astype(jnp.int32)
        return (x, ctx_1024, mask_BxS_ik0)
    x, ctx_1024, mask_BxS_ik0 = _rec_inputs()

    def _L0_attn_setup():
        import jax, jax.numpy as jnp
        import numpy as np
        E = 128
        H = 16
        D = E // H
        M = 4 * D
        B, N = (4, 512)
        KERNEL_EPS = 0.0001

        def softmax_kernel(data, proj, is_query):
            d = data.shape[-1]
            data_n = data * d ** (-0.25)
            ratio = proj.shape[0] ** (-0.5)
            dd = jnp.einsum('bhnd,md->bhnm', data_n, proj)
            diag = 0.5 * jnp.sum(data_n * data_n, axis=-1, keepdims=True)
            if is_query:
                stab = jnp.max(dd, axis=-1, keepdims=True)
            else:
                stab = jnp.max(dd)
            return ratio * (jnp.exp(dd - diag - stab) + KERNEL_EPS)
        key = jax.random.key(seed)
        ks = jax.random.split(key, 7)
        s = E ** (-0.5)
        return {'x': jax.random.normal(ks[0], (B, N, E), jnp.float32), 'Wq': jax.random.normal(ks[1], (E, E), jnp.float32) * s, 'bq': jnp.zeros((E,), jnp.float32), 'Wk': jax.random.normal(ks[2], (E, E), jnp.float32) * s, 'bk': jnp.zeros((E,), jnp.float32), 'Wv': jax.random.normal(ks[3], (E, E), jnp.float32) * s, 'bv': jnp.zeros((E,), jnp.float32), 'Wo': jax.random.normal(ks[4], (E, E), jnp.float32) * s, 'bo': jnp.zeros((E,), jnp.float32), 'proj': jax.random.normal(ks[5], (M, D), jnp.float32)}
    _L0_attn_all = _L0_attn_setup()
    _L0_attn_in = {k: v for k, v in _L0_attn_all.items() if k in ('Wq', 'bq', 'Wk', 'bk', 'Wv', 'bv', 'Wo', 'bo', 'proj')}
    del _L0_attn_all

    def _L0_xattn_setup():
        import jax, jax.numpy as jnp
        import numpy as np
        HEADS = 16
        HIDDEN = 128
        DH = HIDDEN // HEADS
        STD = 0.02

        def _split_heads(x):
            B, S, _ = x.shape
            return x.reshape(B, S, HEADS, DH).transpose(0, 2, 1, 3)
        key = jax.random.key(seed)
        ks = jax.random.split(key, 12)
        B, S = (4, 256)
        inp = {'q': jax.random.normal(ks[0], (B, S, HIDDEN), jnp.float32), 'k': jax.random.normal(ks[1], (B, S, HIDDEN), jnp.float32), 'v': jax.random.normal(ks[2], (B, S, HIDDEN), jnp.float32), 'mask': jax.random.randint(ks[3], (B, S), 0, 2, jnp.int32), 'wq': STD * jax.random.normal(ks[4], (HIDDEN, HIDDEN), jnp.float32), 'bq': jnp.zeros((HIDDEN,), jnp.float32), 'wk': STD * jax.random.normal(ks[5], (HIDDEN, HIDDEN), jnp.float32), 'bk': jnp.zeros((HIDDEN,), jnp.float32), 'wv': STD * jax.random.normal(ks[6], (HIDDEN, HIDDEN), jnp.float32), 'bv': jnp.zeros((HIDDEN,), jnp.float32), 'wo': STD * jax.random.normal(ks[7], (HIDDEN, HIDDEN), jnp.float32), 'bo': jnp.zeros((HIDDEN,), jnp.float32)}
        return inp
    _L0_xattn_all = _L0_xattn_setup()
    _L0_xattn_in = {k: v for k, v in _L0_xattn_all.items() if k in ('wq', 'bq', 'wk', 'bk', 'wv', 'bv', 'wo', 'bo')}
    del _L0_xattn_all

    def _L0_ffn_setup():
        import jax, jax.numpy as jnp
        import numpy as np
        D = 128
        LW = 16
        DEPTH = 8
        NN = 2 ** DEPTH - 1
        NL = 2 ** DEPTH
        B, S = (2, 128)

        def _fff(x, nw, nb, w1, b1, w2, b2, act):
            node = jnp.zeros(x.shape[:2], dtype=jnp.int32)
            for _ in range(DEPTH):
                logit = jnp.einsum('bsd,bsd->bs', x, nw[node]) + nb[node]
                node = 2 * node + 1 + (logit > 0).astype(jnp.int32)
            leaf = node - NN
            h = act(jnp.einsum('bsd,bsdl->bsl', x, w1[leaf]) + b1[leaf])
            return jnp.einsum('bsl,bsld->bsd', h, w2[leaf]) + b2[leaf]

        def _forward(x, q_nw, q_nb, q_w1, q_b1, q_w2, q_b2, k_nw, k_nb, k_w1, k_b1, k_w2, k_b2, v_nw, v_nb, v_w1, v_b1, v_w2, v_b2, f_nw, f_nb, f_w1, f_b1, f_w2, f_b2):
            mu = jnp.mean(x, -1, keepdims=True)
            sd = jnp.std(x, -1, ddof=1, keepdims=True)
            xn = (x - mu) / jnp.sqrt(sd + 1e-05)
            relu = jax.nn.relu
            q = _fff(xn, q_nw, q_nb, q_w1, q_b1, q_w2, q_b2, relu)
            k = _fff(xn, k_nw, k_nb, k_w1, k_b1, k_w2, k_b2, relu)
            v = _fff(xn, v_nw, v_nb, v_w1, v_b1, v_w2, v_b2, relu)
            att = jax.nn.softmax(jnp.einsum('bqd,bkd->bqk', q, k) / jnp.sqrt(jnp.float32(D)), axis=-1)
            y = xn + jnp.einsum('bqk,bkd->bqd', att, v)
            gelu = lambda t: jax.nn.gelu(t, approximate=False)
            return y + _fff(y, f_nw, f_nb, f_w1, f_b1, f_w2, f_b2, gelu)

        def _make_fff_params(key, scale_in, scale_leaf):
            ks = jax.random.split(key, 4)
            nw = jax.random.normal(ks[0], (NN, D), jnp.float32) * scale_in
            nb = jnp.zeros((NN,), jnp.float32)
            w1 = jax.random.normal(ks[1], (NL, D, LW), jnp.float32) * scale_in
            b1 = jax.random.normal(ks[2], (NL, LW), jnp.float32) * 0.01
            w2 = jax.random.normal(ks[3], (NL, LW, D), jnp.float32) * scale_leaf
            b2 = jnp.zeros((NL, D), jnp.float32)
            return (nw, nb, w1, b1, w2, b2)
        key = jax.random.key(seed)
        kx, kq, kk, kv, kf = jax.random.split(key, 5)
        s_in = 1.0 / np.sqrt(D)
        s_lf = 1.0 / np.sqrt(LW)
        inp = {'x': jax.random.normal(kx, (B, S, D), jnp.float32)}
        for name, kk_ in (('q', kq), ('k', kk), ('v', kv), ('f', kf)):
            nw, nb, w1, b1, w2, b2 = _make_fff_params(kk_, s_in, s_lf)
            inp.update({f'{name}_nw': nw, f'{name}_nb': nb, f'{name}_w1': w1, f'{name}_b1': b1, f'{name}_w2': w2, f'{name}_b2': b2})
        return inp
    _L0_ffn_all = _L0_ffn_setup()
    _L0_ffn_in = {k: v for k, v in _L0_ffn_all.items() if k in ('q_nw', 'q_nb', 'q_w1', 'q_b1', 'q_w2', 'q_b2', 'k_nw', 'k_nb', 'k_w1', 'k_b1', 'k_w2', 'k_b2', 'v_nw', 'v_nb', 'v_w1', 'v_b1', 'v_w2', 'v_b2', 'f_nw', 'f_nb', 'f_w1', 'f_b1', 'f_w2', 'f_b2')}
    del _L0_ffn_all

    def _L1_attn_setup():
        import jax, jax.numpy as jnp
        import numpy as np
        import math
        NUM_HEADS = 16
        key = jax.random.key(seed)
        ks = jax.random.split(key, 5)
        d_model = 128
        std = math.sqrt(2.0 / (d_model + d_model))
        x = jax.random.normal(ks[0], (2, 256, d_model), dtype=jnp.float32)
        Wq = jax.random.normal(ks[1], (d_model, d_model), dtype=jnp.float32) * std
        Wk = jax.random.normal(ks[2], (d_model, d_model), dtype=jnp.float32) * std
        Wv = jax.random.normal(ks[3], (d_model, d_model), dtype=jnp.float32) * std
        Wo = jax.random.normal(ks[4], (d_model, d_model), dtype=jnp.float32) * std
        return {'x': x, 'Wq': Wq, 'Wk': Wk, 'Wv': Wv, 'Wo': Wo}
    _L1_attn_all = _L1_attn_setup()
    _L1_attn_in = {k: v for k, v in _L1_attn_all.items() if k in ('Wq', 'Wk', 'Wv', 'Wo')}
    del _L1_attn_all

    def _L1_xattn_setup():
        import jax, jax.numpy as jnp
        import numpy as np
        EMB = 128
        HEADS = 16
        HEAD_DIM = EMB // HEADS
        key = jax.random.key(seed)
        ks = jax.random.split(key, 7)
        B, Q, KV = (2, 256, 512)
        s = 1.0 / np.sqrt(EMB)
        return {'x': jax.random.normal(ks[0], (B, Q, EMB), dtype=jnp.float32), 'context': jax.random.normal(ks[1], (B, KV, EMB), dtype=jnp.float32), 'Wq': jax.random.normal(ks[2], (EMB, EMB), dtype=jnp.float32) * s, 'Wk': jax.random.normal(ks[3], (EMB, EMB), dtype=jnp.float32) * s, 'Wv': jax.random.normal(ks[4], (EMB, EMB), dtype=jnp.float32) * s, 'Wo': jax.random.normal(ks[5], (EMB, EMB), dtype=jnp.float32) * s, 'bo': jax.random.normal(ks[6], (EMB,), dtype=jnp.float32) * 0.01}
    _L1_xattn_all = _L1_xattn_setup()
    _L1_xattn_in = {k: v for k, v in _L1_xattn_all.items() if k in ('Wq', 'Wk', 'Wv', 'Wo', 'bo')}
    del _L1_xattn_all

    def _L1_ffn_setup():
        import jax, jax.numpy as jnp
        import numpy as np
        DIM = 128
        HEADS = 8
        NUM_EXPERTS = 8192
        NUM_KEYS = 32
        DIM_KEY = 64
        TOPK = 16

        def _rmsnorm(v, g):
            scale = jnp.sqrt(jnp.asarray(v.shape[-1], v.dtype))
            n = jnp.maximum(jnp.linalg.norm(v, axis=-1, keepdims=True), 1e-12)
            return v / n * g * scale
        key = jax.random.key(seed)
        ks = jax.random.split(key, 6)
        B, N = (2, 64)
        x = jax.random.normal(ks[0], (B, N, DIM), dtype=jnp.float32)
        gamma = jnp.ones((DIM,), dtype=jnp.float32)
        wq = jax.random.normal(ks[1], (2 * HEADS * DIM_KEY, DIM), dtype=jnp.float32) * 0.02
        keys = jax.random.normal(ks[2], (HEADS, NUM_KEYS, 2, DIM_KEY), dtype=jnp.float32) * 0.02
        table_down = jax.random.normal(ks[3], (NUM_EXPERTS, DIM), dtype=jnp.float32) * 0.02
        table_up = jax.random.normal(ks[4], (NUM_EXPERTS, DIM), dtype=jnp.float32) * 0.02
        return {'x': x, 'gamma': gamma, 'wq': wq, 'keys': keys, 'table_down': table_down, 'table_up': table_up}
    _L1_ffn_all = _L1_ffn_setup()
    _L1_ffn_in = {k: v for k, v in _L1_ffn_all.items() if k in ('gamma', 'wq', 'keys', 'table_down', 'table_up')}
    del _L1_ffn_all
    return {'x': x, 'ctx_1024': ctx_1024, 'mask_BxS_ik0': mask_BxS_ik0, 'L0_attn_Wq': _L0_attn_in['Wq'], 'L0_attn_bq': _L0_attn_in['bq'], 'L0_attn_Wk': _L0_attn_in['Wk'], 'L0_attn_bk': _L0_attn_in['bk'], 'L0_attn_Wv': _L0_attn_in['Wv'], 'L0_attn_bv': _L0_attn_in['bv'], 'L0_attn_Wo': _L0_attn_in['Wo'], 'L0_attn_bo': _L0_attn_in['bo'], 'L0_attn_proj': _L0_attn_in['proj'], 'L0_xattn_wq': _L0_xattn_in['wq'], 'L0_xattn_bq': _L0_xattn_in['bq'], 'L0_xattn_wk': _L0_xattn_in['wk'], 'L0_xattn_bk': _L0_xattn_in['bk'], 'L0_xattn_wv': _L0_xattn_in['wv'], 'L0_xattn_bv': _L0_xattn_in['bv'], 'L0_xattn_wo': _L0_xattn_in['wo'], 'L0_xattn_bo': _L0_xattn_in['bo'], 'L0_ffn_q_nw': _L0_ffn_in['q_nw'], 'L0_ffn_q_nb': _L0_ffn_in['q_nb'], 'L0_ffn_q_w1': _L0_ffn_in['q_w1'], 'L0_ffn_q_b1': _L0_ffn_in['q_b1'], 'L0_ffn_q_w2': _L0_ffn_in['q_w2'], 'L0_ffn_q_b2': _L0_ffn_in['q_b2'], 'L0_ffn_k_nw': _L0_ffn_in['k_nw'], 'L0_ffn_k_nb': _L0_ffn_in['k_nb'], 'L0_ffn_k_w1': _L0_ffn_in['k_w1'], 'L0_ffn_k_b1': _L0_ffn_in['k_b1'], 'L0_ffn_k_w2': _L0_ffn_in['k_w2'], 'L0_ffn_k_b2': _L0_ffn_in['k_b2'], 'L0_ffn_v_nw': _L0_ffn_in['v_nw'], 'L0_ffn_v_nb': _L0_ffn_in['v_nb'], 'L0_ffn_v_w1': _L0_ffn_in['v_w1'], 'L0_ffn_v_b1': _L0_ffn_in['v_b1'], 'L0_ffn_v_w2': _L0_ffn_in['v_w2'], 'L0_ffn_v_b2': _L0_ffn_in['v_b2'], 'L0_ffn_f_nw': _L0_ffn_in['f_nw'], 'L0_ffn_f_nb': _L0_ffn_in['f_nb'], 'L0_ffn_f_w1': _L0_ffn_in['f_w1'], 'L0_ffn_f_b1': _L0_ffn_in['f_b1'], 'L0_ffn_f_w2': _L0_ffn_in['f_w2'], 'L0_ffn_f_b2': _L0_ffn_in['f_b2'], 'L1_attn_Wq': _L1_attn_in['Wq'], 'L1_attn_Wk': _L1_attn_in['Wk'], 'L1_attn_Wv': _L1_attn_in['Wv'], 'L1_attn_Wo': _L1_attn_in['Wo'], 'L1_xattn_Wq': _L1_xattn_in['Wq'], 'L1_xattn_Wk': _L1_xattn_in['Wk'], 'L1_xattn_Wv': _L1_xattn_in['Wv'], 'L1_xattn_Wo': _L1_xattn_in['Wo'], 'L1_xattn_bo': _L1_xattn_in['bo'], 'L1_ffn_gamma': _L1_ffn_in['gamma'], 'L1_ffn_wq': _L1_ffn_in['wq'], 'L1_ffn_keys': _L1_ffn_in['keys'], 'L1_ffn_table_down': _L1_ffn_in['table_down'], 'L1_ffn_table_up': _L1_ffn_in['table_up']}

def reference(x, ctx_1024, mask_BxS_ik0, L0_attn_Wq, L0_attn_bq, L0_attn_Wk, L0_attn_bk, L0_attn_Wv, L0_attn_bv, L0_attn_Wo, L0_attn_bo, L0_attn_proj, L0_xattn_wq, L0_xattn_bq, L0_xattn_wk, L0_xattn_bk, L0_xattn_wv, L0_xattn_bv, L0_xattn_wo, L0_xattn_bo, L0_ffn_q_nw, L0_ffn_q_nb, L0_ffn_q_w1, L0_ffn_q_b1, L0_ffn_q_w2, L0_ffn_q_b2, L0_ffn_k_nw, L0_ffn_k_nb, L0_ffn_k_w1, L0_ffn_k_b1, L0_ffn_k_w2, L0_ffn_k_b2, L0_ffn_v_nw, L0_ffn_v_nb, L0_ffn_v_w1, L0_ffn_v_b1, L0_ffn_v_w2, L0_ffn_v_b2, L0_ffn_f_nw, L0_ffn_f_nb, L0_ffn_f_w1, L0_ffn_f_b1, L0_ffn_f_w2, L0_ffn_f_b2, L1_attn_Wq, L1_attn_Wk, L1_attn_Wv, L1_attn_Wo, L1_xattn_Wq, L1_xattn_Wk, L1_xattn_Wv, L1_xattn_Wo, L1_xattn_bo, L1_ffn_gamma, L1_ffn_wq, L1_ffn_keys, L1_ffn_table_down, L1_ffn_table_up):
    import jax
    import jax.numpy as jnp

    def _L0_attn_ref(x, Wq, bq, Wk, bk, Wv, bv, Wo, bo, proj):
        import jax, jax.numpy as jnp
        import numpy as np
        E = 128
        H = 16
        D = E // H
        M = 4 * D
        B, N = (4, 512)
        KERNEL_EPS = 0.0001

        def softmax_kernel(data, proj, is_query):
            d = data.shape[-1]
            data_n = data * d ** (-0.25)
            ratio = proj.shape[0] ** (-0.5)
            dd = jnp.einsum('bhnd,md->bhnm', data_n, proj)
            diag = 0.5 * jnp.sum(data_n * data_n, axis=-1, keepdims=True)
            if is_query:
                stab = jnp.max(dd, axis=-1, keepdims=True)
            else:
                stab = jnp.max(dd)
            return ratio * (jnp.exp(dd - diag - stab) + KERNEL_EPS)
        b, n, e = x.shape

        def split_heads(t):
            return t.reshape(b, n, H, D).transpose(0, 2, 1, 3)
        q = split_heads(x @ Wq.T + bq)
        k = split_heads(x @ Wk.T + bk)
        v = split_heads(x @ Wv.T + bv)
        qf = softmax_kernel(q, proj, is_query=True)
        kf = softmax_kernel(k, proj, is_query=False)
        k_sum = jnp.sum(kf, axis=-2)
        d_inv = 1.0 / jnp.einsum('bhnm,bhm->bhn', qf, k_sum)
        context = jnp.einsum('bhnm,bhnd->bhmd', kf, v)
        out = jnp.einsum('bhnm,bhmd,bhn->bhnd', qf, context, d_inv)
        out = out.transpose(0, 2, 1, 3).reshape(b, n, e)
        return out @ Wo.T + bo

    def _L0_xattn_ref(q, k, v, mask, wq, bq, wk, bk, wv, bv, wo, bo):
        import jax, jax.numpy as jnp
        import numpy as np
        HEADS = 16
        HIDDEN = 128
        DH = HIDDEN // HEADS
        STD = 0.02

        def _split_heads(x):
            B, S, _ = x.shape
            return x.reshape(B, S, HEADS, DH).transpose(0, 2, 1, 3)
        B, S, _ = q.shape
        qh = _split_heads(q @ wq.T + bq)
        kh = _split_heads(k @ wk.T + bk)
        vh = _split_heads(v @ wv.T + bv)
        scale = 1.0 / jnp.sqrt(jnp.float32(DH))
        corr = jnp.einsum('bhqd,bhkd->bhqk', qh, kh) * scale
        row_mask = (mask != 0)[:, None, :, None]
        corr = jnp.where(row_mask, corr, jnp.float32(-1000000000.0))
        prob = jax.nn.softmax(corr, axis=-1)
        hidden = jnp.einsum('bhqk,bhkd->bhqd', prob, vh)
        hidden = hidden.transpose(0, 2, 1, 3).reshape(B, S, HIDDEN)
        return hidden @ wo.T + bo

    def _L0_ffn_ref(x, q_nw, q_nb, q_w1, q_b1, q_w2, q_b2, k_nw, k_nb, k_w1, k_b1, k_w2, k_b2, v_nw, v_nb, v_w1, v_b1, v_w2, v_b2, f_nw, f_nb, f_w1, f_b1, f_w2, f_b2):
        import jax, jax.numpy as jnp
        import numpy as np
        D = 128
        LW = 16
        DEPTH = 8
        NN = 2 ** DEPTH - 1
        NL = 2 ** DEPTH
        B, S = (2, 128)

        def _fff(x, nw, nb, w1, b1, w2, b2, act):
            node = jnp.zeros(x.shape[:2], dtype=jnp.int32)
            for _ in range(DEPTH):
                logit = jnp.einsum('bsd,bsd->bs', x, nw[node]) + nb[node]
                node = 2 * node + 1 + (logit > 0).astype(jnp.int32)
            leaf = node - NN
            h = act(jnp.einsum('bsd,bsdl->bsl', x, w1[leaf]) + b1[leaf])
            return jnp.einsum('bsl,bsld->bsd', h, w2[leaf]) + b2[leaf]

        def _forward(x, q_nw, q_nb, q_w1, q_b1, q_w2, q_b2, k_nw, k_nb, k_w1, k_b1, k_w2, k_b2, v_nw, v_nb, v_w1, v_b1, v_w2, v_b2, f_nw, f_nb, f_w1, f_b1, f_w2, f_b2):
            mu = jnp.mean(x, -1, keepdims=True)
            sd = jnp.std(x, -1, ddof=1, keepdims=True)
            xn = (x - mu) / jnp.sqrt(sd + 1e-05)
            relu = jax.nn.relu
            q = _fff(xn, q_nw, q_nb, q_w1, q_b1, q_w2, q_b2, relu)
            k = _fff(xn, k_nw, k_nb, k_w1, k_b1, k_w2, k_b2, relu)
            v = _fff(xn, v_nw, v_nb, v_w1, v_b1, v_w2, v_b2, relu)
            att = jax.nn.softmax(jnp.einsum('bqd,bkd->bqk', q, k) / jnp.sqrt(jnp.float32(D)), axis=-1)
            y = xn + jnp.einsum('bqk,bkd->bqd', att, v)
            gelu = lambda t: jax.nn.gelu(t, approximate=False)
            return y + _fff(y, f_nw, f_nb, f_w1, f_b1, f_w2, f_b2, gelu)

        def _make_fff_params(key, scale_in, scale_leaf):
            ks = jax.random.split(key, 4)
            nw = jax.random.normal(ks[0], (NN, D), jnp.float32) * scale_in
            nb = jnp.zeros((NN,), jnp.float32)
            w1 = jax.random.normal(ks[1], (NL, D, LW), jnp.float32) * scale_in
            b1 = jax.random.normal(ks[2], (NL, LW), jnp.float32) * 0.01
            w2 = jax.random.normal(ks[3], (NL, LW, D), jnp.float32) * scale_leaf
            b2 = jnp.zeros((NL, D), jnp.float32)
            return (nw, nb, w1, b1, w2, b2)
        return _forward(x, q_nw, q_nb, q_w1, q_b1, q_w2, q_b2, k_nw, k_nb, k_w1, k_b1, k_w2, k_b2, v_nw, v_nb, v_w1, v_b1, v_w2, v_b2, f_nw, f_nb, f_w1, f_b1, f_w2, f_b2)

    def _L1_attn_ref(x, Wq, Wk, Wv, Wo):
        import jax, jax.numpy as jnp
        import numpy as np
        import math
        NUM_HEADS = 16
        b, s, d = x.shape
        h = NUM_HEADS
        dh = d // h

        def proj(W):
            y = jnp.einsum('bsd,ed->bse', x, W)
            return y.reshape(b, s, h, dh).transpose(0, 2, 1, 3)
        Q, K, V = (proj(Wq), proj(Wk), proj(Wv))
        scale = 1.0 / math.sqrt(dh)
        logits = jnp.einsum('bhqd,bhkd->bhqk', Q, K) * scale
        causal = jnp.tril(jnp.ones((s, s), dtype=bool))
        logits = jnp.where(causal, logits, -jnp.inf)
        attn = jax.nn.softmax(logits, axis=-1)
        out = jnp.einsum('bhqk,bhkd->bhqd', attn, V)
        out = out.transpose(0, 2, 1, 3).reshape(b, s, d)
        return jnp.einsum('bsv,dv->bsd', out, Wo)

    def _L1_xattn_ref(x, context, Wq, Wk, Wv, Wo, bo):
        import jax, jax.numpy as jnp
        import numpy as np
        EMB = 128
        HEADS = 16
        HEAD_DIM = EMB // HEADS
        B, Qlen, _ = x.shape
        KVlen = context.shape[1]
        scale = jnp.asarray(HEAD_DIM ** 0.5, x.dtype)
        q = (x @ Wq.T).reshape(B, Qlen, HEADS, HEAD_DIM).transpose(0, 2, 1, 3)
        k = (context @ Wk.T).reshape(B, KVlen, HEADS, HEAD_DIM).transpose(0, 2, 1, 3)
        v = (context @ Wv.T).reshape(B, KVlen, HEADS, HEAD_DIM).transpose(0, 2, 1, 3)
        scores = jnp.einsum('bhqd,bhkd->bhqk', q, k) / scale
        attn = jax.nn.softmax(scores, axis=-1)
        out = jnp.einsum('bhqk,bhkd->bhqd', attn, v)
        out = out.transpose(0, 2, 1, 3).reshape(B, Qlen, EMB)
        return out @ Wo.T + bo

    def _L1_ffn_ref(x, gamma, wq, keys, table_down, table_up):
        import jax, jax.numpy as jnp
        import numpy as np
        DIM = 128
        HEADS = 8
        NUM_EXPERTS = 8192
        NUM_KEYS = 32
        DIM_KEY = 64
        TOPK = 16

        def _rmsnorm(v, g):
            scale = jnp.sqrt(jnp.asarray(v.shape[-1], v.dtype))
            n = jnp.maximum(jnp.linalg.norm(v, axis=-1, keepdims=True), 1e-12)
            return v / n * g * scale
        B, N, D = x.shape
        xn = _rmsnorm(x, gamma)
        gate = xn
        q = gate @ wq.T
        q = q.reshape(B, N, 2, HEADS, DIM_KEY).transpose(2, 0, 1, 3, 4)
        sim = jnp.einsum('pbnhd,hkpd->pbnhk', q, keys)
        sx, ix = jax.lax.top_k(sim[0], TOPK)
        sy, iy = jax.lax.top_k(sim[1], TOPK)
        all_scores = (sx[..., :, None] + sy[..., None, :]).reshape(B, N, HEADS, TOPK * TOPK)
        all_indices = (ix[..., :, None] * NUM_KEYS + iy[..., None, :]).reshape(B, N, HEADS, TOPK * TOPK)
        scores, pk = jax.lax.top_k(all_scores, TOPK)
        indices = jnp.take_along_axis(all_indices, pk, axis=-1)
        wd = table_down[indices]
        wu = table_up[indices]
        h = jnp.einsum('bnd,bnhkd->bnhk', xn, wd)
        h = jax.nn.gelu(h, approximate=False) * jax.nn.softmax(scores, axis=-1)
        out = jnp.einsum('bnhk,bnhkd->bnd', h, wu)
        return out
    x = x + _L0_attn_ref(_layernorm(x, axis=-1), L0_attn_Wq, L0_attn_bq, L0_attn_Wk, L0_attn_bk, L0_attn_Wv, L0_attn_bv, L0_attn_Wo, L0_attn_bo, L0_attn_proj)
    x = x + _L0_xattn_ref(_layernorm(x, axis=-1), ctx_1024, ctx_1024, mask_BxS_ik0, L0_xattn_wq, L0_xattn_bq, L0_xattn_wk, L0_xattn_bk, L0_xattn_wv, L0_xattn_bv, L0_xattn_wo, L0_xattn_bo)
    x = x + _L0_ffn_ref(_layernorm(x, axis=-1), L0_ffn_q_nw, L0_ffn_q_nb, L0_ffn_q_w1, L0_ffn_q_b1, L0_ffn_q_w2, L0_ffn_q_b2, L0_ffn_k_nw, L0_ffn_k_nb, L0_ffn_k_w1, L0_ffn_k_b1, L0_ffn_k_w2, L0_ffn_k_b2, L0_ffn_v_nw, L0_ffn_v_nb, L0_ffn_v_w1, L0_ffn_v_b1, L0_ffn_v_w2, L0_ffn_v_b2, L0_ffn_f_nw, L0_ffn_f_nb, L0_ffn_f_w1, L0_ffn_f_b1, L0_ffn_f_w2, L0_ffn_f_b2)
    x = x + _L1_attn_ref(_layernorm(x, axis=-1), L1_attn_Wq, L1_attn_Wk, L1_attn_Wv, L1_attn_Wo)
    x = x + _L1_xattn_ref(_layernorm(x, axis=-1), ctx_1024, L1_xattn_Wq, L1_xattn_Wk, L1_xattn_Wv, L1_xattn_Wo, L1_xattn_bo)
    x = x + _L1_ffn_ref(_layernorm(x, axis=-1), L1_ffn_gamma, L1_ffn_wq, L1_ffn_keys, L1_ffn_table_down, L1_ffn_table_up)
    return x

_drawn_inputs = setup_inputs


def setup_inputs(seed=0):
    import zlib

    import numpy as np

    out = dict(_drawn_inputs(seed))
    spreads = {'L0_attn_bq': (0.0, 0.1),
     'L0_attn_bk': (0.0, 0.1),
     'L0_attn_bv': (0.0, 0.1),
     'L0_attn_bo': (0.0, 0.1),
     'L0_xattn_bq': (0.0, 0.8),
     'L0_xattn_bk': (0.0, 0.8),
     'L0_xattn_bv': (0.0, 0.1),
     'L0_xattn_bo': (0.0, 0.1),
     'L0_ffn_q_nb': (0.0, 0.1),
     'L0_ffn_q_b2': (0.0, 0.1),
     'L0_ffn_k_nb': (0.0, 0.1),
     'L0_ffn_k_b2': (0.0, 0.1),
     'L0_ffn_v_nb': (0.0, 0.1),
     'L0_ffn_v_b2': (0.0, 0.1),
     'L0_ffn_f_nb': (0.0, 0.1),
     'L0_ffn_f_b2': (0.0, 0.1),
     'L1_ffn_gamma': (1.0, 0.6)}
    factors = {'L0_xattn_wq': 2.95,
     'L0_xattn_wk': 8.0,
     'L0_ffn_q_b1': 8.0,
     'L0_ffn_k_b1': 4.431,
     'L0_ffn_v_b1': 3.945,
     'L0_ffn_f_b1': 8.0,
     'L1_xattn_bo': 8.0,
     'L1_ffn_wq': 8.0,
     'L1_ffn_keys': 8.0,
     'L1_ffn_table_down': 8.0,
     'L1_ffn_table_up': 8.0}
    for name, (base, spread) in spreads.items():
        noise = np.random.default_rng([zlib.crc32(name.encode()), seed]).standard_normal(out[name].shape)
        drawn = base * np.exp(spread * noise) if base else spread * noise
        out[name] = jnp.asarray(drawn.astype(out[name].dtype))
    for name, factor in factors.items():
        out[name] = (out[name] * factor).astype(out[name].dtype)
    return out
```

```python
import concourse.bass as bass
from concourse import mybir
from contextlib import ExitStack

B, S, E, H = 4, 256, 128, 16
D = E // H
P = 128
SUB = S // P
T = B * SUB
M = 4 * D
HG = P // M
DEPTH = 8
LEAVES = 2 ** DEPTH
NODES = LEAVES - 1
LW = 16
ROW = LW * E + LW + LW * E + E
PK = 32
PH = 8
PD = 64
TOPK = 16
EXPERTS = PK * PK
NCAND = [TOPK // (a + 1) for a in range(TOPK)]
CAND = sum(NCAND)
TERMS = [(0, 0), (1, 0), (2, 0), (0, 1), (1, 1), (0, 2)]
KS = len(TERMS) * D
BIG = 1.0e30


def decoder_program(nc, x_in, ctx_in, mask_in, attn_w, attn_bias, proj_t, node_w, node_b,
                    tab_q, tab_k, tab_v, tab_f, gamma_in, peer_wq, peer_keys, table_down,
                    table_up, out):
    f32, bf16 = mybir.dt.float32, mybir.dt.bfloat16
    i32, u32 = mybir.dt.int32, mybir.dt.uint32
    ALU = mybir.AluOpType
    ACT = mybir.ActivationFunctionType
    AX = mybir.AxisListType
    RMAX = bass.bass_isa.ReduceOp.max

    stack = ExitStack()
    with stack:
        def sb(name, shape, dt=f32):
            return stack.enter_context(nc.sbuf_tensor(name, shape, dt))

        def sem(name):
            return stack.enter_context(nc.semaphore(name))

        BANK = 512
        psum = stack.enter_context(nc.psum_tensor("psum", [P, 8 * BANK], f32))

        def bank(k, a=0, b=BANK):
            return psum[:, k * BANK + a:k * BANK + b]

        w_sb = sb("w_sb", [P, 16, P])
        bias_sb = sb("bias_sb", [1, 9, P])
        nodes_sb = sb("nodes_sb", [P, 4, NODES])
        nodeb_sb = sb("nodeb_sb", [1, 4, NODES])
        gamma_sb = sb("gamma_sb", [P, P])
        wq_sb = sb("wq_sb", [P, 2 * PH * PD])
        keys_sb = sb("keys_sb", [P, 8, 2 * PK])
        down_sb = sb("down_sb", [P, EXPERTS])
        up_sb = sb("up_sb", [P, EXPERTS // P, P])
        maskrow = sb("maskrow", [P, B * S])
        identf = sb("identf", [P, P])
        identb = sb("identb", [P, P], bf16)
        ones = sb("ones", [1, S])
        head16 = sb("head16", [P, H])
        half16 = sb("half16", [P, H])
        sel16 = sb("sel16", [3 * H, H, P], bf16)
        projb = sb("projb", [P, M])
        feat_w = sb("feat_w", [P, H, M])
        blockm = sb("blockm", [P, HG, D + 1])
        causal_q = sb("causal_q", [P, SUB, S], bf16)
        causal_k = sb("causal_k", [P, SUB, S], bf16)
        halves = sb("halves", [P, 2, 4])
        leaf_ids = sb("leaf_ids", [P, LEAVES])
        arena2 = sb("arena2", [P, 5120])

        x = sb("x", [P, T, P])
        ctx_t = sb("ctx_t", [P, B * S])
        stats = sb("stats", [P, 2, 6])
        mv = sb("mv", [P, 2, 2])
        var_e = sb("var_e", [P, 2])
        rstd = sb("rstd", [P, 2])
        mv2 = sb("mv2", [P, 2, 2])
        sd2 = sb("sd2", [P, 2])
        sd2e = sb("sd2e", [P, 2])
        rs2 = sb("rs2", [P, 2])
        ln = sb("ln", [P, SUB, P])
        xn = [sb(f"xn{i}", [P, SUB, P]) for i in range(3)]
        xn_t = [sb(f"xn_t{i}", [P, S]) for i in range(2)]
        qk_f = [sb(f"qk_f{i}", [P, 2, S]) for i in range(2)]
        resid_f = sb("resid_f", [P, 2, S])
        parts = [sb(f"parts{i}", [P, 3, 2, S], bf16) for i in range(2)]
        vaug = [sb(f"vaug{i}", [P, SUB, H, D + 1]) for i in range(4)]
        rowmax = [sb(f"rowmax{i}", [P, SUB, H]) for i in range(2)]
        negmax = sb("negmax", [P, SUB, H])
        remax = sb("remax", [P, SUB, H])
        mparts = [sb(f"mparts{i}", [P, SUB, 3, H], bf16) for i in range(2)]
        mt = [sb(f"mt{i}", [3 * H, S], bf16) for i in range(2)]
        probs = [sb(f"probs{i}", [P, SUB, S]) for i in range(3)]
        rsum = sb("rsum", [P, SUB, H])
        o_n = sb("o_n", [P, SUB, P])
        o_t = sb("o_t", [P, S])
        arena = sb("arena", [P, 17408])
        aw = arena[:, :].bitcast(bf16)
        STK = H * 2 * S
        stk = [aw[0:64, i * STK:(i + 1) * STK].rearrange("p (h w n) -> p h w n", h=H, w=2)
               for i in range(3)]
        leaf_rows = [arena[:, i * ROW:(i + 1) * ROW] for i in range(4)]
        zk = arena[:, 0:4096].rearrange("p (t c) -> p t c", t=T)
        qf_t = arena[:, 4096:8192].rearrange("p (t g n) -> p t g n", t=T, g=HG)
        zq = arena[:, 8192:9216]
        eq = arena[:, 9216:10240]
        kf = [arena[:, 10240 + i * 1024:11264 + i * 1024].rearrange("p (s c) -> p s c", s=SUB)
              for i in range(2)]
        sq = arena[:, 12288:12800].rearrange("p (w n) -> p w n", w=2)
        ctx_m = arena[:, 12800:12944].rearrange("p (g c) -> p g c", g=HG)
        ctx_rows = arena[:, 13312:14336].rearrange("p (t n) -> p t n", t=T)
        mask_i = arena[:, 14336:15360].bitcast(i32)
        stab = sb("stab", [P, 2, H])
        kmax = sb("kmax", [P, T])
        kmax1 = sb("kmax1", [P, 1])
        kmaxg = sb("kmaxg", [P, 1])
        nkmax = sb("nkmax", [P, 1])

        fx = sb("fx", [P, T, P])
        fx_t = sb("fx_t", [P, S])
        dec = arena2[:, 0:1536].bitcast(i32).rearrange("p (f n) -> p f n", f=6)
        walk = arena2[:, 1536:3072].rearrange("p (f n) -> p f n", f=6)
        leaf_no = [sb(f"leaf_no{i}", [P, 6], u32) for i in range(B)]
        leaf_nof = [sb(f"leaf_nof{i}", [P, 2], u32) for i in range(B)]
        hid = [sb(f"hid{i}", [P, LW]) for i in range(2)]
        hact = [sb(f"hact{i}", [P, LW]) for i in range(2)]
        qkv = [arena2[:, 3072 + i * 768:3840 + i * 768].rearrange("p (s f e) -> p s f e", s=SUB, f=3)
               for i in range(2)]
        fqk_t = sb("fqk_t", [P, 4 * P])
        frow = sb("frow", [P, 2])
        fneg = sb("fneg", [P, 2])
        fsum = sb("fsum", [P, 2])
        frec = sb("frec", [P, 2])
        att = arena2[:, 4608:5120].rearrange("p (s n) -> p s n", s=SUB)
        att_t = sb("att_t", [P, 4, P])
        fy = [sb(f"fy{i}", [P, SUB, P]) for i in range(2)]
        fy_t = sb("fy_t", [P, S])
        fo = sb("fo", [P, SUB, P])
        qp_t = arena[:, 0:2048].rearrange("p (c n) -> p c n", c=8)
        sim = arena[:, 2048:6144].rearrange("p (t g k) -> p t g k", t=T, g=2 * PH)
        hg = arena[:, 6144:14336].rearrange("p (c n) -> p c n", c=8)
        grid = [arena[:, 14336 + i * 1024:15360 + i * 1024] for i in range(3)]
        picked = [arena2[:, i * 1024:(i + 1) * 1024] for i in range(2)]
        px = [sb(f"px{i}", [P, SUB, P]) for i in range(2)]
        px_t = sb("px_t", [P, S])
        pn = sb("pn", [P, 2])
        pss = sb("pss", [P, 2])
        simw = sb("simw", [P, 2 * PH, PK])
        best = sb("best", [P, 2 * PH, TOPK])
        pairs = sb("pairs", [P, PH, CAND])
        pairw = sb("pairw", [P, PH, CAND])
        top = [sb(f"top{i}", [P, PH, TOPK]) for i in range(2)]
        tdif = sb("tdif", [P, PH, TOPK])
        texp = sb("texp", [P, PH, TOPK])
        tneg = [sb(f"tneg{i}", [P, PH]) for i in range(2)]
        tsum = sb("tsum", [P, PH])
        trec = sb("trec", [P, PH])
        diag = [arena2[:, 2048 + i * 1024:3072 + i * 1024].rearrange("p (h n) -> p h n", h=PH) for i in range(2)]
        mixed = arena2[:, 4096:5120].rearrange("p (c n) -> p c n", c=8)

        in_x, in_w, in_ctx = sem("in_x"), sem("in_w"), sem("in_ctx")
        in_tab, in_keys, zeros_done = sem("in_tab"), sem("in_keys"), sem("zeros_done")
        consts = sem("consts")
        ctxt_ps, ctxt_ready, mask_ready, feat_ready = (sem("ctxt_ps"), sem("ctxt_ready"),
                                                       sem("mask_ready"), sem("feat_ready"))
        var_ready, rstd_ready, xn_ready = sem("var_ready"), sem("rstd_ready"), sem("xn_ready")
        xt_ps, xt_ready = sem("xt_ps"), sem("xt_ready")
        qk_ps, qk_ready, v_ps, v_ready = sem("qk_ps"), sem("qk_ready"), sem("v_ps"), sem("v_ready")
        parts_ready = sem("parts_ready")
        stk_ready = [sem(f"stk_ready{i}") for i in range(3)]
        rows_ps, rows_max = sem("rows_ps"), sem("rows_max")
        mparts_ready, mt_ps, mt_ready = sem("mparts_ready"), sem("mt_ps"), sem("mt_ready")
        cols_ps, probs_ready, pv_ps = sem("cols_ps"), sem("probs_ready"), sem("pv_ps")
        o_ready, ot_ps, ot_ready = sem("o_ready"), sem("ot_ps"), sem("ot_ready")
        y_ps, x_ready = sem("y_ps"), sem("x_ready")
        sq_ready, dd_ps, zq_ready, zk_ready = sem("sq_ready"), sem("dd_ps"), sem("zq_ready"), sem("zk_ready")
        eq_ready, qft_ps, qft_ready = sem("eq_ready"), sem("qft_ps"), sem("qft_ready")
        kmax_ready, kmax_all, nkmax_ready = sem("kmax_ready"), sem("kmax_all"), sem("nkmax_ready")
        ke_ready, kf_ready, cx_ps, cx_ready = sem("ke_ready"), sem("kf_ready"), sem("cx_ps"), sem("cx_ready")
        dve_step, act_step, pool_step = sem("dve_step"), sem("act_step"), sem("pool_step")
        out_done = sem("out_done")
        fv, fp, fx_ready, fxt_ps, fxt_ready, lg_ps = (sem("fv"), sem("fp"), sem("fx_ready"), sem("fxt_ps"),
                                                      sem("fxt_ready"), sem("lg_ps"))
        dec_ready, idx_ready, leaf_done = sem("dec_ready"), sem("idx_ready"), sem("leaf_done")
        rows_in = [sem(f"rows_in{i}") for i in range(4)]
        fqk_ps, fqk_ready, fs_ps, fmax_ready = sem("fqk_ps"), sem("fqk_ready"), sem("fs_ps"), sem("fmax_ready")
        att_ready, at_ps, at_ready, fy_ps, fy_ready = (sem("att_ready"), sem("at_ps"), sem("at_ready"),
                                                       sem("fy_ps"), sem("fy_ready"))
        fyt_ps, fyt_ready, lgf_ps, decf_ready, idxf_ready = (sem("fyt_ps"), sem("fyt_ready"), sem("lgf_ps"),
                                                             sem("decf_ready"), sem("idxf_ready"))
        fh_ready, fg_ready, ffn_done = sem("fh_ready"), sem("fg_ready"), sem("ffn_done")
        pv2, pp2, px_ready, pxt_ps, pxt_ready = (sem("pv2"), sem("pp2"), sem("px_ready"), sem("pxt_ps"),
                                                 sem("pxt_ready"))
        qp_ps, qp_ready, sim_ps, sim_ready = sem("qp_ps"), sem("qp_ready"), sem("sim_ps"), sem("sim_ready")
        hp_ps, hp_ready = sem("hp_ps"), sem("hp_ready")
        grid_ready, e_ready, picked_ready, mix_ps = sem("grid_ready"), sem("e_ready"), sem("picked_ready"), sem("mix_ps")
        tdif_ready, texp_ready, diag_ready = sem("tdif_ready"), sem("texp_ready"), sem("diag_ready")
        mixed_ready, po_ps, tile_ready = sem("mixed_ready"), sem("po_ps"), sem("tile_ready")

        def chain(eng, s):
            n = [0]

            def link(i):
                n[0] += 1
                i.then_inc(s, 1)
                eng.wait_ge(s, n[0])
            return link

        def stage(n):
            return n // B

        def batch(n):
            return n % B

        def bank_o(s, h, n=1):
            return bank(7)[:, s * 144 + h * 9:s * 144 + (h + n) * 9]

        mt_bank = psum[0:3 * H, 7 * BANK + 384:8 * BANK].bitcast(bf16)
        RUNS = [(4, 7), (8, 15)]

        def run_of(n):
            return next((r for r in RUNS if r[0] <= n <= r[1]), (0, B - 1))

        def tails_ahead(n):
            return max(n - 3, run_of(n)[0])

        def pres_ahead(n):
            first, last = run_of(n)
            return last + 1 if first == 0 else min(n + 4, last + 1)

        def placed(n):
            return len([m for m in range(B, n + 1) if m % 3 == n % 3])

        def finish_sp(sp):
            out_t = out.rearrange("b (s p) e -> p (b s) e", p=P)
            for t in range(T):
                sp.wait_ge(tile_ready, t + 1)
                sp.dma_start(out_t[:, t, :], x[:, t, :]).then_inc(out_done, 16)
            sp.wait_ge(out_done, 16 * T)

        ORDER = []
        for b in range(B + 2):
            if b < B:
                ORDER += [(b, s, f) for s in range(SUB) for f in range(3)]
            if b >= 2:
                ORDER += [(b - 2, s, 3) for s in range(SUB)]
        TABS = [tab_q, tab_k, tab_v, tab_f]

        block = stack.enter_context(nc.Block())

        @block.sync
        def _(sp):
            sp.dma_start(x[:, :, :], x_in.rearrange("b (s p) e -> p (b s) e", p=P)).then_inc(in_x, 16)
            sp.dma_start(w_sb[:, 0:4, :], attn_w[0:4].rearrange("a i o -> i a o")).then_inc(in_w, 16)
            sp.dma_start(bias_sb[:, :, :], attn_bias.rearrange("(a r) e -> a r e", a=1)).then_inc(in_w, 16)
            sp.dma_start(projb[:, :], proj_t).then_inc(in_w, 16)
            sp.dma_start(ctx_rows, ctx_in.rearrange("b (s p) e -> p (b s) e", p=P)).then_inc(in_ctx, 16)
            sp.dma_start(mask_i, mask_in.rearrange("b s -> (b s)").partition_broadcast(P)).then_inc(in_ctx, 16)
            sp.dma_start(w_sb[:, 4:16, :], attn_w[4:16].rearrange("a i o -> i a o")).then_inc(in_ctx, 16)
            sp.dma_start(nodes_sb[:, :, :], node_w).then_inc(in_tab, 16)
            sp.dma_start(nodeb_sb[:, :, :], node_b).then_inc(in_tab, 16)
            sp.dma_start(gamma_sb[:, :], gamma_in.partition_broadcast(P)).then_inc(in_keys, 16)
            sp.dma_start(wq_sb[:, :], peer_wq).then_inc(in_keys, 16)
            sp.dma_start(down_sb[:, :], table_down).then_inc(in_keys, 16)
            sp.dma_start(up_sb[:, :, :], table_up.rearrange("(c p) e -> p c e", p=P)).then_inc(in_keys, 16)
            sp.wait_ge(zeros_done, 1)
            for side in range(2):
                for h in range(PH):
                    r, c = (h % 2) * PD, side * 4 + h // 2
                    sp.dma_start(keys_sb[r:r + PD, c, (h % 2) * PK:(h % 2 + 1) * PK],
                                 peer_keys[side, h]).then_inc(in_keys, 16)

            def place(n):
                sp.wait_ge(parts_ready, n - B + 1)
                if n - 3 >= B:
                    sp.wait_ge(cols_ps, (n - 3 - B + 1) * H)
                for r, (qp, kp) in enumerate(TERMS):
                    for w, part in ((0, qp), (1, kp)):
                        sp.dma_start(stk[n % 3][r * D:(r + 1) * D, :, w, :],
                                     parts[n % 2][:, part, w, :]).then_inc(stk_ready[n % 3], 16)

            def run(first, last):
                place(first)
                place(first + 1)
                for n in range(first, last - 1):
                    place(n + 2)

            run(*RUNS[0])
            run(*RUNS[1])
            finish_sp(sp)

        @block.gpsimd
        def _(pool):
            link = chain(pool, pool_step)
            nc.gpsimd.memset(keys_sb[:, :, :], 0.0).then_inc(zeros_done, 1)
            link(nc.gpsimd.memset(identf[:, :], 0.0))
            link(nc.gpsimd.affine_select(out=identf[:, :], in_=identf[:, :], compare_op=ALU.not_equal, fill=1.0,
                                         base=0, pattern=[[-1, P]], channel_multiplier=1))
            link(nc.gpsimd.tensor_copy(identb[:, :], identf[:, :]))
            link(nc.gpsimd.memset(ones[:, :], 1.0))
            link(nc.gpsimd.memset(halves[:, 0, :], -0.5))
            link(nc.gpsimd.memset(halves[:, 1, :], 0.5))
            link(nc.gpsimd.memset(head16[:, :], 0.0))
            for j in range(D):
                link(nc.gpsimd.affine_select(out=head16[:, :], in_=head16[:, :], compare_op=ALU.not_equal,
                                             fill=1.0, base=-H * j, pattern=[[-1, H]], channel_multiplier=1))
            for i in range(4):
                link(nc.gpsimd.memset(vaug[i][:, :, :, :], 1.0))
            link(nc.gpsimd.memset(blockm[:, :, :], 1.0))
            link(nc.gpsimd.affine_select(out=blockm[:, :, :], in_=blockm[:, :, :], compare_op=ALU.is_ge, fill=0.0,
                                         base=0, pattern=[[-M, HG], [0, D + 1]], channel_multiplier=1))
            link(nc.gpsimd.affine_select(out=blockm[:, :, :], in_=blockm[:, :, :], compare_op=ALU.is_ge, fill=0.0,
                                         base=M - 1, pattern=[[M, HG], [0, D + 1]], channel_multiplier=-1))
            nc.gpsimd.tensor_scalar(half16[:, :], head16[:, :], 0.5, None, ALU.mult).then_inc(consts, 1)

            def power(n):
                pool.wait_ge(var_ready, n + 1)
                nc.gpsimd.tensor_tensor(rstd[:, :], var_e[:, :], halves[:, 0, 0:2], ALU.pow).then_inc(rstd_ready, 1)

            def squares(n):
                pool.wait_ge(qk_ready, n + 1)
                if n >= 1:
                    pool.wait_ge(dd_ps, n)
                nc.gpsimd.tensor_tensor(sq, qk_f[n % 2][:, :, :], qk_f[n % 2][:, :, :], ALU.mult).then_inc(sq_ready, 1)

            def split(n):
                q = qk_f[n % 2][:, :, :]
                p = parts[n % 2]
                pool.wait_ge(qk_ready, n + 1)
                if n - 2 >= B:
                    pool.wait_ge(stk_ready[(n - 2) % 3], 16 * 12 * placed(n - 2))
                if stage(n) == 1:
                    b = batch(n)
                    link(nc.gpsimd.tensor_tensor(qk_f[n % 2][:, 0, :], qk_f[n % 2][:, 0, :],
                                                 maskrow[:, b * S:(b + 1) * S], ALU.mult))
                link(nc.gpsimd.tensor_copy(p[:, 0, :, :], q))
                link(nc.gpsimd.tensor_tensor(resid_f[:, :, :], q, p[:, 0, :, :], ALU.subtract))
                link(nc.gpsimd.tensor_copy(p[:, 1, :, :], resid_f[:, :, :]))
                nc.gpsimd.tensor_tensor(p[:, 2, :, :], resid_f[:, :, :], p[:, 1, :, :], ALU.subtract).then_inc(parts_ready, 1)
                pool.wait_ge(parts_ready, n - B + 1)

            for n in range(B):
                power(n)
                squares(n)
            link(nc.gpsimd.tensor_copy(sel16[:, :, :], head16[0:3 * H, :].unsqueeze(2).to_broadcast([3 * H, H, P])))
            for c, (m, qs, ks) in enumerate(((causal_q, 1, -1), (causal_k, -1, 1))):
                link(nc.gpsimd.memset(m[:, :, :], 0.0))
                for s in range(SUB):
                    link(nc.gpsimd.affine_select(out=m[:, s, :], in_=m[:, s, :], compare_op=ALU.is_ge, fill=-BIG,
                                                 base=qs * s * P, pattern=[[ks, S]], channel_multiplier=qs))
            link(nc.gpsimd.iota(leaf_ids[:, :], pattern=[[1, LEAVES]], base=0, channel_multiplier=0,
                                allow_small_or_imprecise_dtypes=True))
            nc.gpsimd.memset(o_t[:, 0:1], 0.0).then_inc(consts, 1)
            pool.wait_ge(kmax_ready, 1)
            nc.gpsimd.partition_all_reduce(kmaxg[:, :], kmax1[:, :], P, RMAX).then_inc(kmax_all, 1)

            def run(first, last):
                for n in range(first, first + 3):
                    power(n)
                split(first)
                split(first + 1)
                for n in range(first, last + 1):
                    if n + 2 <= last:
                        split(n + 2)
                    if n + 3 <= last:
                        power(n + 3)

            def ffn():
                for b in range(B):
                    for j, (i, o, e) in enumerate(((var_e, rstd, 0), (var_e, sd2, 1), (sd2e, rs2, 0))):
                        pool.wait_ge(fv, 3 * b + j + 1)
                        nc.gpsimd.tensor_tensor(o[:, :], i[:, :], halves[:, e, 0:2], ALU.pow).then_inc(fp, 1)
                for g, (b, s, f) in enumerate(ORDER):
                    if f == 3:
                        pool.wait_ge(idxf_ready, b + 1)
                        no = leaf_nof[b][:, s:s + 1]
                    else:
                        pool.wait_ge(idx_ready, b + 1)
                        no = leaf_no[b][:, s * 3 + f:s * 3 + f + 1]
                    if g >= 4:
                        pool.wait_ge(leaf_done, g - 3)
                    nc.gpsimd.indirect_dma_start(leaf_rows[g % 4], None, TABS[f],
                                                 bass.IndirectOffsetOnAxis(no, 0)).then_inc(rows_in[g % 4], 16)

            def peer():
                for b in range(B):
                    for j, (i, o, e) in enumerate(((var_e, rstd, 0), (pss, pn, 1))):
                        pool.wait_ge(pv2, 2 * b + j + 1)
                        nc.gpsimd.tensor_tensor(o[:, :], i[:, :], halves[:, e, 0:2], ALU.pow).then_inc(pp2, 1)
                for t in range(T):
                    pool.wait_ge(sim_ready, t + 1)
                    for h in range(PH):
                        k = t * PH + h
                        if k >= 3:
                            pool.wait_ge(picked_ready, k - 2)
                        nc.gpsimd.tensor_tensor(grid[k % 3].rearrange("p (i j) -> p i j", i=PK),
                                                sim[:, t, h, :].unsqueeze(2).to_broadcast([P, PK, PK]),
                                                sim[:, t, PH + h, :].unsqueeze(1).to_broadcast([P, PK, PK]),
                                                ALU.add).then_inc(grid_ready, 1)

            run(*RUNS[0])
            ffn()
            run(*RUNS[1])
            peer()

        @block.scalar
        def _(act):
            link = chain(act, act_step)

            def copy(o, i, s):
                nc.scalar.activation(o, i, ACT.Copy).then_inc(s, 1)

            def evac_x(n):
                act.wait_ge(xt_ps, n + 1)
                if n >= 2:
                    act.wait_ge(v_ps, n - 1)
                copy(xn_t[n % 2][:, :], bank(4, 0, S), xt_ready)

            def evac_qkv(n):
                act.wait_ge(qk_ps, n + 1)
                if n >= B + 2:
                    act.wait_ge(parts_ready, n - B - 1)
                elif n >= 2:
                    act.wait_ge(dd_ps, min(n - 1, B))
                scale = float(D) ** -0.25 if stage(n) == 0 else 1.0
                nc.scalar.activation(qk_f[n % 2][:, :, :], bank(5).rearrange("p (w n) -> p w n", w=2),
                                     ACT.Copy, scale=scale).then_inc(qk_ready, 1)
                act.wait_ge(v_ps, n + 1)
                act.wait_ge(consts, 1)
                if n >= 4:
                    act.wait_ge(pv_ps, (n - 3) if n - 4 < B else B + (n - 3 - B) * H)
                copy(vaug[n % 4][:, :, :, 0:D],
                     bank(6, 0, S).rearrange("p (s h d) -> p s h d", s=SUB, h=H), v_ready)

            def evac_ot(n):
                act.wait_ge(ot_ps, n + 1)
                if n >= 1:
                    act.wait_ge(y_ps, n)
                copy(o_t[:, :], bank(4, S, 2 * S), ot_ready)

            def exps(n, h):
                act.wait_ge(cols_ps, (n - B) * H + h + 1)
                k = (n - B) * H + h
                if k >= 3:
                    act.wait_ge(pv_ps, B + k - 2)
                nc.scalar.activation(probs[k % 3][:, :, :], bank(2 + k % 2).rearrange("p (c n) -> p c n", c=SUB),
                                     ACT.Exp, scale=float(D) ** -0.5).then_inc(probs_ready, 1)

            act.wait_ge(consts, 1)
            for half in range(2):
                act.wait_ge(ctxt_ps, half + 1)
                copy(ctx_t[:, half * BANK:(half + 1) * BANK], bank(half), ctxt_ready)
            for n in range(B):
                evac_x(n)
                evac_qkv(n)
                act.wait_ge(zq_ready, n + 1)
                if n >= 1:
                    act.wait_ge(qft_ps, n)
                nc.scalar.activation(eq, zq, ACT.Exp).then_inc(eq_ready, 1)
            act.wait_ge(nkmax_ready, 1)
            for n in range(B):
                if n >= 2:
                    act.wait_ge(cx_ps, n - 1)
                nc.scalar.activation(kf[n % 2], zk[:, SUB * n:SUB * n + SUB, :], ACT.Exp,
                                     bias=nkmax[:, 0:1]).then_inc(ke_ready, 1)
                if n >= 1:
                    evac_ot(n - 1)
            evac_ot(B - 1)

            def run(first, last):
                for n in (first, first + 1):
                    evac_x(n)
                    evac_qkv(n)
                for n in range(first, last + 1):
                    if n + 2 <= last:
                        evac_x(n + 2)
                        evac_qkv(n + 2)
                    act.wait_ge(mt_ps, n - B + 1)
                    if n - 2 >= B:
                        act.wait_ge(cols_ps, (n - 1 - B) * H)
                    copy(mt[n % 2][:, :], mt_bank, mt_ready)
                    for h in range(H):
                        exps(n, h)
                        if h == 5 and n > first:
                            evac_ot(n - 1)
                evac_ot(last)

            def ffn():
                for b in range(B):
                    act.wait_ge(fxt_ps, b + 1)
                    if b >= 1:
                        act.wait_ge(lg_ps, b)
                    copy(fx_t[:, :], bank(4, 0, S), fxt_ready)
                for slot in range(B + 2):
                    b = slot - 1
                    if 0 <= b < B:
                        act.wait_ge(fqk_ps, b + 1)
                        copy(fqk_t[:, :], bank(4), fqk_ready)
                        act.wait_ge(fmax_ready, b + 1)
                        for s in range(SUB):
                            nc.scalar.activation(att[:, s, :], bank(5, s * S, s * S + S), ACT.Exp, bias=fneg[:, s:s + 1],
                                                 scale=float(E) ** -0.5, accum_out=fsum[:, s:s + 1]).then_inc(att_ready, 1)
                        act.wait_ge(at_ps, b + 1)
                        copy(att_t[:, :, :], bank(6).rearrange("p (c n) -> p c n", c=4), at_ready)
                        act.wait_ge(fyt_ps, b + 1)
                        copy(fy_t[:, :], bank(4, 0, S), fyt_ready)
                    b = slot - 2
                    if b >= 0:
                        for s in range(SUB):
                            act.wait_ge(fh_ready, 2 * b + s + 1)
                            nc.scalar.activation(hact[s][:, :], hid[s][:, :], ACT.Gelu).then_inc(fg_ready, 1)

            def peer():
                for b in range(B):
                    act.wait_ge(pxt_ps, b + 1)
                    if b >= 1:
                        act.wait_ge(hp_ps, b)
                    copy(px_t[:, :], bank(4, 0, S), pxt_ready)
                    act.wait_ge(qp_ps, b + 1)
                    if b >= 1:
                        act.wait_ge(sim_ps, SUB * b)
                    copy(qp_t, psum[:, 0:4 * BANK].rearrange("p (c n) -> p c n", c=8), qp_ready)
                    for s in range(SUB):
                        act.wait_ge(sim_ps, SUB * b + s + 1)
                        copy(sim[:, SUB * b + s, :, :], bank(5 + s).rearrange("p (g k) -> p g k", k=PK), sim_ready)
                    act.wait_ge(hp_ps, b + 1)
                    nc.scalar.activation(hg[:, :, b * S:(b + 1) * S], psum[:, 0:4 * BANK].rearrange("p (c n) -> p c n", c=8),
                                         ACT.Gelu).then_inc(hp_ready, 1)

                def top_exp(t):
                    act.wait_ge(tdif_ready, t + 1)
                    nc.scalar.activation(texp[:, :, :], tdif[:, :, :], ACT.Exp).then_inc(texp_ready, 1)

                top_exp(0)
                for t in range(T):
                    for h in range(PH):
                        k = t * PH + h
                        act.wait_ge(grid_ready, k + 1)
                        if k >= 2:
                            act.wait_ge(picked_ready, k - 1)
                        act.wait_ge(diag_ready, t + 1)
                        nc.scalar.activation(psum[:, (4 + 2 * (k % 2)) * BANK:(6 + 2 * (k % 2)) * BANK], grid[k % 3],
                                             ACT.Exp, bias=tneg[t % 2][:, h:h + 1]).then_inc(e_ready, 1)
                        if h == 6 and t + 1 < T:
                            top_exp(t + 1)

            run(*RUNS[0])
            ffn()
            run(*RUNS[1])
            peer()

        @block.vector
        def _(dve):
            link = chain(dve, dve_step)

            def norm(n):
                b = batch(n)
                if n < B:
                    dve.wait_ge(in_x, 16)
                elif stage(n) == 2:
                    dve.wait_ge(ffn_done, b + 1)
                else:
                    dve.wait_ge(x_ready, n - B + 1)
                for s in range(SUB):
                    link(nc.vector.bn_stats(stats[:, s, :], x[:, SUB * b + s, :]))
                    link(nc.vector.bn_aggr(mv[:, s, :], stats[:, s, :]))
                if n >= 1:
                    dve.wait_ge(rstd_ready, n)
                nc.vector.tensor_scalar(var_e[:, :], mv[:, :, 1], 1e-5, None, ALU.add).then_inc(var_ready, 1)
                dve.wait_ge(rstd_ready, n + 1)
                if n >= 3:
                    dve.wait_ge(xt_ps, n - 2)
                for s in range(SUB):
                    i = nc.vector.tensor_scalar(xn[n % 3][:, s, :], x[:, SUB * b + s, :], mv[:, s, 0:1],
                                                rstd[:, s:s + 1], ALU.subtract, ALU.mult)
                i.then_inc(xn_ready, 1)
                dve.wait_ge(xn_ready, n + 1)

            def onorm(n):
                dve.wait_ge(pv_ps, n + 1 if n < B else B + (n - B + 1) * H)
                o4 = bank(7, 0, 288).rearrange("p (g c) -> p g c", c=D + 1)
                link(nc.vector.reciprocal(rsum[:, :, :].rearrange("p s h -> p (s h)").unsqueeze(2), o4[:, :, D:D + 1]))
                if n >= 1:
                    dve.wait_ge(ot_ps, n)
                nc.vector.tensor_tensor(o_n[:, :, :].rearrange("p s (h d) -> p (s h) d", d=D), o4[:, :, 0:D],
                                        rsum[:, :, :].rearrange("p s h -> p (s h)").unsqueeze(2).to_broadcast([P, SUB * H, D]),
                                        ALU.mult).then_inc(o_ready, 1)

            def resid(n):
                b = batch(n)
                dve.wait_ge(y_ps, n + 1)
                nc.vector.tensor_tensor(x[:, SUB * b:SUB * b + SUB, :],
                                        bank(6, S, 2 * S).rearrange("p (s e) -> p s e", s=SUB),
                                        x[:, SUB * b:SUB * b + SUB, :], ALU.add).then_inc(x_ready, 1)

            def row_max(n, h):
                k = (n - B) * H + h
                dve.wait_ge(rows_ps, k + 1)
                nc.vector.tensor_reduce(rowmax[n % 2][:, :, h], bank(k % 2).rearrange("p (s n) -> p s n", s=SUB),
                                        AX.X, ALU.max).then_inc(rows_max, 1)

            def max_parts(n):
                dve.wait_ge(rows_max, (n - B + 1) * H)
                if n - 2 >= B:
                    dve.wait_ge(mt_ps, n - 1 - B)
                mp = mparts[n % 2]
                link(nc.vector.tensor_scalar(negmax[:, :, :], rowmax[n % 2][:, :, :], -1.0, None, ALU.mult))
                link(nc.vector.tensor_copy(mp[:, :, 0, :], negmax[:, :, :]))
                link(nc.vector.tensor_tensor(remax[:, :, :], negmax[:, :, :], mp[:, :, 0, :], ALU.subtract))
                link(nc.vector.tensor_copy(mp[:, :, 1, :], remax[:, :, :]))
                nc.vector.tensor_tensor(mp[:, :, 2, :], remax[:, :, :], mp[:, :, 1, :], ALU.subtract).then_inc(mparts_ready, 1)
                dve.wait_ge(mparts_ready, n - B + 1)

            dve.wait_ge(consts, 1)
            dve.wait_ge(in_w, 48)
            nc.vector.tensor_tensor(feat_w[:, :, :], head16[:, :].unsqueeze(2).to_broadcast([P, H, M]),
                                    projb[:, :].unsqueeze(1).to_broadcast([P, H, M]), ALU.mult).then_inc(feat_ready, 1)
            norm(0)
            for n in range(B):
                if n + 1 < B:
                    norm(n + 1)
                dve.wait_ge(dd_ps, n + 1)
                if n >= 1:
                    dve.wait_ge(eq_ready, n)
                ddq = psum[:, 0:2 * BANK].rearrange("p (g m) -> p g m", m=M)
                ddk = psum[:, 2 * BANK:4 * BANK].rearrange("p (g m) -> p g m", m=M)
                half_norm = bank(7, 0, 64).rearrange("p (w s h) -> p w (s h)", w=2, s=SUB)
                sv = stab[:, :, :].rearrange("p s h -> p (s h)")
                link(nc.vector.tensor_reduce(sv, ddq, AX.X, ALU.max))
                link(nc.vector.tensor_tensor(sv, half_norm[:, 0, :], sv, ALU.add))
                nc.vector.tensor_tensor(zq.rearrange("p (g m) -> p g m", m=M), ddq,
                                        sv.unsqueeze(2).to_broadcast([P, 2 * H, M]), ALU.subtract).then_inc(zq_ready, 1)
                nc.vector.tensor_reduce(kmax[:, SUB * n:SUB * n + SUB],
                                        psum[:, 2 * BANK:4 * BANK].rearrange("p (s c) -> p s c", s=SUB), AX.X, ALU.max)
                dve.wait_ge(zq_ready, n + 1)
                link(nc.vector.tensor_copy(sv, half_norm[:, 1, :]))
                nc.vector.tensor_tensor(zk[:, SUB * n:SUB * n + SUB, :].rearrange("p s (g m) -> p (s g) m", m=M), ddk,
                                        sv.unsqueeze(2).to_broadcast([P, 2 * H, M]), ALU.subtract).then_inc(zk_ready, 1)
                dve.wait_ge(zk_ready, n + 1)
                dve.wait_ge(qft_ps, n + 1)
                nc.vector.tensor_scalar(qf_t[:, SUB * n:SUB * n + SUB, :, :],
                                        psum[:, 0:2 * BANK].rearrange("p (s g n) -> p s g n", s=SUB, g=HG),
                                        1e-4, None, ALU.add).then_inc(qft_ready, 1)
            link(nc.vector.tensor_reduce(kmax1[:, :], kmax[:, :], AX.X, ALU.max))
            nc.vector.tensor_copy(kmax1[:, :], kmax1[:, :]).then_inc(kmax_ready, 1)
            dve.wait_ge(in_ctx, 48)
            nc.vector.tensor_scalar(maskrow[:, :], mask_i, 0.0, None, ALU.not_equal).then_inc(mask_ready, 1)
            dve.wait_ge(kmax_all, 1)
            nc.vector.tensor_scalar(nkmax[:, :], kmaxg[:, :], -1.0, None, ALU.mult).then_inc(nkmax_ready, 1)
            for n in range(B):
                dve.wait_ge(ke_ready, n + 1)
                nc.vector.tensor_scalar(kf[n % 2], kf[n % 2], 1e-4, None, ALU.add).then_inc(kf_ready, 1)
                dve.wait_ge(cx_ps, n + 1)
                nc.vector.tensor_tensor(ctx_m, bank(3, 0, 144).rearrange("p (g c) -> p g c", g=HG),
                                        blockm[:, :, :].rearrange("p g c -> p (g c)").unsqueeze(1).to_broadcast([P, HG, 36]),
                                        ALU.mult).then_inc(cx_ready, 1)
                onorm(n)
                resid(n)

            def run(first, last):
                for n in range(first, first + 3):
                    norm(n)
                for h in range(H):
                    row_max(first, h)
                max_parts(first)
                for n in range(first, last + 1):
                    for h in range(H):
                        if n + 1 <= last:
                            row_max(n + 1, h)
                        if n > first and h == 8:
                            resid(n - 1)
                        if h == 11 and n + 3 <= last:
                            norm(n + 3)
                    if n + 1 <= last:
                        max_parts(n + 1)
                    onorm(n)
                resid(last)

            def stats_of(src, out_mv):
                for s in range(SUB):
                    link(nc.vector.bn_stats(stats[:, s, :], src[:, s, :]))
                    link(nc.vector.bn_aggr(out_mv[:, s, :], stats[:, s, :]))

            def normed(dst, src, m, r, last):
                for s in range(SUB):
                    i = nc.vector.tensor_scalar(dst[:, s, :], src[:, s, :], m[:, s, 0:1], r[:, s:s + 1],
                                                ALU.subtract, ALU.mult)
                    if last is None or s < SUB - 1:
                        link(i)
                    else:
                        i.then_inc(last, 1)

            def ffn_norm(b):
                xb = x[:, SUB * b:SUB * b + SUB, :]
                dve.wait_ge(x_ready, 2 * B)
                stats_of(xb, mv)
                nc.vector.tensor_scalar(var_e[:, :], mv[:, :, 1], 1e-5, None, ALU.add).then_inc(fv, 1)
                dve.wait_ge(fp, 3 * b + 1)
                normed(ln, xb, mv, rstd, None)
                stats_of(ln, mv2)
                nc.vector.tensor_scalar(var_e[:, :], mv2[:, :, 1], float(E) / (E - 1), None, ALU.mult).then_inc(fv, 1)
                dve.wait_ge(fp, 3 * b + 2)
                nc.vector.tensor_scalar(sd2e[:, :], sd2[:, :], 1e-5, None, ALU.add).then_inc(fv, 1)
                dve.wait_ge(fp, 3 * b + 3)
                normed(fx[:, SUB * b:SUB * b + SUB, :], ln, mv2, rs2, fx_ready)

            def route(n, logits, numbers, decided, ready):
                d, v = dec[:, 0:n, :], walk[:, 0:n, :]
                nc.vector.tensor_scalar(d.rearrange("p (s f) n -> p s f n", s=SUB)[:, :, :, 0:NODES], logits, 0.0, None,
                                        ALU.is_gt).then_inc(*decided[0:2])
                link(nc.vector.tensor_copy(v, leaf_ids[:, :].unsqueeze(1).to_broadcast([P, n, LEAVES])))
                dve.wait_ge(decided[0], decided[2])
                for level in reversed(range(DEPTH)):
                    st = 2 ** (DEPTH - level)
                    link(nc.vector.copy_predicated(v[:, :, 0:LEAVES:st], d[:, :, 2 ** level - 1:2 ** (level + 1) - 1],
                                                   v[:, :, st // 2:LEAVES:st]))
                nc.vector.tensor_copy(numbers, v[:, :, 0]).then_inc(*ready[0:2])
                dve.wait_ge(ready[0], ready[2])

            def hidden(g, src, add_only):
                dve.wait_ge(rows_in[g % 4], 16 * (g // 4 + 1))
                r = leaf_rows[g % 4]
                for l in range(LW):
                    w = r[:, l * E:(l + 1) * E]
                    i = nc.vector.tensor_tensor_reduce(w, w, src, 1.0, 0.0, ALU.mult, ALU.add, hid[g % 2][:, l:l + 1])
                link(i)
                i = nc.vector.tensor_tensor(hid[g % 2][:, :], hid[g % 2][:, :], r[:, LW * E:LW * E + LW], ALU.add)
                if add_only:
                    i.then_inc(fh_ready, 1)
                else:
                    link(i)
                    link(nc.vector.tensor_scalar(hact[g % 2][:, :], hid[g % 2][:, :], 0.0, None, ALU.max))

            def leaf_out(g, dst):
                r = leaf_rows[g % 4]
                for l in range(LW):
                    w = r[:, LW * E + LW + l * E:LW * E + LW + (l + 1) * E]
                    i = nc.vector.scalar_tensor_tensor(out=dst, in0=w, scalar=hact[g % 2][:, l:l + 1],
                                                       in1=r[:, ROW - E:ROW] if l == 0 else dst,
                                                       op0=ALU.mult, op1=ALU.add)
                    if l < LW - 1:
                        link(i)
                i.then_inc(leaf_done, 1)
                dve.wait_ge(leaf_done, g + 1)

            def att_max(b):
                dve.wait_ge(fs_ps, b + 1)
                link(nc.vector.tensor_reduce(frow[:, :], bank(5).rearrange("p (s n) -> p s n", s=SUB), AX.X, ALU.max))
                nc.vector.tensor_scalar(fneg[:, :], frow[:, :], -float(E) ** -0.5, None, ALU.mult).then_inc(fmax_ready, 1)

            def att_y(b):
                dve.wait_ge(att_ready, SUB * (b + 1))
                link(nc.vector.reciprocal(frec[:, :], fsum[:, :]))
                dve.wait_ge(fy_ps, b + 1)
                for s in range(SUB):
                    i = nc.vector.scalar_tensor_tensor(out=fy[b % 2][:, s, :], in0=bank(7, s * P, s * P + P),
                                                       scalar=frec[:, s:s + 1], in1=fx[:, SUB * b + s, :],
                                                       op0=ALU.mult, op1=ALU.add)
                    if s < SUB - 1:
                        link(i)
                i.then_inc(fy_ready, 1)
                dve.wait_ge(fy_ready, b + 1)

            def ffn():
                for b in range(B):
                    ffn_norm(b)
                    dve.wait_ge(lg_ps, b + 1)
                    lg = psum[:, 0:4 * BANK].rearrange("p (s f n) -> p s f n", s=SUB, f=4)[:, :, 0:3, 0:NODES]
                    route(6, lg, leaf_no[b][:, :], (dec_ready, 1, b + 1), (idx_ready, 1, b + 1))
                g = 0
                for slot in range(B + 2):
                    a = slot - 1
                    hooks = {}
                    if 0 <= a < B:
                        hooks = {0: lambda: att_max(a), 2: lambda: att_y(a), 4: lambda: route_f(a)}
                    for j in range(6):
                        if slot < B:
                            s, f = j // 3, j % 3
                            hidden(g, fx[:, SUB * slot + s, :], False)
                            leaf_out(g, qkv[slot % 2][:, s, f, :])
                            g += 1
                        if j in hooks:
                            hooks[j]()
                    if slot >= 2:
                        b = slot - 2
                        for s in range(SUB):
                            hidden(g + s, fy[b % 2][:, s, :], True)
                        for s in range(SUB):
                            dve.wait_ge(fg_ready, SUB * b + s + 1)
                            leaf_out(g + s, fo[:, s, :])
                        g += SUB
                        link(nc.vector.tensor_tensor(fo[:, :, :], fo[:, :, :], fy[b % 2][:, :, :], ALU.add))
                        xb = x[:, SUB * b:SUB * b + SUB, :]
                        nc.vector.tensor_tensor(xb, xb, fo[:, :, :], ALU.add).then_inc(ffn_done, 1)
                        dve.wait_ge(ffn_done, b + 1)

            def route_f(b):
                dve.wait_ge(lgf_ps, b + 1)
                lg = bank(0).rearrange("p (s f n) -> p s f n", s=SUB, f=1)[:, :, :, 0:NODES]
                route(2, lg, leaf_nof[b][:, :], (decf_ready, 1, b + 1), (idxf_ready, 1, b + 1))

            def peer_norm(b):
                xb = x[:, SUB * b:SUB * b + SUB, :]
                dve.wait_ge(x_ready, 3 * B + b + 1)
                stats_of(xb, mv)
                if b == 0:
                    dve.wait_ge(in_keys, 320)
                nc.vector.tensor_scalar(var_e[:, :], mv[:, :, 1], 1e-5, None, ALU.add).then_inc(pv2, 1)
                dve.wait_ge(pp2, 2 * b + 1)
                normed(ln, xb, mv, rstd, None)
                stats_of(ln, mv2)
                link(nc.vector.tensor_tensor(pss[:, :], mv2[:, :, 0], mv2[:, :, 0], ALU.mult))
                link(nc.vector.tensor_tensor(pss[:, :], pss[:, :], mv2[:, :, 1], ALU.add))
                nc.vector.tensor_scalar(pss[:, :], pss[:, :], float(E), None, ALU.mult).then_inc(pv2, 1)
                dve.wait_ge(pp2, 2 * b + 2)
                link(nc.vector.tensor_scalar(pn[:, :], pn[:, :], 1e-12, None, ALU.max))
                link(nc.vector.reciprocal(pn[:, :], pn[:, :]))
                link(nc.vector.tensor_scalar(pn[:, :], pn[:, :], float(E) ** 0.5, None, ALU.mult))
                if b >= 2:
                    dve.wait_ge(pxt_ps, b - 1)
                for s in range(SUB):
                    i = nc.vector.scalar_tensor_tensor(out=px[b % 2][:, s, :], in0=ln[:, s, :], scalar=pn[:, s:s + 1],
                                                       in1=gamma_sb[:, :], op0=ALU.mult, op1=ALU.mult)
                    if s < SUB - 1:
                        link(i)
                i.then_inc(px_ready, 1)
                dve.wait_ge(px_ready, b + 1)

            def topk_step(t, j):
                st = sim[:, t, :, :]
                tp = top[t % 2]

                def best8(out, src, n):
                    for g in range(n):
                        i = nc.vector.max(out[g], src[g])
                    link(i)

                if j == 0:
                    dve.wait_ge(sim_ready, t + 1)
                    best8([best[:, g, 0:8] for g in range(16)], [st[:, g, :] for g in range(16)], 16)
                elif j == 1:
                    for g in range(16):
                        i = nc.vector.match_replace(simw[:, g, :], best[:, g, 0:8], st[:, g, :], -3e38)
                    link(i)
                elif j == 2:
                    best8([best[:, g, 8:16] for g in range(16)], [simw[:, g, :] for g in range(16)], 16)
                elif j == 3:
                    off = 0
                    for a in range(8):
                        n = NCAND[a]
                        nc.vector.tensor_tensor(pairs[:, :, off:off + n], best[:, 0:PH, a:a + 1].to_broadcast([P, PH, n]),
                                                best[:, PH:2 * PH, 0:n], ALU.add)
                        off += n
                    link(nc.vector.tensor_tensor(pairs[:, :, off:CAND], best[:, 0:PH, 8:TOPK],
                                                 best[:, PH:2 * PH, 0:1].to_broadcast([P, PH, 8]), ALU.add))
                elif j == 4:
                    best8([tp[:, g, 0:8] for g in range(PH)], [pairs[:, g, :] for g in range(PH)], PH)
                elif j == 5:
                    for g in range(PH):
                        i = nc.vector.match_replace(pairw[:, g, :], tp[:, g, 0:8], pairs[:, g, :], -3e38)
                    link(i)
                elif j == 6:
                    best8([tp[:, g, 8:16] for g in range(PH)], [pairw[:, g, :] for g in range(PH)], PH)
                    nc.vector.tensor_tensor(tdif[:, :, :], tp[:, :, :], tp[:, :, 0:1].to_broadcast([P, PH, TOPK]),
                                            ALU.subtract).then_inc(tdif_ready, 1)
                    link(nc.vector.tensor_scalar(tneg[t % 2][:, :], tp[:, :, 0], -1.0, None, ALU.mult))
                else:
                    dve.wait_ge(texp_ready, t + 1)
                    link(nc.vector.tensor_reduce(tsum[:, :], texp[:, :, :], AX.X, ALU.add))
                    link(nc.vector.reciprocal(trec[:, :], tsum[:, :]))
                    if t >= 2:
                        dve.wait_ge(mix_ps, (t - 1) * PH)
                    for h in range(PH):
                        i = nc.vector.tensor_scalar(diag[t % 2][:, h, :], identf[:, :], trec[:, h:h + 1], None, ALU.mult)
                    i.then_inc(diag_ready, 1)

            def peer():
                for b in range(B):
                    peer_norm(b)
                for j in range(8):
                    topk_step(0, j)

                def mix(t):
                    dve.wait_ge(mix_ps, PH * (t + 1))
                    if t == 0:
                        dve.wait_ge(hp_ready, B)
                    else:
                        dve.wait_ge(po_ps, t)
                    st = psum[:, (t % 2) * 2 * BANK:((t % 2) * 2 + 2) * BANK].rearrange("p (c n) -> p c n", c=8)
                    nc.vector.tensor_tensor(mixed, st, hg[:, :, t * P:t * P + P], ALU.mult).then_inc(mixed_ready, 1)

                def add(t):
                    dve.wait_ge(po_ps, t + 1)
                    nc.vector.tensor_tensor(x[:, t, :], bank((t % 2) * 2, 0, P), x[:, t, :], ALU.add).then_inc(tile_ready, 1)

                for t in range(T):
                    for h in range(PH):
                        k = t * PH + h
                        dve.wait_ge(e_ready, k + 1)
                        if k >= 2:
                            dve.wait_ge(mix_ps, k - 1)
                        nc.vector.scalar_tensor_tensor(out=picked[k % 2], in0=grid[k % 3],
                                                       scalar=top[t % 2][:, h, TOPK - 1:TOPK],
                                                       in1=psum[:, (4 + 2 * (k % 2)) * BANK:(6 + 2 * (k % 2)) * BANK],
                                                       op0=ALU.is_ge, op1=ALU.mult).then_inc(picked_ready, 1)
                        if t + 1 < T:
                            topk_step(t + 1, h)
                        if t >= 1 and h == 1:
                            mix(t - 1)
                        if t >= 1 and h == 3:
                            add(t - 1)
                mix(T - 1)
                add(T - 1)

            run(*RUNS[0])
            ffn()
            run(*RUNS[1])
            peer()

        @block.tensor
        def _(pe):
            def bias_row(r):
                return bias_sb[0:1, r, :]

            BIAS = {(0, 0): 0, (0, 1): 1, (0, 2): 2, (0, 3): 3, (1, 0): 4, (1, 1): 5, (1, 2): 6, (1, 3): 7, (3, 3): 8}

            def pre(n):
                a, b = stage(n), batch(n)
                pe.wait_ge(xn_ready, n + 1)
                if n >= 1:
                    pe.wait_ge(xt_ready, n)
                if tails_ahead(n):
                    pe.wait_ge(ot_ready, tails_ahead(n))
                for s in range(SUB):
                    i = nc.tensor.transpose(bank(4, s * P, s * P + P), xn[n % 3][:, s, :], identf[:, :])
                i.then_inc(xt_ps, 1)
                pe.wait_ge(xt_ready, n + 1)
                if n >= 1:
                    pe.wait_ge(qk_ready, n)
                    pe.wait_ge(v_ready, n)
                own = xn_t[n % 2][:, :]
                kv = ctx_t[:, b * S:(b + 1) * S] if a in (1, 3) else own
                for w, src in ((0, own), (1, kv)):
                    row = BIAS.get((a, w))
                    o = bank(5, w * S, w * S + S)
                    i = nc.tensor.matmul(o, w_sb[:, 4 * a + w, :], src, start=True, stop=row is None)
                    if row is not None:
                        i = nc.tensor.matmul(o, bias_row(row), ones[0:1, :], start=False, stop=True)
                i.then_inc(qk_ps, 1)
                row = BIAS.get((a, 2))
                if tails_ahead(n):
                    pe.wait_ge(x_ready, tails_ahead(n))
                for s in range(SUB):
                    o = bank(6, s * P, s * P + P)
                    i = nc.tensor.matmul(o, kv[:, s * P:s * P + P], w_sb[:, 4 * a + 2, :], start=True, stop=row is None)
                    if row is not None:
                        i = nc.tensor.matmul(o, ones[0:1, 0:P], bias_row(row), start=False, stop=True)
                i.then_inc(v_ps, 1)

            def tail_a(n):
                pe.wait_ge(o_ready, n + 1)
                pe.wait_ge(xt_ready, pres_ahead(n))
                for s in range(SUB):
                    i = nc.tensor.transpose(bank(4, S + s * P, S + s * P + P), o_n[:, s, :], identf[:, :])
                i.then_inc(ot_ps, 1)

            def tail_b(n):
                a = stage(n)
                row = BIAS.get((a, 3))
                pe.wait_ge(ot_ready, n + 1)
                pe.wait_ge(v_ready, pres_ahead(n))
                if n >= 1:
                    pe.wait_ge(x_ready, n)
                for s in range(SUB):
                    o = bank(6, S + s * P, S + s * P + P)
                    i = nc.tensor.matmul(o, o_t[:, s * P:s * P + P], w_sb[:, 4 * a + 3, :], start=True, stop=row is None)
                    if row is not None:
                        i = nc.tensor.matmul(o, ones[0:1, 0:P], bias_row(row), start=False, stop=True)
                i.then_inc(y_ps, 1)

            def score_rows(n, h):
                k = (n - B) * H + h
                if h == 0:
                    pe.wait_ge(stk_ready[n % 3], 16 * 12 * placed(n))
                if k >= 2:
                    pe.wait_ge(rows_max, k - 1)
                t = stk[n % 3]
                for s in range(SUB):
                    o = bank(k % 2, s * S, s * S + S)
                    c = stage(n) == 2
                    i = nc.tensor.matmul(o, t[0:KS, h, 0, s * P:s * P + P], t[0:KS, h, 1, :], start=True, stop=not c)
                    if c:
                        i = nc.tensor.matmul(o, identb[:, :], causal_q[:, s, :], start=False, stop=True)
                i.then_inc(rows_ps, 1)

            def score_cols(n, h):
                k = (n - B) * H + h
                if h == 0:
                    pe.wait_ge(mt_ready, n - B + 1)
                if k >= 2:
                    pe.wait_ge(probs_ready, k - 1)
                t = stk[n % 3]
                for c in range(SUB):
                    o = bank(2 + k % 2, c * S, c * S + S)
                    nc.tensor.matmul(o, t[0:KS, h, 1, c * P:c * P + P], t[0:KS, h, 0, :], start=True, stop=False)
                    if stage(n) == 2:
                        nc.tensor.matmul(o, identb[:, :], causal_k[:, c, :], start=False, stop=False)
                    i = nc.tensor.matmul(o, sel16[:, h, :], mt[n % 2][:, :], start=False, stop=True)
                i.then_inc(cols_ps, 1)

            def values(n, h):
                k = (n - B) * H + h
                pe.wait_ge(probs_ready, k + 1)
                if h == 0:
                    pe.wait_ge(v_ready, n + 1)
                    pe.wait_ge(mt_ready, n - B + 1)
                for s in range(SUB):
                    for c in range(SUB):
                        i = nc.tensor.matmul(bank_o(s, h), probs[k % 3][:, c, s * P:s * P + P],
                                             vaug[n % 4][:, c, h, :], start=(c == 0), stop=(c == SUB - 1))
                i.then_inc(pv_ps, 1)

            def max_turn(n):
                pe.wait_ge(mparts_ready, n - B + 1)
                pe.wait_ge(o_ready, n)
                for s in range(SUB):
                    i = nc.tensor.transpose(mt_bank[:, s * P:s * P + P],
                                            mparts[n % 2][:, s, :, :].rearrange("p a h -> p (a h)"), identb[:, :])
                i.then_inc(mt_ps, 1)

            pe.wait_ge(consts, 1)
            pe.wait_ge(in_ctx, 48)
            for t in range(T):
                i = nc.tensor.transpose(psum[:, t * P:t * P + P], ctx_rows[:, t, :], identf[:, :])
                if t % 4 == 3:
                    i.then_inc(ctxt_ps, 1)
            pe.wait_ge(in_w, 48)
            pe.wait_ge(feat_ready, 1)
            for n in range(B):
                pre(n)
                if n >= 1:
                    pe.wait_ge(qft_ready, n)
                    pe.wait_ge(zk_ready, n)
                else:
                    pe.wait_ge(ctxt_ready, 2)
                pe.wait_ge(qk_ready, n + 1)
                fw = feat_w[:, :, :].rearrange("p h m -> p (h m)")
                for w in range(2):
                    for s in range(SUB):
                        nc.tensor.matmul(bank(2 * w + s), qk_f[n % 2][:, w, s * P:s * P + P], fw, start=True, stop=True)
                pe.wait_ge(sq_ready, n + 1)
                for w in range(2):
                    for s in range(SUB):
                        j = (w * SUB + s) * H
                        i = nc.tensor.matmul(bank(7, j, j + H), sq[:, w, s * P:s * P + P], half16[:, :], start=True, stop=True)
                i.then_inc(dd_ps, 1)
                pe.wait_ge(eq_ready, n + 1)
                for s in range(SUB):
                    for g in range(HG):
                        j = (s * HG + g) * P
                        i = nc.tensor.transpose(psum[:, j:j + P], eq[:, j:j + P], identf[:, :])
                i.then_inc(qft_ps, 1)
            for n in range(B):
                pe.wait_ge(kf_ready, n + 1)
                if n == 0:
                    pe.wait_ge(zk_ready, B)
                    pe.wait_ge(qft_ready, B)
                    pe.wait_ge(v_ready, B)
                else:
                    pe.wait_ge(cx_ready, n)
                for g in range(HG):
                    for s in range(SUB):
                        i = nc.tensor.matmul(bank(3, g * 36, g * 36 + 36), kf[n % 2][:, s, g * P:g * P + P],
                                             vaug[n % 4][:, s, g * HG:g * HG + HG, :].rearrange("p h c -> p (h c)"),
                                             start=(s == 0), stop=(s == SUB - 1))
                i.then_inc(cx_ps, 1)
                pe.wait_ge(cx_ready, n + 1)
                if n >= 1:
                    pe.wait_ge(o_ready, n)
                for s in range(SUB):
                    for g in range(HG):
                        i = nc.tensor.matmul(bank_o(s, g * HG, HG), qf_t[:, SUB * n + s, g, :], ctx_m[:, g, :],
                                             start=True, stop=True)
                i.then_inc(pv_ps, 1)
                tail_a(n)
                tail_b(n)

            def run(first, last):
                pre(first)
                pre(first + 1)
                for h in range(H):
                    score_rows(first, h)
                for n in range(first, last + 1):
                    if n + 2 <= last:
                        pre(n + 2)
                    max_turn(n)
                    for h in range(H):
                        score_cols(n, h)
                        if n + 1 <= last:
                            score_rows(n + 1, h)
                        if h >= 1:
                            values(n, h - 1)
                        if n > first and h == 3:
                            tail_a(n - 1)
                        if n > first and h == 6:
                            tail_b(n - 1)
                    values(n, H - 1)
                tail_a(last)
                tail_b(last)

            def logits(s, f, src, o):
                o = o[:, 0:NODES]
                nc.tensor.matmul(o, src[:, s * P:s * P + P], nodes_sb[:, f, :], start=True, stop=False)
                return nc.tensor.matmul(o, ones[0:1, 0:P], nodeb_sb[0:1, f, :], start=False, stop=True)

            def ffn():
                pe.wait_ge(in_tab, 32)
                pe.wait_ge(ot_ready, 2 * B)
                for b in range(B):
                    pe.wait_ge(fx_ready, b + 1)
                    if b >= 1:
                        pe.wait_ge(dec_ready, b)
                    for s in range(SUB):
                        i = nc.tensor.transpose(bank(4, s * P, s * P + P), fx[:, SUB * b + s, :], identf[:, :])
                    i.then_inc(fxt_ps, 1)
                    pe.wait_ge(fxt_ready, b + 1)
                    for s in range(SUB):
                        for f in range(3):
                            j = (s * 4 + f) * S
                            i = logits(s, f, fx_t, psum[:, j:j + S])
                    i.then_inc(lg_ps, 1)
                pe.wait_ge(dec_ready, B)
                for b in range(B):
                    g = ORDER.index((b, SUB - 1, 2))
                    pe.wait_ge(leaf_done, g + 1)
                    t = qkv[b % 2]
                    if b >= 1:
                        pe.wait_ge(fyt_ready, b)
                    for f in range(2):
                        for s in range(SUB):
                            j = (f * SUB + s) * P
                            i = nc.tensor.transpose(bank(4, j, j + P), t[:, s, f, :], identf[:, :])
                    i.then_inc(fqk_ps, 1)
                    pe.wait_ge(fqk_ready, b + 1)
                    if b >= 1:
                        pe.wait_ge(att_ready, SUB * b)
                    for s in range(SUB):
                        i = nc.tensor.matmul(bank(5, s * S, s * S + S), fqk_t[:, s * P:s * P + P], fqk_t[:, S:2 * S],
                                             start=True, stop=True)
                    i.then_inc(fs_ps, 1)
                    pe.wait_ge(att_ready, SUB * (b + 1))
                    if b >= 1:
                        pe.wait_ge(at_ready, b)
                    for s in range(SUB):
                        for c in range(SUB):
                            j = (s * SUB + c) * P
                            i = nc.tensor.transpose(bank(6, j, j + P), att[:, s, c * P:c * P + P], identf[:, :])
                    i.then_inc(at_ps, 1)
                    pe.wait_ge(at_ready, b + 1)
                    if b >= 1:
                        pe.wait_ge(fy_ready, b)
                    for s in range(SUB):
                        for c in range(SUB):
                            i = nc.tensor.matmul(bank(7, s * P, s * P + P), att_t[:, s * SUB + c, :], t[:, c, 2, :],
                                                 start=(c == 0), stop=(c == SUB - 1))
                    i.then_inc(fy_ps, 1)
                    pe.wait_ge(fy_ready, b + 1)
                    for s in range(SUB):
                        i = nc.tensor.transpose(bank(4, s * P, s * P + P), fy[b % 2][:, s, :], identf[:, :])
                    i.then_inc(fyt_ps, 1)
                    pe.wait_ge(fyt_ready, b + 1)
                    if b >= 1:
                        pe.wait_ge(decf_ready, b)
                    for s in range(SUB):
                        i = logits(s, 3, fy_t, bank(0, s * S, s * S + S))
                    i.then_inc(lgf_ps, 1)
                pe.wait_ge(decf_ready, B)

            def peer():
                pe.wait_ge(in_keys, 320)
                pe.wait_ge(ot_ready, 4 * B)
                for b in range(B):
                    pe.wait_ge(px_ready, b + 1)
                    for s in range(SUB):
                        i = nc.tensor.transpose(bank(4, s * P, s * P + P), px[b % 2][:, s, :], identf[:, :])
                    i.then_inc(pxt_ps, 1)
                    pe.wait_ge(pxt_ready, b + 1)
                    if b >= 1:
                        pe.wait_ge(hp_ready, b)
                    for c in range(8):
                        i = nc.tensor.matmul(psum[:, c * S:(c + 1) * S], wq_sb[:, c * P:c * P + P], px_t[:, :],
                                             start=True, stop=True)
                    i.then_inc(qp_ps, 1)
                    pe.wait_ge(qp_ready, b + 1)
                    for s in range(SUB):
                        if b >= 1:
                            pe.wait_ge(sim_ready, SUB * (b - 1) + s + 1)
                        for c in range(8):
                            i = nc.tensor.matmul(bank(5 + s, c * 2 * PK, (c + 1) * 2 * PK), qp_t[:, c, s * P:s * P + P],
                                                 keys_sb[:, c, :], start=True, stop=True)
                        i.then_inc(sim_ps, 1)
                    for c in range(8):
                        i = nc.tensor.matmul(psum[:, c * S:(c + 1) * S], down_sb[:, c * P:c * P + P], px_t[:, :],
                                             start=True, stop=True)
                    i.then_inc(hp_ps, 1)
                pe.wait_ge(hp_ready, B)

                def out_of(t):
                    pe.wait_ge(mixed_ready, t + 1)
                    for c in range(8):
                        i = nc.tensor.matmul(bank((t % 2) * 2, 0, P), mixed[:, c, :], up_sb[:, c, :],
                                             start=(c == 0), stop=(c == 7))
                    i.then_inc(po_ps, 1)

                for t in range(T):
                    pe.wait_ge(diag_ready, t + 1)
                    if t >= 2:
                        pe.wait_ge(tile_ready, t - 1)
                    for h in range(PH):
                        k = t * PH + h
                        pe.wait_ge(picked_ready, k + 1)
                        for c in range(8):
                            o = ((t % 2) * 2) * BANK + c * P
                            i = nc.tensor.matmul(psum[:, o:o + P], picked[k % 2][:, c * P:c * P + P], diag[t % 2][:, h, :],
                                                 start=(h == 0 and c % 4 == 0), stop=(h == PH - 1),
                                                 skip_group_check=True)
                        i.then_inc(mix_ps, 1)
                        if t >= 1 and h == 2:
                            out_of(t - 1)
                out_of(T - 1)

            pe.wait_ge(consts, 2)
            run(*RUNS[0])
            ffn()
            run(*RUNS[1])
            peer()


def kernel(**a):
    import numpy as np
    import concourse.bacc as bacc
    from concourse.bass_utils import run_bass_kernel_spmd

    a = {k: np.asarray(v) for k, v in a.items()}

    def by_width(w):
        return w.reshape(w.shape[:-1] + (H, D)).swapaxes(-1, -2).reshape(w.shape)

    ws = []
    for names in (("L0_attn_Wq", "L0_attn_Wk", "L0_attn_Wv", "L0_attn_Wo"),
                  ("L0_xattn_wq", "L0_xattn_wk", "L0_xattn_wv", "L0_xattn_wo"),
                  ("L1_attn_Wq", "L1_attn_Wk", "L1_attn_Wv", "L1_attn_Wo"),
                  ("L1_xattn_Wq", "L1_xattn_Wk", "L1_xattn_Wv", "L1_xattn_Wo")):
        q, k, v, o = (a[n].T for n in names)
        ws += [by_width(q), by_width(k), v, o]
    bias = [by_width(a["L0_attn_bq"]), by_width(a["L0_attn_bk"]), a["L0_attn_bv"], a["L0_attn_bo"],
            by_width(a["L0_xattn_bq"]), by_width(a["L0_xattn_bk"]), a["L0_xattn_bv"], a["L0_xattn_bo"],
            a["L1_xattn_bo"]]
    kinds = "qkvf"

    def leaves(c):
        w1, w2 = a[f"L0_ffn_{c}_w1"], a[f"L0_ffn_{c}_w2"]
        return np.concatenate([w1.transpose(0, 2, 1).reshape(LEAVES, LW * E), a[f"L0_ffn_{c}_b1"],
                               w2.reshape(LEAVES, LW * E), a[f"L0_ffn_{c}_b2"]], axis=1)

    ins = {
        "x_in": a["x"], "ctx_in": a["ctx_1024"], "mask_in": a["mask_BxS_ik0"],
        "attn_w": np.stack(ws), "attn_bias": np.stack(bias),
        "proj_t": np.repeat(a["L0_attn_proj"].T, H, axis=0),
        "node_w": np.stack([a[f"L0_ffn_{c}_nw"].T for c in kinds], axis=1),
        "node_b": np.stack([a[f"L0_ffn_{c}_nb"] for c in kinds])[None],
        "tab_q": leaves("q"), "tab_k": leaves("k"), "tab_v": leaves("v"), "tab_f": leaves("f"),
        "gamma_in": a["L1_ffn_gamma"], "peer_wq": a["L1_ffn_wq"].T,
        "peer_keys": a["L1_ffn_keys"].transpose(2, 0, 3, 1),
        "table_down": a["L1_ffn_table_down"][:EXPERTS].T, "table_up": a["L1_ffn_table_up"][:EXPERTS],
    }
    nc = bacc.Bacc("TRN2", target_bir_lowering=False, num_devices=1)
    arrays, aps = {}, []
    for name, v in ins.items():
        v = np.ascontiguousarray(v)
        arrays[name] = v
        aps.append(nc.dram_tensor(name, v.shape, mybir.dt.from_np(v.dtype), kind="ExternalInput").ap())
    out = nc.dram_tensor("out", (B, S, E), mybir.dt.float32, kind="ExternalOutput").ap()
    decoder_program(nc, *aps, out)
    r = run_bass_kernel_spmd(nc, [arrays], core_ids=[0])
    return r.results[0]["out"]
```

```python
import concourse.bass as bass
from concourse import mybir
from contextlib import ExitStack

B, S, E, H = 4, 256, 128, 16
D = E // H
P = 128
SUB = S // P
T = B * SUB
M = 4 * D
HG = P // M
DEPTH = 8
LEAVES = 2 ** DEPTH
NODES = LEAVES - 1
LW = 16
ROW = LW * E + LW + LW * E + E
PK = 32
PH = 8
PD = 64
TOPK = 16
EXPERTS = PK * PK
NCAND = [TOPK // (a + 1) for a in range(TOPK)]
CAND = sum(NCAND)
TERMS = [(0, 0), (1, 0), (2, 0), (0, 1), (1, 1), (0, 2)]
KS = len(TERMS) * D
KM = KS + 3
BIG = 1.0e30
VW = 32


def decoder_program(nc, x_in, ctx_in, mask_in, attn_w, attn_bias, proj_t, node_w, node_b,
                    tab_q, tab_k, tab_v, tab_f, gamma_in, peer_wq, peer_keys, table_down,
                    table_up, out):
    f32, bf16 = mybir.dt.float32, mybir.dt.bfloat16
    i32, u32 = mybir.dt.int32, mybir.dt.uint32
    ALU = mybir.AluOpType
    ACT = mybir.ActivationFunctionType
    AX = mybir.AxisListType
    RMAX = bass.bass_isa.ReduceOp.max

    stack = ExitStack()
    with stack:
        def sb(name, shape, dt=f32):
            return stack.enter_context(nc.sbuf_tensor(name, shape, dt))

        def sem(name):
            return stack.enter_context(nc.semaphore(name))

        BANK = 512
        psum = stack.enter_context(nc.psum_tensor("psum", [P, 8 * BANK], f32))

        def bank(k, a=0, b=BANK):
            return psum[:, k * BANK + a:k * BANK + b]

        w_sb = sb("w_sb", [P, 16, P])
        NB = 9 * P + 4 * NODES
        bias_p = sb("bias_p", [3, NB], bf16)
        nodes_sb = sb("nodes_sb", [P, 4, NODES])
        gamma_sb = sb("gamma_sb", [P, P])
        wq_sb = sb("wq_sb", [P, 2 * PH * PD])
        keys_sb = sb("keys_sb", [P, 8, 2 * PK])
        down_sb = sb("down_sb", [P, EXPERTS])
        up_sb = sb("up_sb", [P, EXPERTS // P, P])
        maskrow = sb("maskrow", [P, B * S])
        identf = sb("identf", [P, P])
        identb = sb("identb", [P, P], bf16)
        ones = sb("ones", [3, S], bf16)
        head16 = sb("head16", [P, H])
        half16 = sb("half16", [P, H])
        projb = sb("projb", [P, M])
        feat_w = sb("feat_w", [P, H, M])
        blockm = sb("blockm", [P, HG, D + 1])
        causal_q = sb("causal_q", [P, P], bf16)
        causal_k = sb("causal_k", [P, P], bf16)
        halves = sb("halves", [P, 2, T])
        even_ids = sb("even_ids", [P, LEAVES // 2])
        arena2 = sb("arena2", [P, 5120])
        bias_sb = arena2[0:3, 2948:2948 + NB]
        bias_w = arena2[0:3, 1800:1800 + NB // 2].bitcast(bf16)
        arena3 = sb("arena3", [P, 3072])

        x = sb("x", [P, T, P])
        ctx_t = sb("ctx_t", [P, B * S])
        stats = sb("stats", [P, 2, 6])
        mv = sb("mv", [P, 2, 2])
        var_e = sb("var_e", [P, 2])
        rstd = sb("rstd", [P, 2])
        xn = [sb(f"xn{i}", [P, SUB, P]) for i in range(3)]
        xn_t = [sb(f"xn_t{i}", [P, S]) for i in range(2)]
        qk_f = [sb(f"qk_f{i}", [P, 2, S]) for i in range(2)]
        resid_f = sb("resid_f", [P, 2, S])
        parts = [sb(f"parts{i}", [P, 3, 2, S], bf16) for i in range(2)]
        vaug = [sb(f"vaug{i}", [P, SUB, H, VW]) for i in range(4)]
        rowmax = [sb(f"rowmax{i}", [P, SUB, H]) for i in range(2)]
        negmax = sb("negmax", [P, SUB, H])
        remax = sb("remax", [P, SUB, H])
        mparts = [sb(f"mparts{i}", [P, SUB, 3, H], bf16) for i in range(2)]
        mt = [sb(f"mt{i}", [3 * H, S], bf16) for i in range(2)]
        probs = [arena3[:, i * 512:(i + 1) * 512] for i in range(4)]
        o_sb = arena3[:, 2048:3072].rearrange("p (g n) -> p g n", n=S)
        rsum = sb("rsum", [P, SUB, H])
        o_n = sb("o_n", [P, SUB, P])
        o_t = sb("o_t", [P, S])
        arena = sb("arena", [P, 17408])
        aw = arena[:, :].bitcast(bf16)
        STK = H * 2 * S
        stk = [aw[0:64, i * STK:(i + 1) * STK].rearrange("p (h w n) -> p h w n", h=H, w=2)
               for i in range(3)]
        leaf_rows = [arena[:, i * ROW:(i + 1) * ROW] for i in range(4)]
        zk = arena[:, 12288:16384].rearrange("p (t c) -> p t c", t=T)
        qf_t = arena2[:, 0:4096].rearrange("p (t g n) -> p t g n", t=T, g=HG)
        zq = arena3[:, 0:1024]
        eq = arena3[:, 1024:2048]
        kf = [k.rearrange("p (s c) -> p s c", s=SUB) for k in (arena3[:, 2048:3072], arena[:, 16384:17408])]
        sq = sb("sq", [P, 2, S])
        ctx_m = sb("ctx_m", [P, HG, HG * (D + 1)])
        ctx_rows = arena[:, 8192:9216].rearrange("p (t n) -> p t n", t=T)
        mask_i = arena[:, 9216:10240].bitcast(i32)
        stab = sb("stab", [P, 2, H])
        kmax = sb("kmax", [P, T])
        kmax1 = sb("kmax1", [P, 1])
        kmaxg = sb("kmaxg", [P, 1])
        nkmax = sb("nkmax", [P, 1])

        fx = sb("fx", [P, T, P])
        fstats, fmean = sb("fstats", [P, T, 6]), sb("fmean", [P, T, 2])
        fpow = [sb(f"fpow{i}", [P, T]) for i in range(4)]
        fx_t = arena3[:, 0:256]
        dec = arena2[:, 0:768].bitcast(i32).rearrange("p (f n) -> p f n", f=6)
        walk = arena2[:, 768:1536].rearrange("p (f n) -> p f n", f=6)
        leaf_no = [sb(f"leaf_no{i}", [P, 6], u32) for i in range(B)]
        leaf_nof = [sb(f"leaf_nof{i}", [P, 2], u32) for i in range(B)]
        hid = [sb(f"hid{i}", [P, LW]) for i in range(4)]
        hact = [sb(f"hact{i}", [P, LW]) for i in range(2)]
        fqk_t = [arena2[:, 3072 + i * 512:3584 + i * 512].rearrange("p (f n) -> p f n", f=2) for i in range(2)]
        fval = [arena2[:, 4096 + i * 256:4352 + i * 256].rearrange("p (s e) -> p s e", s=SUB) for i in range(2)]
        frow = sb("frow", [P, 2])
        fneg = sb("fneg", [P, 2])
        fsum = sb("fsum", [P, 2])
        frec = sb("frec", [P, 2])
        att = arena2[:, 4608:5120].rearrange("p (s n) -> p s n", s=SUB)
        att_t = arena3[:, 768:1280].rearrange("p (c n) -> p c n", c=4)
        fy = [arena3[:, 1280 + i * 256:1536 + i * 256].rearrange("p (s e) -> p s e", s=SUB) for i in range(2)]
        fy_t = arena3[:, 1792:2048]
        qp_t = [i.rearrange("p (c n) -> p c n", c=8) for i in (arena[:, 0:2048], arena2[:, 0:2048])]
        sim = arena[:, 2048:6144].rearrange("p (t g k) -> p t g k", t=T, g=2 * PH)
        hg = arena[:, 6144:14336].rearrange("p (c n) -> p c n", c=8)
        grid = [arena[:, 14336 + i * 1024:15360 + i * 1024] for i in range(3)]
        picked = [arena2[:, i * 1024:(i + 1) * 1024] for i in range(2)]
        px_t = [arena3[:, i:i + 2 * S] for i in (0, 2404)]
        simw = arena3[:, 768:1280].rearrange("p (g k) -> p g k", k=PK)
        best = arena3[:, 1280:1536].rearrange("p (g k) -> p g k", k=TOPK)
        pairs = arena3[:, 1536:1536 + PH * CAND].rearrange("p (g k) -> p g k", k=CAND)
        pairw = arena3[:, 2000:2000 + PH * CAND].rearrange("p (g k) -> p g k", k=CAND)
        top = [vaug[t // SUB][:, t % SUB, 0:PH, 0:TOPK] for t in range(T)]
        texp = [vaug[t // SUB][:, t % SUB, PH:2 * PH, 0:TOPK] for t in range(T)]
        tneg = sb("tneg", [P, T, PH])
        tsum = sb("tsum", [P, PH])
        trec = [sb(f"trec{i}", [P, PH]) for i in range(2)]
        diag = [arena2[:, 2048 + i * 1024:3072 + i * 1024].rearrange("p (h n) -> p h n", h=PH) for i in range(2)]
        mixed = arena2[:, 4096:5120].rearrange("p (c n) -> p c n", c=8)

        in_x, in_w, in_ctx = sem("in_x"), sem("in_w"), sem("in_ctx")
        in_tab, in_keys, zeros_done = sem("in_tab"), sem("in_keys"), sem("zeros_done")
        consts = sem("consts")
        ctxt_ps, ctxt_ready, mask_ready, feat_ready = (sem("ctxt_ps"), sem("ctxt_ready"),
                                                       sem("mask_ready"), sem("feat_ready"))
        var_ready, rstd_ready, xn_ready = sem("var_ready"), sem("rstd_ready"), sem("xn_ready")
        xt_ps, xt_ready = sem("xt_ps"), sem("xt_ready")
        qk_ps, qk_ready, v_ps, v_ready = sem("qk_ps"), sem("qk_ready"), sem("v_ps"), sem("v_ready")
        parts_ready = sem("parts_ready")
        stk_ready = [sem(f"stk_ready{i}") for i in range(3)]
        max_in = [sem(f"max_in{i}") for i in range(3)]
        ones_ready = sem("ones_ready")
        rows_ps, rows_max = sem("rows_ps"), sem("rows_max")
        mparts_ready, mt_ps, mt_ready = sem("mparts_ready"), sem("mt_ps"), sem("mt_ready")
        cols_ps, probs_ready, pv_ps = sem("cols_ps"), sem("probs_ready"), sem("pv_ps")
        o_ready, ot_ps, ot_ready = sem("o_ready"), sem("ot_ps"), sem("ot_ready")
        y_ps, x_ready = sem("y_ps"), sem("x_ready")
        sq_ready, dd_ps, zq_ready, zk_ready = sem("sq_ready"), sem("dd_ps"), sem("zq_ready"), sem("zk_ready")
        eq_ready, qft_ps, qft_ready = sem("eq_ready"), sem("qft_ps"), sem("qft_ready")
        kmax_ready, kmax_all, nkmax_ready = sem("kmax_ready"), sem("kmax_all"), sem("nkmax_ready")
        ke_ready, kf_ready, cx_ps, cx_ready = sem("ke_ready"), sem("kf_ready"), sem("cx_ps"), sem("cx_ready")
        dve_step, act_step, pool_step = sem("dve_step"), sem("act_step"), sem("pool_step")
        out_done = sem("out_done")
        bias_ready, osb_ready, or_ps = sem("bias_ready"), sem("osb_ready"), sem("or_ps")
        fv, fp, fx_ready, fxt_ps, fxt_ready, lg_ps = (sem("fv"), sem("fp"), sem("fx_ready"), sem("fxt_ps"),
                                                      sem("fxt_ready"), sem("lg_ps"))
        dec_ready, idx_ready, leaf_done = sem("dec_ready"), sem("idx_ready"), sem("leaf_done")
        rows_in = [sem(f"rows_in{i}") for i in range(4)]
        scaled, leaf_kept, leaf_added = sem("scaled"), sem("leaf_kept"), sem("leaf_added")
        fs_ps, fmax_ready = sem("fs_ps"), sem("fmax_ready")
        att_ready, at_ps, at_ready, fy_ps, fy_ready = (sem("att_ready"), sem("at_ps"), sem("at_ready"),
                                                       sem("fy_ps"), sem("fy_ready"))
        fyt_ps, fyt_ready, lgf_ps, decf_ready, idxf_ready = (sem("fyt_ps"), sem("fyt_ready"), sem("lgf_ps"),
                                                             sem("decf_ready"), sem("idxf_ready"))
        fh_ready, fg_ready = sem("fh_ready"), sem("fg_ready")
        pv2, pp2, px_ready, pxt_ps, pxt_ready = (sem("pv2"), sem("pp2"), sem("px_ready"), sem("pxt_ps"),
                                                 sem("pxt_ready"))
        unit_ps, unit_ready, sim_ps, sim_ready = sem("unit_ps"), sem("unit_ready"), sem("sim_ps"), sem("sim_ready")
        grid_ready, e_ready, picked_ready, mix_ps = sem("grid_ready"), sem("e_ready"), sem("picked_ready"), sem("mix_ps")
        tdif_ready, texp_ready, trec_ready, diag_ready = (sem("tdif_ready"), sem("texp_ready"), sem("trec_ready"),
                                                          sem("diag_ready"))
        mixed_ready, po_ps, tile_ready = sem("mixed_ready"), sem("po_ps"), sem("tile_ready")

        def chain(eng, s):
            n = [0]

            def link(i):
                n[0] += 1
                i.then_inc(s, 1)
                eng.wait_ge(s, n[0])
            return link

        def stage(n):
            return n // B

        def batch(n):
            return n % B

        def bank_o(s, h, n=1):
            return bank(7)[:, s * 144 + h * 9:s * 144 + (h + n) * 9]

        mt_bank = psum[0:3 * H, 5 * BANK:5 * BANK + P].bitcast(bf16)

        def split_bias(engine, link, a, b):
            src, w, p = bias_sb[:, a:b], bias_w[:, a:b], bias_p[:, a:b]
            link(engine.tensor_copy(w, src))
            link(engine.tensor_scalar(p, w, identf[0:3, 0:1], None, ALU.mult))
            for j in (1, 2):
                link(engine.tensor_tensor(src, src, w, ALU.subtract))
                link(engine.tensor_copy(w, src))
                link(engine.tensor_scalar(w, w, identf[0:3, j:j + 1], None, ALU.mult) if j == 2 else
                     engine.tensor_copy(w, src))
                if j == 1:
                    link(engine.scalar_tensor_tensor(out=p, in0=w, scalar=identf[0:3, 1:2], in1=p,
                                                     op0=ALU.mult, op1=ALU.add))
            link(engine.tensor_tensor(p, p, w, ALU.add))
        RUNS = [(4, 7), (8, 15)]

        def run_of(n):
            return next((r for r in RUNS if r[0] <= n <= r[1]), (0, B - 1))

        def tails_ahead(n):
            return 0 if n < B else max(n - 3, run_of(n)[0])

        def pres_ahead(n):
            first, last = run_of(n)
            return last + 1 if first == 0 else min(n + 4, last + 1)

        def turns_ahead(n):
            first = run_of(n)[0]
            return (max(n - 1, first + 1) if n - first > 1 else first) - B

        ROWS_AT = [[2 * h, 2 * h + 1] if h < 4 else [h + 4] if h < 12 else [] for h in range(H)]
        TURN = 14

        def placed(n):
            return len([m for m in range(B, n + 1) if m % 3 == n % 3])

        def finish_sp(sp):
            out_t = out.rearrange("b (s p) e -> p (b s) e", p=P)
            for t in range(T):
                sp.wait_ge(tile_ready, t + 1)
                sp.dma_start(out_t[:, t, :], x[:, t, :]).then_inc(out_done, 16)
            sp.wait_ge(out_done, 16 * T)

        ORDER, STAGES = [], []
        for slot in range(B + 2):
            now, a = [], slot - 1
            if slot < B:
                now += [(slot, s, f) for s in range(SUB) for f in range(3)]
            if slot >= 2 and slot != B - 1:
                now += [(b, s, 3) for b in range(B - 3 if slot == B else slot - 2, slot - 1) for s in range(SUB)]
            fill = [[] for _ in range(max(7, len(now) + 1))]
            if slot + 1 < B:
                fill[0] += [("turn", slot + 1)]
                fill[2] += [("route", slot + 1)]
            if 0 <= a < B:
                for j, what in enumerate(("score", "weigh", "mix", "attend", "turn_f", "route_f")):
                    fill[j if slot < B else (j + 1) // 2] += [(what, a)]
            for j, f in enumerate(fill):
                STAGES += f
                if j < len(now):
                    STAGES += [("leaf", len(ORDER))]
                    ORDER += [now[j]]

        def last_tree(g):
            return ORDER[g][2] == 3

        def leaves_upto(g, last):
            return len([i for i in range(g + 1) if last_tree(i) == last])

        UNITS = 4 * B
        AHEAD = 4

        def unit_bank(u):
            return psum[:, (u % 2) * 2 * BANK:((u % 2) * 2 + 2) * BANK]

        def px_of(b):
            return px_t[b // 2][:, b % 2 * S:(b % 2 + 1) * S]

        TABS = [tab_q, tab_k, tab_v, tab_f]

        block = stack.enter_context(nc.Block())

        @block.sync
        def _(sp):
            sp.dma_start(x[:, :, :], x_in.rearrange("b (s p) e -> p (b s) e", p=P)).then_inc(in_x, 16)
            sp.dma_start(w_sb[:, 0:4, :], attn_w[0:4].rearrange("a i o -> i a o")).then_inc(in_w, 16)
            sp.dma_start(bias_sb[:, 0:9 * P], attn_bias.partition_broadcast(3)).then_inc(in_w, 16)
            sp.dma_start(projb[:, :], proj_t).then_inc(in_w, 16)
            sp.dma_start(ctx_rows, ctx_in.rearrange("b (s p) e -> p (b s) e", p=P)).then_inc(in_ctx, 16)
            sp.dma_start(mask_i, mask_in.rearrange("b s -> (b s)").partition_broadcast(P)).then_inc(in_ctx, 16)
            sp.dma_start(w_sb[:, 4:16, :], attn_w[4:16].rearrange("a i o -> i a o")).then_inc(in_ctx, 16)
            sp.dma_start(nodes_sb[:, :, :], node_w).then_inc(in_tab, 16)
            sp.dma_start(bias_sb[:, 9 * P:NB], node_b.partition_broadcast(3)).then_inc(in_tab, 16)
            sp.dma_start(gamma_sb[:, :], gamma_in.partition_broadcast(P)).then_inc(in_keys, 16)
            sp.dma_start(wq_sb[:, :], peer_wq).then_inc(in_keys, 16)
            sp.dma_start(down_sb[:, :], table_down).then_inc(in_keys, 16)
            sp.dma_start(up_sb[:, :, :], table_up.rearrange("(c p) e -> p c e", p=P)).then_inc(in_keys, 16)
            sp.wait_ge(zeros_done, 1)
            for side in range(2):
                for h in range(PH):
                    r, c = (h % 2) * PD, side * 4 + h // 2
                    sp.dma_start(keys_sb[r:r + PD, c, (h % 2) * PK:(h % 2 + 1) * PK],
                                 peer_keys[side, h]).then_inc(in_keys, 16)

            def place(n):
                sp.wait_ge(parts_ready, n - B + 1)
                if n - 3 >= B:
                    sp.wait_ge(cols_ps, (n - 3 - B + 1) * H)
                for r, (qp, kp) in enumerate(TERMS):
                    for w, part in ((0, qp), (1, kp)):
                        sp.dma_start(stk[n % 3][r * D:(r + 1) * D, :, w, :],
                                     parts[n % 2][:, part, w, :]).then_inc(stk_ready[n % 3], 16)

            def place_max(n):
                sp.wait_ge(mt_ready, n - B + 1)
                sp.dma_start(stk[n % 3][KS:KM, :, 0, :], mt[n % 2][:, :]).then_inc(max_in[n % 3], 16)

            def run(first, last):
                sp.wait_ge(ones_ready, RUNS.index((first, last)) + 1)
                place(first)
                place(first + 1)
                place_max(first)
                for n in range(first, last + 1):
                    if n + 2 <= last:
                        place(n + 2)
                    if n + 1 <= last:
                        place_max(n + 1)

            run(*RUNS[0])
            run(*RUNS[1])
            finish_sp(sp)

        @block.gpsimd
        def _(pool):
            link = chain(pool, pool_step)
            nc.gpsimd.memset(keys_sb[:, :, :], 0.0).then_inc(zeros_done, 1)
            link(nc.gpsimd.memset(identf[:, :], 0.0))
            link(nc.gpsimd.affine_select(out=identf[:, :], in_=identf[:, :], compare_op=ALU.not_equal, fill=1.0,
                                         base=0, pattern=[[-1, P]], channel_multiplier=1))
            link(nc.gpsimd.tensor_copy(identb[:, :], identf[:, :]))
            link(nc.gpsimd.memset(ones[:, :], 1.0))
            link(nc.gpsimd.memset(halves[:, 0, :], -0.5))
            link(nc.gpsimd.memset(halves[:, 1, :], 0.5))
            link(nc.gpsimd.memset(head16[:, :], 0.0))
            for j in range(D):
                link(nc.gpsimd.affine_select(out=head16[:, :], in_=head16[:, :], compare_op=ALU.not_equal,
                                             fill=1.0, base=-H * j, pattern=[[-1, H]], channel_multiplier=1))
            for i in range(4):
                link(nc.gpsimd.memset(vaug[i][:, :, :, :], 0.0))
                link(nc.gpsimd.memset(vaug[i][:, :, :, D:D + 1], 1.0))
            link(nc.gpsimd.memset(blockm[:, :, :], 1.0))
            link(nc.gpsimd.affine_select(out=blockm[:, :, :], in_=blockm[:, :, :], compare_op=ALU.is_ge, fill=0.0,
                                         base=0, pattern=[[-M, HG], [0, D + 1]], channel_multiplier=1))
            link(nc.gpsimd.affine_select(out=blockm[:, :, :], in_=blockm[:, :, :], compare_op=ALU.is_ge, fill=0.0,
                                         base=M - 1, pattern=[[M, HG], [0, D + 1]], channel_multiplier=-1))
            nc.gpsimd.tensor_scalar(half16[:, :], head16[:, :], 0.5, None, ALU.mult).then_inc(consts, 1)

            def power(n):
                pool.wait_ge(var_ready, n + 1)
                nc.gpsimd.tensor_tensor(rstd[:, :], var_e[:, :], halves[:, 0, 0:2], ALU.pow).then_inc(rstd_ready, 1)

            def squares(n):
                pool.wait_ge(qk_ready, n + 1)
                if n >= 1:
                    pool.wait_ge(dd_ps, n)
                nc.gpsimd.tensor_tensor(sq[:, :, :], qk_f[n % 2][:, :, :], qk_f[n % 2][:, :, :], ALU.mult).then_inc(sq_ready, 1)

            def split(n):
                q = qk_f[n % 2][:, :, :]
                p = parts[n % 2]
                pool.wait_ge(qk_ready, n + 1)
                if n - 2 >= B:
                    pool.wait_ge(stk_ready[(n - 2) % 3], 16 * 12 * placed(n - 2))
                if stage(n) == 1:
                    b = batch(n)
                    link(nc.gpsimd.tensor_tensor(qk_f[n % 2][:, 0, :], qk_f[n % 2][:, 0, :],
                                                 maskrow[:, b * S:(b + 1) * S], ALU.mult))
                link(nc.gpsimd.tensor_copy(p[:, 0, :, :], q))
                link(nc.gpsimd.tensor_tensor(resid_f[:, :, :], q, p[:, 0, :, :], ALU.subtract))
                link(nc.gpsimd.tensor_copy(p[:, 1, :, :], resid_f[:, :, :]))
                nc.gpsimd.tensor_tensor(p[:, 2, :, :], resid_f[:, :, :], p[:, 1, :, :], ALU.subtract).then_inc(parts_ready, 1)
                pool.wait_ge(parts_ready, n - B + 1)

            for n in range(B):
                power(n)
                squares(n)
            for m, sign in ((causal_q, 1), (causal_k, -1)):
                link(nc.gpsimd.memset(m[:, :], 0.0))
                link(nc.gpsimd.affine_select(out=m[:, :], in_=m[:, :], compare_op=ALU.is_ge, fill=-BIG,
                                             base=0, pattern=[[-sign, P]], channel_multiplier=sign))
            link(nc.gpsimd.iota(even_ids[:, :], pattern=[[2, LEAVES // 2]], base=0, channel_multiplier=0,
                                allow_small_or_imprecise_dtypes=True))
            nc.gpsimd.memset(o_t[:, 0:1], 0.0).then_inc(consts, 1)
            pool.wait_ge(kmax_ready, 1)
            nc.gpsimd.partition_all_reduce(kmaxg[:, :], kmax1[:, :], P, RMAX).then_inc(kmax_all, 1)

            def run(first, last):
                if first == B:
                    pool.wait_ge(kmax_all, 1)
                    pool.wait_ge(mask_ready, 1)
                else:
                    pool.wait_ge(leaf_done, len(ORDER))
                for i in range(3):
                    i = nc.gpsimd.memset(stk[i][32:64, :, 1, :], 1.0)
                i.then_inc(ones_ready, 1)
                pool.wait_ge(ones_ready, RUNS.index((first, last)) + 1)
                for n in range(first, first + 3):
                    power(n)
                split(first)
                split(first + 1)
                for n in range(first, last + 1):
                    if n + 2 <= last:
                        split(n + 2)
                    if n + 3 <= last:
                        power(n + 3)

            def ffn():
                def powers(part, a, b):
                    for j, (i, o, e) in enumerate(((0, 1, 0), (0, 2, 1), (2, 3, 0))):
                        pool.wait_ge(fv, 3 * part + j + 1)
                        nc.gpsimd.tensor_tensor(fpow[o][:, a:b], fpow[i][:, a:b], halves[:, e, a:b],
                                                ALU.pow).then_inc(fp, 1)

                powers(0, 0, 2 * SUB)
                for g, (b, s, f) in enumerate(ORDER):
                    if g == 4:
                        powers(1, 2 * SUB, T)
                    if f == 3:
                        pool.wait_ge(idxf_ready, b + 1)
                        no = leaf_nof[b][:, s:s + 1]
                    else:
                        pool.wait_ge(idx_ready, b + 1)
                        no = leaf_no[b][:, f * SUB + s:f * SUB + s + 1]
                    if g >= 4:
                        pool.wait_ge(leaf_done, g - 3)
                    nc.gpsimd.indirect_dma_start(leaf_rows[g % 4], None, TABS[f],
                                                 bass.IndirectOffsetOnAxis(no, 0)).then_inc(rows_in[g % 4], 16)

            def peer():
                for part, (a, b) in enumerate(((0, 2 * SUB), (2 * SUB, T))):
                    for j, (i, o, e) in enumerate(((0, 1, 0), (2, 3, 1))):
                        pool.wait_ge(pv2, 2 * part + j + 1)
                        nc.gpsimd.tensor_tensor(fpow[o][:, a:b], fpow[i][:, a:b], halves[:, e, a:b],
                                                ALU.pow).then_inc(pp2, 1)
                for t in range(T):
                    pool.wait_ge(sim_ready, t + 1)
                    for h in range(PH):
                        k = t * PH + h
                        if k >= 3:
                            pool.wait_ge(picked_ready, k - 2)
                        nc.gpsimd.tensor_tensor(grid[k % 3].rearrange("p (i j) -> p i j", i=PK),
                                                sim[:, t, h, :].unsqueeze(2).to_broadcast([P, PK, PK]),
                                                sim[:, t, PH + h, :].unsqueeze(1).to_broadcast([P, PK, PK]),
                                                ALU.add).then_inc(grid_ready, 1)

            run(*RUNS[0])
            ffn()
            run(*RUNS[1])
            peer()

        @block.scalar
        def _(act):
            link = chain(act, act_step)

            def copy(o, i, s):
                nc.scalar.activation(o, i, ACT.Copy).then_inc(s, 1)

            def evac_x(n):
                act.wait_ge(xt_ps, n + 1)
                if n >= 2:
                    act.wait_ge(v_ps, n - 1)
                copy(xn_t[n % 2][:, :], bank(4, 0, S), xt_ready)

            def evac_qkv(n):
                act.wait_ge(qk_ps, n + 1)
                if n >= B + 2:
                    act.wait_ge(parts_ready, n - B - 1)
                elif n >= 2:
                    act.wait_ge(dd_ps, min(n - 1, B))
                scale = float(D) ** -0.25 if stage(n) == 0 else 1.0
                nc.scalar.activation(qk_f[n % 2][:, :, :], bank(5).rearrange("p (w n) -> p w n", w=2),
                                     ACT.Copy, scale=scale).then_inc(qk_ready, 1)
                act.wait_ge(v_ps, n + 1)
                act.wait_ge(consts, 1)
                if n >= 4:
                    act.wait_ge(pv_ps, (n - 3) if n - 4 < B else B + (n - 3 - B) * H)
                copy(vaug[n % 4][:, :, :, 0:D],
                     bank(4, S, 2 * S).rearrange("p (s h d) -> p s h d", s=SUB, h=H), v_ready)

            def evac_ot(n):
                act.wait_ge(ot_ps, n + 1)
                if n >= 1:
                    act.wait_ge(y_ps, n)
                copy(o_t[:, :], bank(4, 0, S), ot_ready)

            def evac_o(n):
                act.wait_ge(pv_ps, B + (n - B + 1) * H)
                if n > B:
                    act.wait_ge(or_ps, n - B)
                copy(o_sb[:, :, :], psum[:, 6 * BANK:8 * BANK].rearrange("p (g n) -> p g n", n=S), osb_ready)

            def evac_mt(n):
                act.wait_ge(mt_ps, n - B + 1)
                if n - 2 >= B:
                    act.wait_ge(max_in[(n - 2) % 3], 16 * placed(n - 2))
                copy(mt[n % 2][:, :], mt_bank, mt_ready)

            def exps(n, h):
                act.wait_ge(cols_ps, (n - B) * H + h + 1)
                k = (n - B) * H + h
                if k >= 4:
                    act.wait_ge(pv_ps, B + k - 3)
                w = SUB * S - P if stage(n) == 2 else SUB * S
                nc.scalar.activation(probs[k % 4][:, 0:w], bank(2 + k % 2, 0, w), ACT.Exp, scale=float(D) ** -0.5).then_inc(probs_ready, 1)

            act.wait_ge(consts, 1)
            for half in range(2):
                act.wait_ge(ctxt_ps, half + 1)
                copy(ctx_t[:, half * BANK:(half + 1) * BANK], bank(half), ctxt_ready)
            evac_x(0)
            evac_qkv(0)
            for n in range(B):
                if n + 1 < B:
                    evac_x(n + 1)
                    evac_qkv(n + 1)
                act.wait_ge(zq_ready, n + 1)
                if n >= 1:
                    act.wait_ge(qft_ps, n)
                nc.scalar.activation(eq, zq, ACT.Exp).then_inc(eq_ready, 1)
            act.wait_ge(nkmax_ready, 1)
            for n in range(B):
                if n >= 2:
                    act.wait_ge(cx_ps, n - 1)
                nc.scalar.activation(kf[n % 2], zk[:, SUB * n:SUB * n + SUB, :], ACT.Exp,
                                     bias=nkmax[:, 0:1]).then_inc(ke_ready, 1)
                if n >= 1:
                    evac_ot(n - 1)
            evac_ot(B - 1)

            def run(first, last):
                for n in (first, first + 1):
                    evac_x(n)
                    evac_qkv(n)
                evac_mt(first)
                for n in range(first, last + 1):
                    if n > first:
                        evac_o(n - 1)
                    if n + 2 <= last:
                        evac_x(n + 2)
                        evac_qkv(n + 2)
                    for h in range(H):
                        exps(n, h)
                        if h == TURN and n + 1 <= last:
                            evac_mt(n + 1)
                        if h == 8 and n > first:
                            evac_ot(n - 1)
                evac_o(last)
                evac_ot(last)

            def ffn():
                def keep(g):
                    b, s, f = ORDER[g]
                    act.wait_ge(leaf_done, g + 1)
                    copy(fval[b % 2][:, s, :] if f == 2 else fqk_t[b % 2][:, f, s * P:s * P + P],
                         bank(6 + g % 2, 0, P), leaf_kept)

                def turn(b):
                    act.wait_ge(fxt_ps, b + 1)
                    copy(fx_t[:, :], bank(4, 0, S), fxt_ready)

                kept = 0
                turn(0)
                for what, i in STAGES:
                    if what == "turn":
                        turn(i)
                    elif what == "leaf":
                        act.wait_ge(fh_ready, i + 1)
                        nc.scalar.activation(hact[i % 2][:, :], hid[i % 4][:, :],
                                             ACT.Gelu if last_tree(i) else ACT.Relu).then_inc(fg_ready, 1)
                        act.wait_ge(fg_ready, i + 1)
                        for l in range(LW):
                            if l == LW // 2 and kept < i:
                                if not last_tree(i - 1):
                                    keep(i - 1)
                                kept = i
                            w = leaf_rows[i % 4][:, LW * E + LW + l * E:LW * E + LW + (l + 1) * E]
                            a = nc.scalar.activation(w, w, ACT.Copy, scale=hact[i % 2][:, l:l + 1])
                            if l % 4 == 3:
                                a.then_inc(scaled, 1)
                    elif what == "score":
                        g = ORDER.index((i, SUB - 1, 2))
                        if kept == g:
                            keep(g)
                            kept = g + 1
                    elif what == "weigh":
                        act.wait_ge(fmax_ready, i + 1)
                        for s in range(SUB):
                            nc.scalar.activation(att[:, s, :], bank(5, s * S, s * S + S), ACT.Exp, bias=fneg[:, s:s + 1],
                                                 scale=float(E) ** -0.5, accum_out=fsum[:, s:s + 1]).then_inc(att_ready, 1)
                    elif what == "mix":
                        act.wait_ge(at_ps, i + 1)
                        copy(att_t[:, :, :], bank(5).rearrange("p (c n) -> p c n", c=4), at_ready)
                    elif what == "turn_f":
                        act.wait_ge(fyt_ps, i + 1)
                        copy(fy_t[:, :], bank(4, 0, S), fyt_ready)

            def peer():
                def turned(i):
                    act.wait_ge(pxt_ps, i + 1)
                    copy(px_t[i], bank(4 + 3 * i), pxt_ready)

                def sims(t):
                    act.wait_ge(sim_ps, t + 1)
                    copy(sim[:, t, :, :], bank(5 + t % SUB).rearrange("p (g k) -> p g k", k=PK), sim_ready)

                turned(0)
                for u in range(UNITS):
                    b, c = u // 2 % B, u % 2 * 4
                    act.wait_ge(unit_ps, u + 1)
                    src = unit_bank(u).rearrange("p (c n) -> p c n", c=4)
                    if u < 2 * B:
                        copy(qp_t[b % 2][:, c:c + 4, :], src, unit_ready)
                    else:
                        nc.scalar.activation(hg[:, c:c + 4, b * S:(b + 1) * S], src, ACT.Gelu).then_inc(unit_ready, 1)
                    if u == 1:
                        turned(1)
                    if 2 <= u < T + 2:
                        sims(u - 2)

                def top_exp(t):
                    act.wait_ge(tdif_ready, t + 1)
                    nc.scalar.activation(texp[t], texp[t], ACT.Exp).then_inc(texp_ready, 1)

                def diagonals(t):
                    act.wait_ge(trec_ready, t + 1)
                    if t >= 2:
                        act.wait_ge(mix_ps, (t - 1) * PH)
                    for h in range(PH):
                        i = nc.scalar.activation(diag[t % 2][:, h, :], identf[:, :], ACT.Copy,
                                                 scale=trec[t % 2][:, h:h + 1])
                    i.then_inc(diag_ready, 1)

                top_exp(0)
                for t in range(T):
                    for h in range(PH):
                        k = t * PH + h
                        act.wait_ge(grid_ready, k + 1)
                        if k >= 2:
                            act.wait_ge(picked_ready, k - 1)
                        nc.scalar.activation(psum[:, (4 + 2 * (k % 2)) * BANK:(6 + 2 * (k % 2)) * BANK], grid[k % 3],
                                             ACT.Exp, bias=tneg[:, t, h:h + 1]).then_inc(e_ready, 1)
                        if k == 0:
                            diagonals(0)
                        if h == 1 and t + 1 < T:
                            top_exp(t + 1)
                        if h == 6 and t + 1 < T:
                            diagonals(t + 1)

            run(*RUNS[0])
            ffn()
            run(*RUNS[1])
            peer()

        @block.vector
        def _(dve):
            link = chain(dve, dve_step)

            def norm(n):
                b = batch(n)
                if n < B:
                    dve.wait_ge(in_x, 16)
                elif stage(n) == 2:
                    dve.wait_ge(leaf_added, SUB * (b + 1))
                else:
                    dve.wait_ge(x_ready, n - B + 1)
                for s in range(SUB):
                    link(nc.vector.bn_stats(stats[:, s, :], x[:, SUB * b + s, :]))
                    link(nc.vector.bn_aggr(mv[:, s, :], stats[:, s, :]))
                if n >= 1:
                    dve.wait_ge(rstd_ready, n)
                nc.vector.tensor_scalar(var_e[:, :], mv[:, :, 1], 1e-5, None, ALU.add).then_inc(var_ready, 1)
                dve.wait_ge(rstd_ready, n + 1)
                if n >= 3:
                    dve.wait_ge(xt_ps, n - 2)
                for s in range(SUB):
                    i = nc.vector.tensor_scalar(xn[n % 3][:, s, :], x[:, SUB * b + s, :], mv[:, s, 0:1],
                                                rstd[:, s:s + 1], ALU.subtract, ALU.mult)
                i.then_inc(xn_ready, 1)
                dve.wait_ge(xn_ready, n + 1)

            def onorm_rf(n):
                dve.wait_ge(pv_ps, n + 1)
                o4 = bank(7, 0, 288).rearrange("p (g c) -> p g c", c=D + 1)
                rs = rsum[:, :, :].rearrange("p s h -> p (s h)").unsqueeze(2)
                link(nc.vector.reciprocal(rs, o4[:, :, D:D + 1]))
                if n >= 1:
                    dve.wait_ge(ot_ps, n)
                nc.vector.tensor_tensor(o_n[:, :, :].rearrange("p s (h d) -> p (s h) d", d=D), o4[:, :, 0:D],
                                        rs.to_broadcast([P, SUB * H, D]), ALU.mult).then_inc(o_ready, 1)

            def onorm(n):
                dve.wait_ge(or_ps, n - B + 1)
                dve.wait_ge(ot_ps, n)
                for s in range(SUB):
                    o4 = bank(5 - s).rearrange("p (h c) -> p h c", c=VW)
                    link(nc.vector.reciprocal(rsum[:, s, :].unsqueeze(2), o4[:, :, D:D + 1]))
                    i = nc.vector.tensor_tensor(o_n[:, s, :].rearrange("p (h d) -> p h d", d=D), o4[:, :, 0:D],
                                                rsum[:, s, :].unsqueeze(2).to_broadcast([P, H, D]), ALU.mult)
                i.then_inc(o_ready, 1)

            def resid(n):
                b = batch(n)
                dve.wait_ge(y_ps, n + 1)
                nc.vector.tensor_tensor(x[:, SUB * b:SUB * b + SUB, :],
                                        bank(5, 0, S).rearrange("p (s e) -> p s e", s=SUB),
                                        x[:, SUB * b:SUB * b + SUB, :], ALU.add).then_inc(x_ready, 1)

            def row_max(n, h):
                k = (n - B) * H + h
                dve.wait_ge(rows_ps, k + 1)
                if stage(n) == 2:
                    nc.vector.tensor_reduce(rowmax[n % 2][:, 0, h:h + 1], bank(k % 2, 0, P), AX.X, ALU.max)
                    i = nc.vector.tensor_reduce(rowmax[n % 2][:, 1, h:h + 1], bank(k % 2, P, P + S), AX.X, ALU.max)
                else:
                    i = nc.vector.tensor_reduce(rowmax[n % 2][:, :, h], bank(k % 2).rearrange("p (s n) -> p s n", s=SUB),
                                                AX.X, ALU.max)
                i.then_inc(rows_max, 1)

            def max_parts(n):
                dve.wait_ge(rows_max, (n - B + 1) * H)
                if n - 2 >= B:
                    dve.wait_ge(mt_ps, n - 1 - B)
                mp = mparts[n % 2]
                link(nc.vector.tensor_scalar(negmax[:, :, :], rowmax[n % 2][:, :, :], -1.0, None, ALU.mult))
                link(nc.vector.tensor_copy(mp[:, :, 0, :], negmax[:, :, :]))
                link(nc.vector.tensor_tensor(remax[:, :, :], negmax[:, :, :], mp[:, :, 0, :], ALU.subtract))
                link(nc.vector.tensor_copy(mp[:, :, 1, :], remax[:, :, :]))
                nc.vector.tensor_tensor(mp[:, :, 2, :], remax[:, :, :], mp[:, :, 1, :], ALU.subtract).then_inc(mparts_ready, 1)
                dve.wait_ge(mparts_ready, n - B + 1)

            dve.wait_ge(consts, 1)
            dve.wait_ge(in_w, 48)
            nc.vector.tensor_tensor(feat_w[:, :, :], head16[:, :].unsqueeze(2).to_broadcast([P, H, M]),
                                    projb[:, :].unsqueeze(1).to_broadcast([P, H, M]), ALU.mult).then_inc(feat_ready, 1)
            norm(0)
            split_bias(nc.vector, link, 0, 9 * P)
            nc.vector.tensor_copy(bias_w[:, 0:1], bias_p[:, 0:1]).then_inc(bias_ready, 1)
            for n in range(B):
                if n + 1 < B:
                    norm(n + 1)
                dve.wait_ge(dd_ps, n + 1)
                if n >= 1:
                    dve.wait_ge(eq_ready, n)
                ddq = psum[:, 0:2 * BANK].rearrange("p (g m) -> p g m", m=M)
                ddk = psum[:, 2 * BANK:4 * BANK].rearrange("p (g m) -> p g m", m=M)
                half_norm = bank(7, 0, 64).rearrange("p (w s h) -> p w (s h)", w=2, s=SUB)
                sv = stab[:, :, :].rearrange("p s h -> p (s h)")
                link(nc.vector.tensor_reduce(sv, ddq, AX.X, ALU.max))
                link(nc.vector.tensor_tensor(sv, half_norm[:, 0, :], sv, ALU.add))
                nc.vector.tensor_tensor(zq.rearrange("p (g m) -> p g m", m=M), ddq,
                                        sv.unsqueeze(2).to_broadcast([P, 2 * H, M]), ALU.subtract).then_inc(zq_ready, 1)
                nc.vector.tensor_reduce(kmax[:, SUB * n:SUB * n + SUB],
                                        psum[:, 2 * BANK:4 * BANK].rearrange("p (s c) -> p s c", s=SUB), AX.X, ALU.max)
                dve.wait_ge(zq_ready, n + 1)
                link(nc.vector.tensor_copy(sv, half_norm[:, 1, :]))
                nc.vector.tensor_tensor(zk[:, SUB * n:SUB * n + SUB, :].rearrange("p s (g m) -> p (s g) m", m=M), ddk,
                                        sv.unsqueeze(2).to_broadcast([P, 2 * H, M]), ALU.subtract).then_inc(zk_ready, 1)
                dve.wait_ge(zk_ready, n + 1)
                dve.wait_ge(qft_ps, n + 1)
                nc.vector.tensor_scalar(qf_t[:, SUB * n:SUB * n + SUB, :, :],
                                        psum[:, 0:2 * BANK].rearrange("p (s g n) -> p s g n", s=SUB, g=HG),
                                        1e-4, None, ALU.add).then_inc(qft_ready, 1)
            link(nc.vector.tensor_reduce(kmax1[:, :], kmax[:, :], AX.X, ALU.max))
            nc.vector.tensor_copy(kmax1[:, :], kmax1[:, :]).then_inc(kmax_ready, 1)
            dve.wait_ge(in_ctx, 48)
            nc.vector.tensor_scalar(maskrow[:, :], mask_i, 0.0, None, ALU.not_equal).then_inc(mask_ready, 1)
            dve.wait_ge(kmax_all, 1)
            nc.vector.tensor_scalar(nkmax[:, :], kmaxg[:, :], -1.0, None, ALU.mult).then_inc(nkmax_ready, 1)

            def key_features(n):
                dve.wait_ge(ke_ready, n + 1)
                nc.vector.tensor_scalar(kf[n % 2], kf[n % 2], 1e-4, None, ALU.add).then_inc(kf_ready, 1)

            def own_blocks(n):
                dve.wait_ge(cx_ps, n + 1)
                nc.vector.tensor_tensor(ctx_m[:, :, :], bank(3, 0, 144).rearrange("p (g c) -> p g c", g=HG),
                                        blockm[:, :, :].rearrange("p g c -> p (g c)").unsqueeze(1).to_broadcast([P, HG, 36]),
                                        ALU.mult).then_inc(cx_ready, 1)

            key_features(0)
            own_blocks(0)
            for n in range(B):
                if n + 1 < B:
                    key_features(n + 1)
                onorm_rf(n)
                if n >= 1:
                    resid(n - 1)
                if n + 1 < B:
                    own_blocks(n + 1)
            resid(B - 1)

            def run(first, last):
                for n in range(first, first + 3):
                    norm(n)
                if first == B:
                    dve.wait_ge(in_tab, 32)
                    split_bias(nc.vector, link, 9 * P, NB)
                    nc.vector.tensor_copy(bias_w[:, 0:1], bias_p[:, 0:1]).then_inc(bias_ready, 1)
                for h in range(H):
                    row_max(first, h)
                max_parts(first)
                for n in range(first, last + 1):
                    for h in range(H):
                        if n + 1 <= last:
                            for hh in ROWS_AT[h]:
                                row_max(n + 1, hh)
                        if n > first and h == 5:
                            onorm(n - 1)
                        if n > first and h == 11:
                            resid(n - 1)
                        if n + 1 <= last and h == TURN - 2:
                            max_parts(n + 1)
                        if h == 13 and n + 3 <= last:
                            norm(n + 3)
                if first == B:
                    ffn_norm(0, 0, 2 * SUB)
                else:
                    peer_norm(0, 0, 2 * SUB)
                onorm(last)
                resid(last)

            def moments(src, a, b):
                for t in range(a, b):
                    i = nc.vector.bn_stats(fstats[:, t, :], src[:, t, :])
                link(i)
                for t in range(a, b):
                    i = nc.vector.bn_aggr(fmean[:, t, :], fstats[:, t, :])
                link(i)

            def scale(src, r, a, b):
                for t in range(a, b):
                    i = nc.vector.tensor_scalar(fx[:, t, :], src[:, t, :], fmean[:, t, 0:1], r[:, t:t + 1],
                                                ALU.subtract, ALU.mult)
                return i

            def ffn_norm(part, a, b):
                moments(x, a, b)
                nc.vector.tensor_scalar(fpow[0][:, a:b], fmean[:, a:b, 1], 1e-5, None, ALU.add).then_inc(fv, 1)
                dve.wait_ge(fp, 3 * part + 1)
                link(scale(x, fpow[1], a, b))
                moments(fx, a, b)
                nc.vector.tensor_scalar(fpow[0][:, a:b], fmean[:, a:b, 1], float(E) / (E - 1), None,
                                        ALU.mult).then_inc(fv, 1)
                dve.wait_ge(fp, 3 * part + 2)
                nc.vector.tensor_scalar(fpow[2][:, a:b], fpow[2][:, a:b], 1e-5, None, ALU.add).then_inc(fv, 1)
                dve.wait_ge(fp, 3 * part + 3)
                scale(fx, fpow[3], a, b).then_inc(fx_ready, 1)
                dve.wait_ge(fx_ready, part + 1)

            def route(n, k, numbers, decided, ready):
                d, v = dec[:, 0:n, :], walk[:, 0:n, :]
                logits = psum[:, k * BANK:k * BANK + n * S].rearrange("p (f n) -> p f n", f=n)
                half = LEAVES // 2
                nc.vector.tensor_scalar(d[:, :, 0:half - 1], logits[:, :, 0:half - 1], 0.0, None, ALU.is_gt)
                nc.vector.scalar_tensor_tensor(out=v, in0=logits[:, :, half - 1:NODES], scalar=0.0,
                                               in1=even_ids[:, :].unsqueeze(1).to_broadcast([P, n, half]),
                                               op0=ALU.is_gt, op1=ALU.add).then_inc(*decided[0:2])
                dve.wait_ge(decided[0], decided[2])
                for level in reversed(range(DEPTH - 1)):
                    st = 2 ** (DEPTH - 1 - level)
                    link(nc.vector.copy_predicated(v[:, :, 0:half:st], d[:, :, 2 ** level - 1:2 ** (level + 1) - 1],
                                                   v[:, :, st // 2:half:st]))
                nc.vector.tensor_copy(numbers, v[:, :, 0]).then_inc(*ready[0:2])
                dve.wait_ge(ready[0], ready[2])

            def hidden(g):
                b, s, f = ORDER[g]
                src = fy[b % 2][:, s, :] if f == 3 else fx[:, SUB * b + s, :]
                dve.wait_ge(rows_in[g % 4], 16 * (g // 4 + 1))
                if g >= 4:
                    dve.wait_ge(fg_ready, g - 3)
                r = leaf_rows[g % 4]
                for l in range(LW):
                    w = r[:, l * E:(l + 1) * E]
                    i = nc.vector.tensor_tensor_reduce(w, w, src, 1.0, r[:, LW * E + l:LW * E + l + 1], ALU.mult, ALU.add,
                                                       hid[g % 4][:, l:l + 1])
                i.then_inc(fh_ready, 1)

            def add_leaf(g):
                b, s, f = ORDER[g]
                dve.wait_ge(leaf_done, g + 1)
                xb = x[:, SUB * b + s, :]
                nc.vector.tensor_tensor(xb, xb, bank(6 + g % 2, 0, P), ALU.add).then_inc(leaf_added, 1)

            def score_max(b):
                dve.wait_ge(fs_ps, b + 1)
                link(nc.vector.tensor_reduce(frow[:, :], bank(5).rearrange("p (s n) -> p s n", s=SUB), AX.X, ALU.max))
                nc.vector.tensor_scalar(fneg[:, :], frow[:, :], -float(E) ** -0.5, None, ALU.mult).then_inc(fmax_ready, 1)

            def attend(b):
                dve.wait_ge(att_ready, SUB * (b + 1))
                link(nc.vector.reciprocal(frec[:, :], fsum[:, :]))
                dve.wait_ge(fy_ps, b + 1)
                if b >= 2:
                    dve.wait_ge(leaf_done, ORDER.index((b - 2, SUB - 1, 3)) + 1)
                for s in range(SUB):
                    i = nc.vector.scalar_tensor_tensor(out=fy[b % 2][:, s, :], in0=bank(3, s * P, s * P + P),
                                                       scalar=frec[:, s:s + 1], in1=fx[:, SUB * b + s, :],
                                                       op0=ALU.mult, op1=ALU.add)
                i.then_inc(fy_ready, 1)
                dve.wait_ge(fy_ready, b + 1)

            def ffn():
                def walk_of(b):
                    dve.wait_ge(lg_ps, b + 1)
                    route(6, 0, leaf_no[b][:, :], (dec_ready, 1, b + 1), (idx_ready, 1, b + 1))

                walk_of(0)
                ffn_norm(1, 2 * SUB, T)
                for what, i in STAGES:
                    if what == "leaf":
                        hidden(i)
                        if i >= 2 and last_tree(i - 2):
                            add_leaf(i - 2)
                    elif what == "route":
                        walk_of(i)
                    elif what == "weigh":
                        score_max(i)
                    elif what == "attend":
                        attend(i)
                    elif what == "route_f":
                        dve.wait_ge(lgf_ps, i + 1)
                        route(2, 3, leaf_nof[i][:, :], (decf_ready, 1, i + 1), (idxf_ready, 1, i + 1))
                add_leaf(len(ORDER) - 2)
                add_leaf(len(ORDER) - 1)

            def peer_norm(part, a, b):
                moments(x, a, b)
                dve.wait_ge(in_keys, 320)
                nc.vector.tensor_scalar(fpow[0][:, a:b], fmean[:, a:b, 1], 1e-5, None, ALU.add).then_inc(pv2, 1)
                dve.wait_ge(pp2, 2 * part + 1)
                link(scale(x, fpow[1], a, b))
                moments(fx, a, b)
                m, q, n = fmean[:, a:b, 0], fpow[2][:, a:b], fpow[3][:, a:b]
                link(nc.vector.tensor_tensor(q, m, m, ALU.mult))
                link(nc.vector.tensor_tensor(q, q, fmean[:, a:b, 1], ALU.add))
                nc.vector.tensor_scalar(q, q, float(E), None, ALU.mult).then_inc(pv2, 1)
                dve.wait_ge(pp2, 2 * part + 2)
                link(nc.vector.tensor_scalar(n, n, 1e-12, None, ALU.max))
                link(nc.vector.reciprocal(n, n))
                link(nc.vector.tensor_scalar(n, n, float(E) ** 0.5, None, ALU.mult))
                for t in range(a, b):
                    i = nc.vector.scalar_tensor_tensor(out=fx[:, t, :], in0=fx[:, t, :], scalar=fpow[3][:, t:t + 1],
                                                       in1=gamma_sb[:, :], op0=ALU.mult, op1=ALU.mult)
                i.then_inc(px_ready, 1)
                dve.wait_ge(px_ready, part + 1)

            def topk_step(t, j):
                st = sim[:, t, :, :]
                tp = top[t]

                def best8(out, src, n):
                    for g in range(n):
                        i = nc.vector.max(out[g], src[g])
                    link(i)

                if j == 0:
                    dve.wait_ge(sim_ready, t + 1)
                    best8([best[:, g, 0:8] for g in range(16)], [st[:, g, :] for g in range(16)], 16)
                elif j == 1:
                    for g in range(16):
                        i = nc.vector.match_replace(simw[:, g, :], best[:, g, 0:8], st[:, g, :], -3e38)
                    link(i)
                elif j == 2:
                    best8([best[:, g, 8:16] for g in range(16)], [simw[:, g, :] for g in range(16)], 16)
                elif j == 3:
                    off = 0
                    for a in range(8):
                        n = NCAND[a]
                        nc.vector.tensor_tensor(pairs[:, :, off:off + n], best[:, 0:PH, a:a + 1].to_broadcast([P, PH, n]),
                                                best[:, PH:2 * PH, 0:n], ALU.add)
                        off += n
                    link(nc.vector.tensor_tensor(pairs[:, :, off:CAND], best[:, 0:PH, 8:TOPK],
                                                 best[:, PH:2 * PH, 0:1].to_broadcast([P, PH, 8]), ALU.add))
                elif j == 4:
                    best8([tp[:, g, 0:8] for g in range(PH)], [pairs[:, g, :] for g in range(PH)], PH)
                elif j == 5:
                    for g in range(PH):
                        i = nc.vector.match_replace(pairw[:, g, :], tp[:, g, 0:8], pairs[:, g, :], -3e38)
                    link(i)
                else:
                    best8([tp[:, g, 8:16] for g in range(PH)], [pairw[:, g, :] for g in range(PH)], PH)
                    link(nc.vector.tensor_scalar(tneg[:, t, :], tp[:, :, 0], -1.0, None, ALU.mult))
                    nc.vector.tensor_tensor(texp[t], tp, tp[:, :, 0:1].to_broadcast([P, PH, TOPK]),
                                            ALU.subtract).then_inc(tdif_ready, 1)

            def weight_sum(t):
                dve.wait_ge(texp_ready, t + 1)
                if t >= 2:
                    dve.wait_ge(diag_ready, t - 1)
                link(nc.vector.tensor_reduce(tsum[:, :], texp[t], AX.X, ALU.add))
                nc.vector.reciprocal(trec[t % 2][:, :], tsum[:, :]).then_inc(trec_ready, 1)

            def peer():
                dve.wait_ge(x_ready, 4 * B)
                peer_norm(1, 2 * SUB, T)
                for t in range(AHEAD):
                    for j in range(7):
                        topk_step(t, j)
                weight_sum(0)

                def mix(t):
                    dve.wait_ge(mix_ps, PH * (t + 1))
                    dve.wait_ge(unit_ready, UNITS)
                    if t >= 1:
                        dve.wait_ge(po_ps, t)
                    st = psum[:, (t % 2) * 2 * BANK:((t % 2) * 2 + 2) * BANK].rearrange("p (c n) -> p c n", c=8)
                    nc.vector.tensor_tensor(mixed, st, hg[:, :, t * P:t * P + P], ALU.mult).then_inc(mixed_ready, 1)

                def add(t):
                    dve.wait_ge(po_ps, t + 1)
                    nc.vector.tensor_tensor(x[:, t, :], bank((t % 2) * 2, 0, P), x[:, t, :], ALU.add).then_inc(tile_ready, 1)

                for t in range(T):
                    for h in range(PH):
                        k = t * PH + h
                        dve.wait_ge(e_ready, k + 1)
                        if k == 0:
                            dve.wait_ge(sim_ps, T)
                        if k >= 2:
                            dve.wait_ge(mix_ps, k - 1)
                        nc.vector.scalar_tensor_tensor(out=picked[k % 2], in0=grid[k % 3],
                                                       scalar=top[t][:, h, TOPK - 1:TOPK],
                                                       in1=psum[:, (4 + 2 * (k % 2)) * BANK:(6 + 2 * (k % 2)) * BANK],
                                                       op0=ALU.is_ge, op1=ALU.mult).then_inc(picked_ready, 1)
                        if t + AHEAD < T and h < 7:
                            topk_step(t + AHEAD, h)
                        if t + 1 < T and h == 3:
                            weight_sum(t + 1)
                        if t >= 1 and h == 1:
                            mix(t - 1)
                        if t >= 1 and h == 3:
                            add(t - 1)
                mix(T - 1)
                add(T - 1)

            run(*RUNS[0])
            ffn()
            run(*RUNS[1])
            peer()

        @block.tensor
        def _(pe):
            def bias_of(a, b):
                return bias_p[0:3, a:b]

            BIAS = {(0, 0): 0, (0, 1): 1, (0, 2): 2, (0, 3): 3, (1, 0): 4, (1, 1): 5, (1, 2): 6, (1, 3): 7, (3, 3): 8}

            def project(o, lhs, rhs, key, by_row):
                r = BIAS.get(key)
                i = nc.tensor.matmul(o, lhs, rhs, start=True, stop=r is None)
                if r is None:
                    return i
                bias = bias_of(r * P, r * P + P)
                if by_row:
                    return nc.tensor.matmul(o, bias, ones[0:3, :], start=False, stop=True)
                return nc.tensor.matmul(o, ones[0:3, 0:P], bias, start=False, stop=True)

            def pre(n):
                a, b = stage(n), batch(n)
                pe.wait_ge(xn_ready, n + 1)
                if n >= 1:
                    pe.wait_ge(v_ready, n)
                if tails_ahead(n):
                    pe.wait_ge(ot_ready, tails_ahead(n))
                for s in range(SUB):
                    i = nc.tensor.transpose(bank(4, s * P, s * P + P), xn[n % 3][:, s, :], identf[:, :])
                i.then_inc(xt_ps, 1)
                pe.wait_ge(xt_ready, n + 1)
                if n >= 1:
                    pe.wait_ge(qk_ready, n)
                if tails_ahead(n):
                    pe.wait_ge(x_ready, tails_ahead(n))
                if n >= B and turns_ahead(n) > 0:
                    pe.wait_ge(mt_ready, turns_ahead(n))
                own = xn_t[n % 2][:, :]
                kv = ctx_t[:, b * S:(b + 1) * S] if a in (1, 3) else own
                for w, src in ((0, own), (1, kv)):
                    i = project(bank(5, w * S, w * S + S), w_sb[:, 4 * a + w, :], src, (a, w), True)
                i.then_inc(qk_ps, 1)
                for s in range(SUB):
                    i = project(bank(4, S + s * P, S + s * P + P), kv[:, s * P:s * P + P], w_sb[:, 4 * a + 2, :],
                                (a, 2), False)
                i.then_inc(v_ps, 1)

            def turn_out(n):
                pe.wait_ge(osb_ready, n - B + 1)
                pe.wait_ge(x_ready, n)
                pe.wait_ge(v_ready, pres_ahead(n))
                pe.wait_ge(mt_ready, min(n + 2, run_of(n)[1] + 1) - B)
                pe.wait_ge(qk_ready, min(n + 4, run_of(n)[1] + 1))
                for s in range(SUB):
                    for g in range(H // 4):
                        i = nc.tensor.transpose(bank(5 - s, g * P, g * P + P), o_sb[:, g, s * P:s * P + P], identf[:, :])
                i.then_inc(or_ps, 1)

            def tail_a(n):
                pe.wait_ge(o_ready, n + 1)
                if n < B:
                    pe.wait_ge(v_ready, B)
                    if n >= 1:
                        pe.wait_ge(ot_ready, n)
                for s in range(SUB):
                    i = nc.tensor.transpose(bank(4, s * P, s * P + P), o_n[:, s, :], identf[:, :])
                i.then_inc(ot_ps, 1)

            def tail_b(n):
                pe.wait_ge(ot_ready, n + 1)
                if n >= 1:
                    pe.wait_ge(x_ready, n)
                for s in range(SUB):
                    i = project(bank(5, s * P, s * P + P), o_t[:, s * P:s * P + P], w_sb[:, 4 * stage(n) + 3, :],
                                (stage(n), 3), False)
                i.then_inc(y_ps, 1)

            def score_rows(n, h):
                k = (n - B) * H + h
                if h == 0:
                    pe.wait_ge(stk_ready[n % 3], 16 * 12 * placed(n))
                if k >= 2:
                    pe.wait_ge(rows_max, k - 1)
                t = stk[n % 3]
                q, kk = t[0:KS, h, 0, :], t[0:KS, h, 1, :]
                if stage(n) == 2:
                    nc.tensor.matmul(bank(k % 2, 0, P), q[:, 0:P], kk[:, 0:P], start=True, stop=False)
                    nc.tensor.matmul(bank(k % 2, 0, P), identb[:, :], causal_q[:, :], start=False, stop=True)
                    nc.tensor.matmul(bank(k % 2, P, P + S), q[:, P:S], kk, start=True, stop=False)
                    i = nc.tensor.matmul(bank(k % 2, S, S + P), identb[:, :], causal_q[:, :], start=False, stop=True)
                else:
                    for s in range(SUB):
                        i = nc.tensor.matmul(bank(k % 2, s * S, s * S + S), q[:, s * P:s * P + P], kk, start=True, stop=True)
                i.then_inc(rows_ps, 1)

            def score_cols(n, h):
                k = (n - B) * H + h
                if h == 0:
                    pe.wait_ge(max_in[n % 3], 16 * placed(n))
                if k >= 2:
                    pe.wait_ge(probs_ready, k - 1)
                t = stk[n % 3]
                q, kk = t[0:KM, h, 0, :], t[0:KM, h, 1, :]
                causal = stage(n) == 2
                for c in range(SUB):
                    q0 = P if causal and c else 0
                    o = bank(2 + k % 2, c * S, c * S + S - q0)
                    i = nc.tensor.matmul(o, kk[:, c * P:c * P + P], q[:, q0:S], start=True, stop=not causal)
                    if causal:
                        i = nc.tensor.matmul(o[:, 0:P], identb[:, :], causal_k[:, :], start=False, stop=True)
                i.then_inc(cols_ps, 1)

            def values(n, h):
                k = (n - B) * H + h
                pe.wait_ge(probs_ready, k + 1)
                if h == 0:
                    pe.wait_ge(v_ready, n + 1)
                    if n > B:
                        pe.wait_ge(osb_ready, n - B)
                r, col = 32 * (h % 4), (h // 4) * S
                for c in range(SUB):
                    q0 = P if stage(n) == 2 and c else 0
                    o = psum[r:r + VW, 6 * BANK + col + q0:6 * BANK + col + S]
                    i = nc.tensor.matmul(o, vaug[n % 4][:, c, h, :], probs[k % 4][:, c * S:c * S + S - q0],
                                         start=(c == 0), stop=(c == SUB - 1))
                i.then_inc(pv_ps, 1)

            def max_turn(n):
                pe.wait_ge(mparts_ready, n - B + 1)
                first, last = run_of(n)
                pe.wait_ge(qk_ready, min(n + 2, last + 1))
                pe.wait_ge(x_ready, max(n - 1, first))
                for s in range(SUB):
                    i = nc.tensor.transpose(mt_bank[:, s * P:s * P + P],
                                            mparts[n % 2][:, s, :, :].rearrange("p a h -> p (a h)"), identb[:, :])
                i.then_inc(mt_ps, 1)

            pe.wait_ge(consts, 1)
            pe.wait_ge(in_ctx, 48)
            for t in range(T):
                i = nc.tensor.transpose(psum[:, t * P:t * P + P], ctx_rows[:, t, :], identf[:, :])
                if t % 4 == 3:
                    i.then_inc(ctxt_ps, 1)
            pe.wait_ge(in_w, 48)
            pe.wait_ge(feat_ready, 1)
            pe.wait_ge(bias_ready, 1)
            pre(0)
            for n in range(B):
                if n >= 1:
                    pe.wait_ge(qft_ready, n)
                    pe.wait_ge(zk_ready, n)
                else:
                    pe.wait_ge(ctxt_ready, 2)
                pe.wait_ge(qk_ready, n + 1)
                fw = feat_w[:, :, :].rearrange("p h m -> p (h m)")
                for w in range(2):
                    for s in range(SUB):
                        nc.tensor.matmul(bank(2 * w + s), qk_f[n % 2][:, w, s * P:s * P + P], fw, start=True, stop=True)
                pe.wait_ge(sq_ready, n + 1)
                for w in range(2):
                    for s in range(SUB):
                        j = (w * SUB + s) * H
                        i = nc.tensor.matmul(bank(7, j, j + H), sq[:, w, s * P:s * P + P], half16[:, :], start=True, stop=True)
                i.then_inc(dd_ps, 1)
                if n + 1 < B:
                    pre(n + 1)
                pe.wait_ge(eq_ready, n + 1)
                for s in range(SUB):
                    for g in range(HG):
                        j = (s * HG + g) * P
                        i = nc.tensor.transpose(psum[:, j:j + P], eq[:, j:j + P], identf[:, :])
                i.then_inc(qft_ps, 1)

            def keys_values(n):
                pe.wait_ge(kf_ready, n + 1)
                if n == 0:
                    pe.wait_ge(zk_ready, B)
                    pe.wait_ge(qft_ready, B)
                    pe.wait_ge(v_ready, B)
                else:
                    pe.wait_ge(cx_ready, n)
                for g in range(HG):
                    for s in range(SUB):
                        i = nc.tensor.matmul(bank(3, g * 36, g * 36 + 36), kf[n % 2][:, s, g * P:g * P + P],
                                             vaug[n % 4][:, s, g * HG:g * HG + HG, 0:D + 1],
                                             start=(s == 0), stop=(s == SUB - 1))
                i.then_inc(cx_ps, 1)

            keys_values(0)
            for n in range(B):
                pe.wait_ge(cx_ready, n + 1)
                if n >= 1:
                    pe.wait_ge(o_ready, n)
                for s in range(SUB):
                    for g in range(HG):
                        i = nc.tensor.matmul(bank_o(s, g * HG, HG), qf_t[:, SUB * n + s, g, :], ctx_m[:, g, :],
                                             start=True, stop=True)
                i.then_inc(pv_ps, 1)
                if n >= 1:
                    tail_b(n - 1)
                if n + 1 < B:
                    keys_values(n + 1)
                tail_a(n)
            tail_b(B - 1)

            def run(first, last):
                pre(first)
                pre(first + 1)
                for h in range(H):
                    score_rows(first, h)
                max_turn(first)
                for n in range(first, last + 1):
                    if n > first:
                        values(n - 1, H - 2)
                        values(n - 1, H - 1)
                    if n + 2 <= last:
                        pre(n + 2)
                    for h in range(H):
                        score_cols(n, h)
                        if n + 1 <= last:
                            for hh in ROWS_AT[h]:
                                score_rows(n + 1, hh)
                            if h == TURN:
                                max_turn(n + 1)
                        if h >= 2:
                            values(n, h - 2)
                        if n > first and h == 3:
                            turn_out(n - 1)
                        if n > first and h == 6:
                            tail_a(n - 1)
                        if n > first and h == 9:
                            tail_b(n - 1)
                values(last, H - 2)
                values(last, H - 1)
                turn_out(last)
                tail_a(last)
                tail_b(last)

            def logits(s, f, src, o):
                o = o[:, 0:NODES]
                nc.tensor.matmul(o, src[:, s * P:s * P + P], nodes_sb[:, f, :], start=True, stop=False)
                n0 = 9 * P + f * NODES
                return nc.tensor.matmul(o, ones[0:3, 0:P], bias_of(n0, n0 + NODES), start=False, stop=True)

            def ffn():
                pe.wait_ge(in_tab, 32)
                pe.wait_ge(bias_ready, 2)
                pe.wait_ge(ot_ready, 2 * B)

                def turn(b):
                    pe.wait_ge(fx_ready, b // 2 + 1)
                    if b >= 1:
                        pe.wait_ge(dec_ready, b)
                    if b >= 3:
                        pe.wait_ge(fyt_ready, b - 2)
                    for s in range(SUB):
                        i = nc.tensor.transpose(bank(4, s * P, s * P + P), fx[:, SUB * b + s, :], identf[:, :])
                    i.then_inc(fxt_ps, 1)
                    pe.wait_ge(fxt_ready, b + 1)
                    for f in range(3):
                        for s in range(SUB):
                            i = logits(s, f, fx_t, bank(f, s * S, s * S + S))
                    i.then_inc(lg_ps, 1)

                def leaf(g):
                    b, s, f = ORDER[g]
                    r = leaf_rows[g % 4]
                    o = bank(6 + g % 2, 0, P)
                    if g >= 2:
                        last = last_tree(g - 2)
                        pe.wait_ge(leaf_added if last else leaf_kept, leaves_upto(g - 2, last))
                    for l in range(LW + 1):
                        if l < LW and l % 4 == 0:
                            pe.wait_ge(scaled, 4 * g + l // 4 + 1)
                        w = r[:, LW * E + LW + l * E:LW * E + LW + (l + 1) * E]
                        ab = (w, identf[:, :]) if f < 2 else (identf[:, :], w)
                        i = nc.tensor.matmul(o, *ab, start=(l == 0), stop=(l == LW and f < 3))
                    if f == 3:
                        i = nc.tensor.matmul(o, identf[:, :], fy[b % 2][:, s, :], start=False, stop=True)
                    i.then_inc(leaf_done, 1)

                turn(0)
                for what, b in STAGES:
                    if what == "turn":
                        turn(b)
                    elif what == "leaf":
                        leaf(b)
                    elif what == "score":
                        pe.wait_ge(leaf_kept, 3 * SUB * (b + 1))
                        if b >= 1:
                            pe.wait_ge(at_ready, b)
                        t = fqk_t[b % 2]
                        for s in range(SUB):
                            i = nc.tensor.matmul(bank(5, s * S, s * S + S), t[:, 0, s * P:s * P + P], t[:, 1, :],
                                                 start=True, stop=True)
                        i.then_inc(fs_ps, 1)
                    elif what == "mix":
                        pe.wait_ge(att_ready, SUB * (b + 1))
                        for s in range(SUB):
                            for c in range(SUB):
                                j = (s * SUB + c) * P
                                i = nc.tensor.transpose(bank(5, j, j + P), att[:, s, c * P:c * P + P], identf[:, :])
                        i.then_inc(at_ps, 1)
                        pe.wait_ge(at_ready, b + 1)
                        if b >= 1:
                            pe.wait_ge(decf_ready, b)
                        for s in range(SUB):
                            for c in range(SUB):
                                i = nc.tensor.matmul(bank(3, s * P, s * P + P), att_t[:, s * SUB + c, :],
                                                     fval[b % 2][:, c, :], start=(c == 0), stop=(c == SUB - 1))
                        i.then_inc(fy_ps, 1)
                    elif what == "turn_f":
                        pe.wait_ge(fy_ready, b + 1)
                        if b + 2 < B:
                            pe.wait_ge(fxt_ready, b + 3)
                        for s in range(SUB):
                            i = nc.tensor.transpose(bank(4, s * P, s * P + P), fy[b % 2][:, s, :], identf[:, :])
                        i.then_inc(fyt_ps, 1)
                        pe.wait_ge(fyt_ready, b + 1)
                        for s in range(SUB):
                            i = logits(s, 3, fy_t, bank(3, s * S, s * S + S))
                        i.then_inc(lgf_ps, 1)

            def peer():
                pe.wait_ge(in_keys, 320)
                pe.wait_ge(ot_ready, 4 * B)

                def turn(i):
                    pe.wait_ge(px_ready, i + 1)
                    for t in range(2 * SUB):
                        j = nc.tensor.transpose(bank(4 + 3 * i, t * P, t * P + P), fx[:, 2 * SUB * i + t, :], identf[:, :])
                    j.then_inc(pxt_ps, 1)

                def sims(t):
                    b, s = t // SUB, t % SUB
                    pe.wait_ge(unit_ready, 2 * b + 2)
                    if b >= 1:
                        pe.wait_ge(sim_ready, t - SUB + 1)
                    for c in range(8):
                        i = nc.tensor.matmul(bank(5 + s, c * 2 * PK, (c + 1) * 2 * PK),
                                             qp_t[b % 2][:, c, s * P:s * P + P], keys_sb[:, c, :], start=True, stop=True)
                    i.then_inc(sim_ps, 1)

                turn(0)
                for u in range(UNITS):
                    b = u // 2 % B
                    pe.wait_ge(pxt_ready, b // 2 + 1)
                    if u >= 2:
                        pe.wait_ge(unit_ready, u - 1)
                    w = wq_sb if u < 2 * B else down_sb
                    for c in range(4):
                        cc = u % 2 * 4 + c
                        i = nc.tensor.matmul(unit_bank(u)[:, c * S:(c + 1) * S], w[:, cc * P:cc * P + P], px_of(b),
                                             start=True, stop=True)
                    i.then_inc(unit_ps, 1)
                    if u == 1:
                        turn(1)
                    if 2 <= u < T + 2:
                        sims(u - 2)
                pe.wait_ge(unit_ready, UNITS)

                def out_of(t):
                    pe.wait_ge(mixed_ready, t + 1)
                    for c in range(8):
                        i = nc.tensor.matmul(bank((t % 2) * 2, 0, P), mixed[:, c, :], up_sb[:, c, :],
                                             start=(c == 0), stop=(c == 7))
                    i.then_inc(po_ps, 1)

                for t in range(T):
                    pe.wait_ge(diag_ready, t + 1)
                    if t >= 2:
                        pe.wait_ge(tile_ready, t - 1)
                    for h in range(PH):
                        k = t * PH + h
                        pe.wait_ge(picked_ready, k + 1)
                        for c in range(8):
                            o = ((t % 2) * 2) * BANK + c * P
                            i = nc.tensor.matmul(psum[:, o:o + P], picked[k % 2][:, c * P:c * P + P], diag[t % 2][:, h, :],
                                                 start=(h == 0 and c % 4 == 0), stop=(h == PH - 1),
                                                 skip_group_check=True)
                        i.then_inc(mix_ps, 1)
                        if t >= 1 and h == 2:
                            out_of(t - 1)
                out_of(T - 1)

            pe.wait_ge(consts, 2)
            run(*RUNS[0])
            ffn()
            run(*RUNS[1])
            peer()


def kernel(**a):
    import numpy as np
    import concourse.bacc as bacc
    from concourse.bass_utils import run_bass_kernel_spmd

    a = {k: np.asarray(v) for k, v in a.items()}

    def by_width(w):
        return w.reshape(w.shape[:-1] + (H, D)).swapaxes(-1, -2).reshape(w.shape)

    ws = []
    for names in (("L0_attn_Wq", "L0_attn_Wk", "L0_attn_Wv", "L0_attn_Wo"),
                  ("L0_xattn_wq", "L0_xattn_wk", "L0_xattn_wv", "L0_xattn_wo"),
                  ("L1_attn_Wq", "L1_attn_Wk", "L1_attn_Wv", "L1_attn_Wo"),
                  ("L1_xattn_Wq", "L1_xattn_Wk", "L1_xattn_Wv", "L1_xattn_Wo")):
        q, k, v, o = (a[n].T for n in names)
        ws += [by_width(q), by_width(k), v, o]
    bias = [by_width(a["L0_attn_bq"]), by_width(a["L0_attn_bk"]), a["L0_attn_bv"], a["L0_attn_bo"],
            by_width(a["L0_xattn_bq"]), by_width(a["L0_xattn_bk"]), a["L0_xattn_bv"], a["L0_xattn_bo"],
            a["L1_xattn_bo"]]
    kinds = "qkvf"

    def leaves(c):
        w1, w2 = a[f"L0_ffn_{c}_w1"], a[f"L0_ffn_{c}_w2"]
        return np.concatenate([w1.transpose(0, 2, 1).reshape(LEAVES, LW * E), a[f"L0_ffn_{c}_b1"],
                               w2.reshape(LEAVES, LW * E), a[f"L0_ffn_{c}_b2"]], axis=1)

    ins = {
        "x_in": a["x"], "ctx_in": a["ctx_1024"], "mask_in": a["mask_BxS_ik0"],
        "attn_w": np.stack(ws), "attn_bias": np.concatenate(bias),
        "proj_t": np.repeat(a["L0_attn_proj"].T, H, axis=0),
        "node_w": np.stack([a[f"L0_ffn_{c}_nw"].T for c in kinds], axis=1),
        "node_b": np.concatenate([a[f"L0_ffn_{c}_nb"] for c in kinds]),
        "tab_q": leaves("q"), "tab_k": leaves("k"), "tab_v": leaves("v"), "tab_f": leaves("f"),
        "gamma_in": a["L1_ffn_gamma"], "peer_wq": a["L1_ffn_wq"].T,
        "peer_keys": a["L1_ffn_keys"].transpose(2, 0, 3, 1),
        "table_down": a["L1_ffn_table_down"][:EXPERTS].T, "table_up": a["L1_ffn_table_up"][:EXPERTS],
    }
    nc = bacc.Bacc("TRN2", target_bir_lowering=False, num_devices=1)
    arrays, aps = {}, []
    for name, v in ins.items():
        v = np.ascontiguousarray(v)
        arrays[name] = v
        aps.append(nc.dram_tensor(name, v.shape, mybir.dt.from_np(v.dtype), kind="ExternalInput").ap())
    out = nc.dram_tensor("out", (B, S, E), mybir.dt.float32, kind="ExternalOutput").ap()
    decoder_program(nc, *aps, out)
    r = run_bass_kernel_spmd(nc, [arrays], core_ids=[0])
    return r.results[0]["out"]
```

```python
import concourse.bass as bass
from concourse import mybir
from contextlib import ExitStack

B, S, E, H = 4, 256, 128, 16
D = E // H
P = 128
SUB = S // P
T = B * SUB
M = 4 * D
HG = P // M
DEPTH = 8
LEAVES = 2 ** DEPTH
NODES = LEAVES - 1
LW = 16
ROW1 = LW * E + LW
ROW2 = LW * E + E
RING1, RING2 = 3, 5
PK = 32
PH = 8
PD = 64
TOPK = 16
EXPERTS = PK * PK
NCAND = [TOPK // (a + 1) for a in range(TOPK)]
CAND = sum(NCAND)
TERMS = [(0, 0), (1, 0), (2, 0), (0, 1), (1, 1), (0, 2)]
KS = len(TERMS) * D
KM = KS + 3
BIG = 1.0e30
VW = 32


def decoder_program(nc, x_in, ctx_in, mask_in, attn_w, attn_bias, proj_t, node_w, node_b,
                    tab1_q, tab1_k, tab1_v, tab1_f, tab2_q, tab2_k, tab2_v, tab2_f,
                    gamma_in, peer_wq, peer_keys, table_down, table_up, out):
    f32, bf16 = mybir.dt.float32, mybir.dt.bfloat16
    i32, u32 = mybir.dt.int32, mybir.dt.uint32
    ALU = mybir.AluOpType
    ACT = mybir.ActivationFunctionType
    AX = mybir.AxisListType
    RMAX = bass.bass_isa.ReduceOp.max

    stack = ExitStack()
    with stack:
        def sb(name, shape, dt=f32):
            return stack.enter_context(nc.sbuf_tensor(name, shape, dt))

        def sem(name):
            return stack.enter_context(nc.semaphore(name))

        BANK = 512
        psum = stack.enter_context(nc.psum_tensor("psum", [P, 8 * BANK], f32))

        def bank(k, a=0, b=BANK):
            return psum[:, k * BANK + a:k * BANK + b]

        w_sb = sb("w_sb", [P, 16, P])
        NB = 9 * P + 4 * NODES
        bias_p = sb("bias_p", [3, NB], bf16)
        nodes_sb = sb("nodes_sb", [P, 4, NODES])
        gamma_sb = sb("gamma_sb", [P, P])
        wq_sb = sb("wq_sb", [P, 2 * PH * PD])
        keys_sb = sb("keys_sb", [P, 8, 2 * PK])
        down_sb = sb("down_sb", [P, EXPERTS])
        up_sb = sb("up_sb", [P, EXPERTS // P, P])
        maskrow = sb("maskrow", [P, B * S])
        identf = sb("identf", [P, P])
        identb = sb("identb", [P, P], bf16)
        ones = sb("ones", [3, S], bf16)
        head16 = sb("head16", [P, H])
        half16 = sb("half16", [P, H])
        projb = sb("projb", [P, M])
        feat_w = sb("feat_w", [P, H, M])
        blockm = sb("blockm", [P, HG, D + 1])
        causal_q = sb("causal_q", [P, P], bf16)
        causal_k = sb("causal_k", [P, P], bf16)
        halves = sb("halves", [P, 2, T])
        even_ids = sb("even_ids", [P, LEAVES // 2])
        arena2 = sb("arena2", [P, 5120])
        arena3 = sb("arena3", [P, 3072])

        x = sb("x", [P, T, P])
        ctx_t = sb("ctx_t", [P, B * S])
        stats = sb("stats", [P, 2, 6])
        mv = sb("mv", [P, 2, 2])
        var_e = sb("var_e", [P, 2])
        rstd = sb("rstd", [P, 2])
        xn = [sb(f"xn{i}", [P, SUB, P]) for i in range(3)]
        xn_t = [sb(f"xn_t{i}", [P, S]) for i in range(2)]
        qk_f = [sb(f"qk_f{i}", [P, 2, S]) for i in range(2)]
        resid_f = sb("resid_f", [P, 2, S])
        parts = [sb(f"parts{i}", [P, 3, 2, S], bf16) for i in range(2)]
        vaug = [sb(f"vaug{i}", [P, SUB, H, VW]) for i in range(4)]
        rowmax = [sb(f"rowmax{i}", [P, SUB, H]) for i in range(2)]
        negmax = sb("negmax", [P, SUB, H])
        remax = sb("remax", [P, SUB, H])
        mparts = [sb(f"mparts{i}", [P, SUB, 3, H], bf16) for i in range(2)]
        mt = [sb(f"mt{i}", [3 * H, S], bf16) for i in range(2)]
        probs = [arena3[:, i * 512:(i + 1) * 512] for i in range(4)]
        o_sb = arena3[:, 2048:3072].rearrange("p (g n) -> p g n", n=S)
        rsum = sb("rsum", [P, SUB, H])
        o_n = sb("o_n", [P, SUB, P])
        o_t = sb("o_t", [P, S])
        arena = sb("arena", [P, 17408])
        aw = arena[:, :].bitcast(bf16)
        STK = H * 2 * S
        stk = [aw[0:64, i * STK:(i + 1) * STK].rearrange("p (h w n) -> p h w n", h=H, w=2)
               for i in range(3)]
        bias_sb, bias_w = arena[0:3, 0:9 * P], arena[0:3, 9 * P:9 * P + 9 * P // 2].bitcast(bf16)
        nbias_sb, nbias_w = arena2[0:3, 4096:5116], arena2[0:3, 3072:3072 + 510].bitcast(bf16)
        leaf1 = [arena[:, i * ROW1:(i + 1) * ROW1] for i in range(RING1)]
        leaf2 = [arena[:, RING1 * ROW1 + i * ROW2:RING1 * ROW1 + (i + 1) * ROW2] for i in (3, 4, 1, 0, 2)]
        zk = arena[:, 12288:16384].rearrange("p (t c) -> p t c", t=T)
        qf_t = arena2[:, 0:4096].rearrange("p (t g n) -> p t g n", t=T, g=HG)
        zq = arena3[:, 0:1024]
        eq = arena3[:, 1024:2048]
        kf = [k.rearrange("p (s c) -> p s c", s=SUB) for k in (arena3[:, 2048:3072], arena[:, 16384:17408])]
        sq = sb("sq", [P, 2, S])
        ctx_m = sb("ctx_m", [P, HG, HG * (D + 1)])
        ctx_rows = arena[:, 8192:9216].rearrange("p (t n) -> p t n", t=T)
        mask_i = arena[:, 9216:10240].bitcast(i32)
        stab = sb("stab", [P, 2, H])
        kmax = sb("kmax", [P, T])
        kmax1 = sb("kmax1", [P, 1])
        kmaxg = sb("kmaxg", [P, 1])
        nkmax = sb("nkmax", [P, 1])

        fx = sb("fx", [P, T, P])
        fstats, fmean = sb("fstats", [P, T, 6]), sb("fmean", [P, T, 2])
        fpow = [sb(f"fpow{i}", [P, T]) for i in range(4)]
        fx_t = arena3[:, 0:256]
        dec = arena2[:, 0:768].bitcast(i32).rearrange("p (f n) -> p f n", f=6)
        walk = arena2[:, 768:1536].rearrange("p (f n) -> p f n", f=6)
        leaf_no = [sb(f"leaf_no{i}", [P, 6], u32) for i in range(B)]
        leaf_nof = [sb(f"leaf_nof{i}", [P, 2], u32) for i in range(B)]
        hid = [sb(f"hid{i}", [P, LW]) for i in range(4)]
        hact = [sb(f"hact{i}", [P, LW]) for i in range(2)]
        fqk_t = [arena2[:, 3072 + i * 512:3584 + i * 512].rearrange("p (f n) -> p f n", f=2) for i in range(2)]
        fval = [arena2[:, 4096 + i * 256:4352 + i * 256].rearrange("p (s e) -> p s e", s=SUB) for i in range(2)]
        frow = sb("frow", [P, 2])
        fneg = sb("fneg", [P, 2])
        fsum = sb("fsum", [P, 2])
        frec = sb("frec", [P, 2])
        att = arena2[:, 4608:5120].rearrange("p (s n) -> p s n", s=SUB)
        att_t = arena3[:, 768:1280].rearrange("p (c n) -> p c n", c=4)
        fy = [arena3[:, i:i + 256].rearrange("p (s e) -> p s e", s=SUB) for i in (1280, 1536, 2048, 2304)]
        fy_t = arena3[:, 1792:2048]
        qp_t = [i.rearrange("p (c n) -> p c n", c=8) for i in (arena[:, 0:2048], arena2[:, 0:2048])]
        sim = arena[:, 2048:6144].rearrange("p (t g k) -> p t g k", t=T, g=2 * PH)
        hg = arena[:, 6144:14336].rearrange("p (c n) -> p c n", c=8)
        grid = [arena[:, 14336 + i * 1024:15360 + i * 1024] for i in range(3)]
        picked = [arena2[:, i * 1024:(i + 1) * 1024] for i in range(2)] + [sb("picked2", [P, EXPERTS])[:, :]]
        px_t = [arena3[:, i:i + 2 * S] for i in (0, 2404)]
        simw = arena3[:, 768:1280].rearrange("p (g k) -> p g k", k=PK)
        best = arena3[:, 1280:1536].rearrange("p (g k) -> p g k", k=TOPK)
        pairs = arena3[:, 1536:1536 + PH * CAND].rearrange("p (g k) -> p g k", k=CAND)
        pairw = arena3[:, 2000:2000 + PH * CAND].rearrange("p (g k) -> p g k", k=CAND)
        top = [vaug[t // SUB][:, t % SUB, 0:PH, 0:TOPK] for t in range(T)]
        texp = [vaug[t // SUB][:, t % SUB, PH:2 * PH, 0:TOPK] for t in range(T)]
        tneg = sb("tneg", [P, T, PH])
        tsum = sb("tsum", [P, PH])
        trec = [sb(f"trec{i}", [P, PH]) for i in range(2)]
        diag = [arena2[:, 2048 + i * 1024:3072 + i * 1024].rearrange("p (h n) -> p h n", h=PH) for i in range(2)]
        mixed = arena2[:, 4096:5120].rearrange("p (c n) -> p c n", c=8)

        in_x, in_w, in_ctx = sem("in_x"), sem("in_w"), sem("in_ctx")
        in_tab, in_keys, zeros_done = sem("in_tab"), sem("in_keys"), sem("zeros_done")
        consts, vaug_clear = sem("consts"), sem("vaug_clear")
        ctxt_ps, ctxt_ready, mask_ready, feat_ready = (sem("ctxt_ps"), sem("ctxt_ready"),
                                                       sem("mask_ready"), sem("feat_ready"))
        var_ready, rstd_ready, xn_ready = sem("var_ready"), sem("rstd_ready"), sem("xn_ready")
        xt_ps, xt_ready = sem("xt_ps"), sem("xt_ready")
        qk_ps, qk_ready, v_ps, v_ready = sem("qk_ps"), sem("qk_ready"), sem("v_ps"), sem("v_ready")
        part0_ready, part1_ready, parts_ready = sem("part0_ready"), sem("part1_ready"), sem("parts_ready")
        stk_ready = [sem(f"stk_ready{i}") for i in range(3)]
        max_in = [sem(f"max_in{i}") for i in range(3)]
        ones_ready = sem("ones_ready")
        rows_ps, rows_max = sem("rows_ps"), sem("rows_max")
        mparts_ready, mt_ps, mt_ready = sem("mparts_ready"), sem("mt_ps"), sem("mt_ready")
        cols_ps, probs_ready, pv_ps = sem("cols_ps"), sem("probs_ready"), sem("pv_ps")
        o_ready, ot_ps, ot_ready = sem("o_ready"), sem("ot_ps"), sem("ot_ready")
        y_ps, x_ready = sem("y_ps"), sem("x_ready")
        sq_ready, dd_ps, zq_ready, zk_ready = sem("sq_ready"), sem("dd_ps"), sem("zq_ready"), sem("zk_ready")
        eq_ready, qft_ps, qft_ready = sem("eq_ready"), sem("qft_ps"), sem("qft_ready")
        kmax_ready, kmax_all, nkmax_ready = sem("kmax_ready"), sem("kmax_all"), sem("nkmax_ready")
        ke_ready, kf_ready, cx_ps, cx_ready = sem("ke_ready"), sem("kf_ready"), sem("cx_ps"), sem("cx_ready")
        dve_step, act_step, pool_step = sem("dve_step"), sem("act_step"), sem("pool_step")
        out_done = sem("out_done")
        bias_ready, osb_ready, or_ps = sem("bias_ready"), sem("osb_ready"), sem("or_ps")
        fv, fp, fx_ready, fxt_ps, fxt_ready, lg_ps = (sem("fv"), sem("fp"), sem("fx_ready"), sem("fxt_ps"),
                                                      sem("fxt_ready"), sem("lg_ps"))
        dec_ready, idx_ready, leaf_done = sem("dec_ready"), sem("idx_ready"), sem("leaf_done")
        rows1_in = [sem(f"rows1_in{i}") for i in range(RING1)]
        rows2_in = [sem(f"rows2_in{i}") for i in range(RING2)]
        scaled, leaf_kept, leaf_added = sem("scaled"), sem("leaf_kept"), sem("leaf_added")
        fs_ps, fmax_ready = sem("fs_ps"), sem("fmax_ready")
        att_ready, at_ps, at_ready, fy_ps, fy_ready = (sem("att_ready"), sem("at_ps"), sem("at_ready"),
                                                       sem("fy_ps"), sem("fy_ready"))
        fyt_ps, fyt_ready, lgf_ps, decf_ready, idxf_ready = (sem("fyt_ps"), sem("fyt_ready"), sem("lgf_ps"),
                                                             sem("decf_ready"), sem("idxf_ready"))
        fh_ready, fg_ready = sem("fh_ready"), sem("fg_ready")
        pv2, pp2, px_ready, pxt_ps, pxt_ready = (sem("pv2"), sem("pp2"), sem("px_ready"), sem("pxt_ps"),
                                                 sem("pxt_ready"))
        unit_ps, unit_ready, sim_ps, sim_ready = sem("unit_ps"), sem("unit_ready"), sem("sim_ps"), sem("sim_ready")
        grid_ready, e_ready, picked_ready, mix_ps = sem("grid_ready"), sem("e_ready"), sem("picked_ready"), sem("mix_ps")
        tdif_ready, texp_ready, trec_ready, diag_ready = (sem("tdif_ready"), sem("texp_ready"), sem("trec_ready"),
                                                          sem("diag_ready"))
        mixed_ready, po_ps, tile_ready = sem("mixed_ready"), sem("po_ps"), sem("tile_ready")

        def chain(eng, s):
            n = [0]

            def link(i):
                n[0] += 1
                i.then_inc(s, 1)
                eng.wait_ge(s, n[0])
            return link

        def stage(n):
            return n // B

        def batch(n):
            return n % B

        def bank_o(s, h, n=1):
            return bank(7)[:, s * 144 + h * 9:s * 144 + (h + n) * 9]

        mt_bank = psum[0:3 * H, 5 * BANK:5 * BANK + P].bitcast(bf16)

        def split_bias(engine, link, a, b):
            p = bias_p[:, a:b]
            if a < 9 * P:
                src, w = bias_sb[:, a:b], bias_w[:, a:b]
            else:
                src, w = nbias_sb[:, a - 9 * P:b - 9 * P], nbias_w[:, a - 9 * P:b - 9 * P]
            link(engine.tensor_copy(w, src))
            link(engine.tensor_scalar(p, w, identf[0:3, 0:1], None, ALU.mult))
            for j in (1, 2):
                link(engine.tensor_tensor(src, src, w, ALU.subtract))
                link(engine.tensor_copy(w, src))
                if j == 2:
                    link(engine.tensor_scalar(w, w, identf[0:3, 2:3], None, ALU.mult))
                else:
                    link(engine.scalar_tensor_tensor(out=p, in0=w, scalar=identf[0:3, 1:2], in1=p,
                                                     op0=ALU.mult, op1=ALU.add))
            link(engine.tensor_tensor(p, p, w, ALU.add))
        RUNS = [(4, 7), (8, 15)]

        def run_of(n):
            return next((r for r in RUNS if r[0] <= n <= r[1]), (0, B - 1))

        def tail_bank(n):
            return 0 if n < B else 4

        def tails_ahead(n):
            return 0 if n < B + 2 else max(n - 3, run_of(n)[0])

        def pres_ahead(n):
            first, last = run_of(n)
            return last + 1 if first == 0 else min(n + 4, last + 1)

        def turns_ahead(n):
            first = run_of(n)[0]
            return (max(n - 1, first + 1) if n - first > 1 else first) - B

        ROWS_AT = [[2 * h, 2 * h + 1] if h < 5 else [h + 5] if h < 11 else [] for h in range(H)]
        TURN = 13

        def placed(n):
            return len([m for m in range(B, n + 1) if m % 3 == n % 3])

        def finish_sp(sp):
            out_t = out.rearrange("b (s p) e -> p (b s) e", p=P)
            for t in range(T):
                sp.wait_ge(tile_ready, t + 1)
                sp.dma_start(out_t[:, t, :], x[:, t, :]).then_inc(out_done, 16)
            sp.wait_ge(out_done, 16 * T)

        ORDER, STAGES, STAGES_V = [], [], []
        NEXT = (2 * B, 2 * B + 1)
        SPOTS = {"score": 0, "weigh": 1, "mix": 2, "turn_f": 4}
        SPOTS_V = {"weigh": 2, "attend": 4, "route_f": 6}
        LAST_SPOTS = {"score": 0, "weigh": 1, "mix": 1, "turn_f": 2}
        LAST_SPOTS_V = {"weigh": 1, "attend": 2, "route_f": 3}
        for slot in range(B + 2):
            now, a = [], slot - 1
            if slot < B:
                now += [(slot, s, f) for s in range(SUB) for f in range(3)]
            if slot >= B:
                now += [(b, s, 3) for b in (range(B - 1) if slot == B else [B - 1]) for s in range(SUB)]
            for j in range(7 + len(now)):
                for stages, spots in ((STAGES, LAST_SPOTS if slot == B else SPOTS),
                                      (STAGES_V, LAST_SPOTS_V if slot == B else SPOTS_V)):
                    if slot + 1 < B:
                        stages += [("turn", slot + 1)] * (j == 0) + [("route", slot + 1)] * (j == 3)
                    if 0 <= a < B:
                        stages += [(what, a) for what, spot in spots.items() if spot == j]
                    if slot == B and j in (5, 6):
                        stages += [("next", NEXT[j - 5])]
                    if j < len(now):
                        stages += [("leaf", len(ORDER))]
                if j < len(now):
                    ORDER += [now[j]]

        def last_tree(g):
            return ORDER[g][2] == 3

        def leaves_upto(g, last):
            return len([i for i in range(g + 1) if last_tree(i) == last])

        UNITS = 4 * B
        AHEAD = 27
        CHOICES = {}
        for i in range(AHEAD, 7 * T):
            CHOICES.setdefault((i - AHEAD) * 7 // 4, []).append(i)

        def unit_bank(u):
            return psum[:, (u % 2) * 2 * BANK:((u % 2) * 2 + 2) * BANK]

        def px_of(b):
            return px_t[b // 2][:, b % 2 * S:(b % 2 + 1) * S]

        TABS1, TABS2 = [tab1_q, tab1_k, tab1_v, tab1_f], [tab2_q, tab2_k, tab2_v, tab2_f]

        block = stack.enter_context(nc.Block())

        @block.sync
        def _(sp):
            sp.dma_start(x[:, :, :], x_in.rearrange("b (s p) e -> p (b s) e", p=P)).then_inc(in_x, 16)
            sp.dma_start(w_sb[:, 0:4, :], attn_w[0:4].rearrange("a i o -> i a o")).then_inc(in_w, 16)
            sp.dma_start(bias_sb, attn_bias.partition_broadcast(3)).then_inc(in_w, 16)
            sp.dma_start(projb[:, :], proj_t).then_inc(in_w, 16)
            sp.dma_start(ctx_rows, ctx_in.rearrange("b (s p) e -> p (b s) e", p=P)).then_inc(in_ctx, 16)
            sp.dma_start(mask_i, mask_in.rearrange("b s -> (b s)").partition_broadcast(P)).then_inc(in_ctx, 16)
            sp.dma_start(w_sb[:, 4:16, :], attn_w[4:16].rearrange("a i o -> i a o")).then_inc(in_ctx, 16)
            sp.dma_start(nodes_sb[:, :, :], node_w).then_inc(in_tab, 16)
            sp.dma_start(nbias_sb, node_b.partition_broadcast(3)).then_inc(in_tab, 16)
            sp.dma_start(gamma_sb[:, :], gamma_in.partition_broadcast(P)).then_inc(in_keys, 16)
            sp.dma_start(wq_sb[:, :], peer_wq).then_inc(in_keys, 16)
            sp.dma_start(down_sb[:, :], table_down).then_inc(in_keys, 16)
            sp.dma_start(up_sb[:, :, :], table_up.rearrange("(c p) e -> p c e", p=P)).then_inc(in_keys, 16)
            sp.wait_ge(zeros_done, 1)
            for side in range(2):
                for h in range(PH):
                    r, c = (h % 2) * PD, side * 4 + h // 2
                    sp.dma_start(keys_sb[r:r + PD, c, (h % 2) * PK:(h % 2 + 1) * PK],
                                 peer_keys[side, h]).then_inc(in_keys, 16)

            def place(n):
                if n - 3 >= B:
                    sp.wait_ge(cols_ps, (n - 3 - B + 1) * H)
                for part, ready in enumerate((part0_ready, part1_ready, parts_ready)):
                    sp.wait_ge(ready, n - B + 1)
                    for r, term in enumerate(TERMS):
                        for w in range(2):
                            if term[w] == part:
                                sp.dma_start(stk[n % 3][r * D:(r + 1) * D, :, w, :],
                                             parts[n % 2][:, part, w, :]).then_inc(stk_ready[n % 3], 16)

            def place_max(n):
                sp.wait_ge(mt_ready, n - B + 1)
                sp.dma_start(stk[n % 3][KS:KM, :, 0, :], mt[n % 2][:, :]).then_inc(max_in[n % 3], 16)

            def run(first, last):
                if first == B:
                    sp.wait_ge(consts, 1)
                    sp.wait_ge(ctxt_ready, 2)
                    sp.wait_ge(mask_ready, 1)
                    sp.wait_ge(bias_ready, 2)
                else:
                    sp.wait_ge(leaf_done, len(ORDER) - 2)
                place(first)
                for i in range(3):
                    if first > B and i == 1:
                        sp.wait_ge(fh_ready, len(ORDER))
                    sp.dma_start(stk[(first + i) % 3][KS:KM, :, 1, :],
                                 ones[:, :].unsqueeze(1).to_broadcast([KM - KS, H, S])).then_inc(ones_ready, 16)
                place(first + 1)
                place_max(first)
                for n in range(first, last + 1):
                    if n + 2 <= last:
                        place(n + 2)
                    if n + 1 <= last:
                        place_max(n + 1)

            run(*RUNS[0])
            run(*RUNS[1])
            finish_sp(sp)

        @block.gpsimd
        def _(pool):
            link = chain(pool, pool_step)
            nc.gpsimd.memset(keys_sb[:, :, :], 0.0).then_inc(zeros_done, 1)
            link(nc.gpsimd.memset(identf[:, :], 0.0))
            link(nc.gpsimd.affine_select(out=identf[:, :], in_=identf[:, :], compare_op=ALU.not_equal, fill=1.0,
                                         base=0, pattern=[[-1, P]], channel_multiplier=1))
            link(nc.gpsimd.tensor_copy(identb[:, :], identf[:, :]))
            link(nc.gpsimd.memset(ones[:, :], 1.0))
            link(nc.gpsimd.memset(halves[:, 0, :], -0.5))
            link(nc.gpsimd.memset(halves[:, 1, :], 0.5))
            link(nc.gpsimd.memset(head16[:, :], 0.0))
            for j in range(D):
                link(nc.gpsimd.affine_select(out=head16[:, :], in_=head16[:, :], compare_op=ALU.not_equal,
                                             fill=1.0, base=-H * j, pattern=[[-1, H]], channel_multiplier=1))
            link(nc.gpsimd.memset(blockm[:, :, :], 1.0))
            link(nc.gpsimd.affine_select(out=blockm[:, :, :], in_=blockm[:, :, :], compare_op=ALU.is_ge, fill=0.0,
                                         base=0, pattern=[[-M, HG], [0, D + 1]], channel_multiplier=1))
            link(nc.gpsimd.affine_select(out=blockm[:, :, :], in_=blockm[:, :, :], compare_op=ALU.is_ge, fill=0.0,
                                         base=M - 1, pattern=[[M, HG], [0, D + 1]], channel_multiplier=-1))
            nc.gpsimd.tensor_scalar(half16[:, :], head16[:, :], 0.5, None, ALU.mult).then_inc(consts, 1)

            def power(n):
                pool.wait_ge(var_ready, n + 1)
                nc.gpsimd.tensor_tensor(rstd[:, :], var_e[:, :], halves[:, 0, 0:2], ALU.pow).then_inc(rstd_ready, 1)

            def squares(n):
                pool.wait_ge(qk_ready, n + 1)
                if n >= 1:
                    pool.wait_ge(dd_ps, n)
                nc.gpsimd.tensor_tensor(sq[:, :, :], qk_f[n % 2][:, :, :], qk_f[n % 2][:, :, :], ALU.mult).then_inc(sq_ready, 1)

            def split(n):
                q = qk_f[n % 2][:, :, :]
                p = parts[n % 2]
                pool.wait_ge(qk_ready, n + 1)
                if n - 2 >= B:
                    pool.wait_ge(stk_ready[(n - 2) % 3], 16 * 12 * placed(n - 2))
                if stage(n) == 1:
                    b = batch(n)
                    link(nc.gpsimd.tensor_tensor(qk_f[n % 2][:, 0, :], qk_f[n % 2][:, 0, :],
                                                 maskrow[:, b * S:(b + 1) * S], ALU.mult))
                nc.gpsimd.tensor_copy(p[:, 0, :, :], q).then_inc(part0_ready, 1)
                pool.wait_ge(part0_ready, n - B + 1)
                link(nc.gpsimd.tensor_tensor(resid_f[:, :, :], q, p[:, 0, :, :], ALU.subtract))
                nc.gpsimd.tensor_copy(p[:, 1, :, :], resid_f[:, :, :]).then_inc(part1_ready, 1)
                pool.wait_ge(part1_ready, n - B + 1)
                nc.gpsimd.tensor_tensor(p[:, 2, :, :], resid_f[:, :, :], p[:, 1, :, :], ALU.subtract).then_inc(parts_ready, 1)
                pool.wait_ge(parts_ready, n - B + 1)

            for n in range(B):
                power(n)
                squares(n)
            for m, sign in ((causal_q, 1), (causal_k, -1)):
                link(nc.gpsimd.memset(m[:, :], 0.0))
                link(nc.gpsimd.affine_select(out=m[:, :], in_=m[:, :], compare_op=ALU.is_ge, fill=-BIG,
                                             base=0, pattern=[[-sign, P]], channel_multiplier=sign))
            link(nc.gpsimd.iota(even_ids[:, :], pattern=[[2, LEAVES // 2]], base=0, channel_multiplier=0,
                                allow_small_or_imprecise_dtypes=True))
            nc.gpsimd.memset(o_t[:, 0:1], 0.0).then_inc(consts, 1)
            pool.wait_ge(kmax_ready, 1)
            nc.gpsimd.partition_all_reduce(kmaxg[:, :], kmax1[:, :], P, RMAX).then_inc(kmax_all, 1)

            def run(first, last):
                for n in range(first, last + 1):
                    if n + 2 <= last:
                        split(n + 2)
                    if n + 3 <= last:
                        power(n + 3)

            def ffn():
                def powers(part, a, b):
                    for j, (i, o, e) in enumerate(((0, 1, 0), (0, 2, 1), (2, 3, 0))):
                        pool.wait_ge(fv, 3 * part + j + 1)
                        nc.gpsimd.tensor_tensor(fpow[o][:, a:b], fpow[i][:, a:b], halves[:, e, a:b],
                                                ALU.pow).then_inc(fp, 1)

                powers(0, 0, 2 * SUB)
                for g, (b, s, f) in enumerate(ORDER):
                    if g == RING1:
                        powers(1, 2 * SUB, T)
                    if f == 3:
                        pool.wait_ge(idxf_ready, b + 1)
                        no = leaf_nof[b][:, s:s + 1]
                    else:
                        pool.wait_ge(idx_ready, b + 1)
                        no = leaf_no[b][:, f * SUB + s:f * SUB + s + 1]
                    if g >= RING1:
                        pool.wait_ge(fh_ready, g - RING1 + 1)
                    nc.gpsimd.indirect_dma_start(leaf1[g % RING1], None, TABS1[f],
                                                 bass.IndirectOffsetOnAxis(no, 0)).then_inc(rows1_in[g % RING1], 16)
                    if g >= RING2:
                        pool.wait_ge(leaf_done, g - RING2 + 1)
                    nc.gpsimd.indirect_dma_start(leaf2[g % RING2], None, TABS2[f],
                                                 bass.IndirectOffsetOnAxis(no, 0)).then_inc(rows2_in[g % RING2], 16)
                    if g >= len(ORDER) - SUB:
                        power(NEXT[g - len(ORDER)])
                for n in NEXT:
                    split(n)
                power(NEXT[-1] + 1)

            def peer():
                for part, (a, b) in enumerate(((0, 2 * SUB), (2 * SUB, T))):
                    for j, (i, o, e) in enumerate(((0, 1, 0), (2, 3, 1))):
                        pool.wait_ge(pv2, 2 * part + j + 1)
                        nc.gpsimd.tensor_tensor(fpow[o][:, a:b], fpow[i][:, a:b], halves[:, e, a:b],
                                                ALU.pow).then_inc(pp2, 1)
                for t in range(T):
                    pool.wait_ge(sim_ready, t + 1)
                    for h in range(PH):
                        k = t * PH + h
                        if k >= 3:
                            pool.wait_ge(picked_ready, k - 2)
                        nc.gpsimd.tensor_tensor(grid[k % 3].rearrange("p (i j) -> p i j", i=PK),
                                                sim[:, t, h, :].unsqueeze(2).to_broadcast([P, PK, PK]),
                                                sim[:, t, PH + h, :].unsqueeze(1).to_broadcast([P, PK, PK]),
                                                ALU.add).then_inc(grid_ready, 1)

            pool.wait_ge(kmax_all, 1)
            power(B)
            power(B + 1)
            split(B)
            power(B + 2)
            split(B + 1)
            run(*RUNS[0])
            ffn()
            run(*RUNS[1])
            peer()

        @block.scalar
        def _(act):
            link = chain(act, act_step)

            def copy(o, i, s):
                nc.scalar.activation(o, i, ACT.Copy).then_inc(s, 1)

            def evac_x(n):
                act.wait_ge(xt_ps, n + 1)
                if n >= 2:
                    act.wait_ge(v_ps, n - 1)
                copy(xn_t[n % 2][:, :], bank(4, 0, S), xt_ready)

            def evac_qk(n):
                act.wait_ge(qk_ps, n + 1)
                if n >= B + 2:
                    act.wait_ge(parts_ready, n - B - 1)
                elif n >= 2:
                    act.wait_ge(dd_ps, min(n - 1, B))
                scale = float(D) ** -0.25 if stage(n) == 0 else 1.0
                nc.scalar.activation(qk_f[n % 2][:, :, :], bank(5).rearrange("p (w n) -> p w n", w=2),
                                     ACT.Copy, scale=scale).then_inc(qk_ready, 1)

            def evac_v(n):
                act.wait_ge(v_ps, n + 1)
                act.wait_ge(vaug_clear, 1)
                if n >= 4:
                    act.wait_ge(pv_ps, (n - 3) if n - 4 < B else B + (n - 3 - B) * H)
                copy(vaug[n % 4][:, :, :, 0:D],
                     bank(4, S, 2 * S).rearrange("p (s h d) -> p s h d", s=SUB, h=H), v_ready)

            def evac_qkv(n):
                evac_qk(n)
                evac_v(n)

            def evac_ot(n):
                act.wait_ge(ot_ps, n + 1)
                if n >= 1:
                    act.wait_ge(y_ps, n)
                copy(o_t[:, :], bank(tail_bank(n), 0, S), ot_ready)

            def evac_o(n):
                act.wait_ge(pv_ps, B + (n - B + 1) * H)
                if n > B:
                    act.wait_ge(or_ps, n - B)
                copy(o_sb[:, :, :], psum[:, 6 * BANK:8 * BANK].rearrange("p (g n) -> p g n", n=S), osb_ready)

            def evac_mt(n):
                act.wait_ge(mt_ps, n - B + 1)
                if n - 2 >= B:
                    act.wait_ge(max_in[(n - 2) % 3], 16 * placed(n - 2))
                copy(mt[n % 2][:, :], mt_bank, mt_ready)

            def exps(n, h):
                act.wait_ge(cols_ps, (n - B) * H + h + 1)
                k = (n - B) * H + h
                if k >= 4:
                    act.wait_ge(pv_ps, B + k - 3)
                w = SUB * S - P if stage(n) == 2 else SUB * S
                nc.scalar.activation(probs[k % 4][:, 0:w], bank(2 + k % 2, 0, w), ACT.Exp, scale=float(D) ** -0.5).then_inc(probs_ready, 1)

            evac_x(0)
            evac_qkv(0)
            for n in range(B):
                if n + 1 < B:
                    evac_x(n + 1)
                    evac_qkv(n + 1)
                act.wait_ge(zq_ready, n + 1)
                if n >= 1:
                    act.wait_ge(qft_ps, n)
                nc.scalar.activation(eq, zq, ACT.Exp).then_inc(eq_ready, 1)
            for half in range(2):
                act.wait_ge(ctxt_ps, half + 1)
                copy(ctx_t[:, half * BANK:(half + 1) * BANK], bank(2 + 4 * half), ctxt_ready)
            act.wait_ge(nkmax_ready, 1)
            for n in range(B):
                if n >= 2:
                    act.wait_ge(cx_ps, n - 1)
                nc.scalar.activation(kf[n % 2], zk[:, SUB * n:SUB * n + SUB, :], ACT.Exp,
                                     bias=nkmax[:, 0:1]).then_inc(ke_ready, 1)
                if n >= 1:
                    evac_ot(n - 1)
            evac_x(B)
            evac_qkv(B)
            evac_ot(B - 1)
            evac_x(B + 1)
            evac_qkv(B + 1)

            def run(first, last):
                evac_mt(first)
                for n in range(first, last + 1):
                    if n + 2 <= last:
                        evac_x(n + 2)
                    if n > first:
                        evac_o(n - 1)
                    for h in range(H):
                        exps(n, h)
                        if n + 2 <= last and h == 0:
                            evac_qk(n + 2)
                        if n + 2 <= last and h == 1:
                            evac_v(n + 2)
                        if h == TURN and n + 1 <= last:
                            evac_mt(n + 1)
                        if h == 8 and n > first:
                            evac_ot(n - 1)
                evac_o(last)
                if first == B:
                    evac_fx(0)
                else:
                    evac_px(0)
                    evac_unit(0)
                evac_ot(last)
                if first > B:
                    evac_unit(1)

            def evac_fx(b):
                act.wait_ge(fxt_ps, b + 1)
                copy(fx_t[:, :], bank(4 if b else 3, 0, S), fxt_ready)

            def evac_px(i):
                act.wait_ge(pxt_ps, i + 1)
                copy(px_t[i], bank(7 if i else 3), pxt_ready)

            def evac_unit(u):
                b, c = u // 2 % B, u % 2 * 4
                act.wait_ge(unit_ps, u + 1)
                src = unit_bank(u).rearrange("p (c n) -> p c n", c=4)
                if u < 2 * B:
                    copy(qp_t[b % 2][:, c:c + 4, :], src, unit_ready)
                else:
                    nc.scalar.activation(hg[:, c:c + 4, b * S:(b + 1) * S], src, ACT.Gelu).then_inc(unit_ready, 1)

            def ffn():
                def keep(g):
                    b, s, f = ORDER[g]
                    act.wait_ge(leaf_done, g + 1)
                    copy(fval[b % 2][:, s, :] if f == 2 else fqk_t[b % 2][:, f, s * P:s * P + P],
                         bank(6 + g % 2, 0, P), leaf_kept)

                kept = 0
                for what, i in STAGES:
                    if what == "turn":
                        evac_fx(i)
                    elif what == "next":
                        evac_x(i)
                        evac_qkv(i)
                    elif what == "leaf":
                        act.wait_ge(fh_ready, i + 1)
                        nc.scalar.activation(hact[i % 2][:, :], hid[i % 4][:, :],
                                             ACT.Gelu if last_tree(i) else ACT.Relu).then_inc(fg_ready, 1)
                        act.wait_ge(fg_ready, i + 1)
                        act.wait_ge(rows2_in[i % RING2], 16 * (i // RING2 + 1))
                        for l in range(LW):
                            if l == LW // 2 and kept < i:
                                if not last_tree(i - 1):
                                    keep(i - 1)
                                kept = i
                            w = leaf2[i % RING2][:, l * E:(l + 1) * E]
                            a = nc.scalar.activation(w, w, ACT.Copy, scale=hact[i % 2][:, l:l + 1])
                            if l % 4 == 3:
                                a.then_inc(scaled, 1)
                    elif what == "score":
                        g = ORDER.index((i, SUB - 1, 2))
                        if kept == g:
                            keep(g)
                            kept = g + 1
                    elif what == "weigh":
                        act.wait_ge(fmax_ready, i + 1)
                        for s in range(SUB):
                            nc.scalar.activation(att[:, s, :], bank(5, s * S, s * S + S), ACT.Exp, bias=fneg[:, s:s + 1],
                                                 scale=float(E) ** -0.5, accum_out=fsum[:, s:s + 1]).then_inc(att_ready, 1)
                    elif what == "mix":
                        act.wait_ge(at_ps, i + 1)
                        copy(att_t[:, :, :], bank(5).rearrange("p (c n) -> p c n", c=4), at_ready)
                    elif what == "turn_f":
                        act.wait_ge(fyt_ps, i + 1)
                        copy(fy_t[:, :], bank(4, 0, S), fyt_ready)

            def peer():
                def evac_sims(t):
                    act.wait_ge(sim_ps, t + 1)
                    copy(sim[:, t, :, :], bank(5 + t % SUB).rearrange("p (g k) -> p g k", k=PK), sim_ready)

                for u in range(2, UNITS):
                    if u == 4:
                        evac_px(1)
                    evac_unit(u)
                    if u < T + 2:
                        evac_sims(u - 2)

                def top_exp(t):
                    act.wait_ge(tdif_ready, t + 1)
                    nc.scalar.activation(texp[t], texp[t], ACT.Exp).then_inc(texp_ready, 1)

                def diagonals(t, a, b):
                    act.wait_ge(trec_ready, t + 1)
                    if t >= 2:
                        act.wait_ge(mix_ps, (t - 1) * PH)
                    for h in range(a, b):
                        i = nc.scalar.activation(diag[t % 2][:, h, :], identf[:, :], ACT.Copy,
                                                 scale=trec[t % 2][:, h:h + 1])
                    i.then_inc(diag_ready, 1)

                top_exp(0)
                for t in range(T):
                    for h in range(PH):
                        k = t * PH + h
                        act.wait_ge(grid_ready, k + 1)
                        if k >= 2:
                            act.wait_ge(picked_ready, k - 1)
                        nc.scalar.activation(psum[:, (4 + 2 * (k % 2)) * BANK:(6 + 2 * (k % 2)) * BANK], grid[k % 3],
                                             ACT.Exp, bias=tneg[:, t, h:h + 1]).then_inc(e_ready, 1)
                        if k == 0:
                            for i in range(4):
                                diagonals(0, 2 * i, 2 * i + 2)
                        if h == 2 and t + 1 < T:
                            top_exp(t + 1)
                        if h >= 4 and t + 1 < T:
                            diagonals(t + 1, 2 * (h - 4), 2 * (h - 4) + 2)

            run(*RUNS[0])
            ffn()
            run(*RUNS[1])
            peer()

        @block.vector
        def _(dve):
            link = chain(dve, dve_step)

            def norm(n):
                b = batch(n)
                if n < B:
                    dve.wait_ge(in_x, 16)
                elif stage(n) == 2:
                    dve.wait_ge(leaf_added, SUB * (b + 1))
                else:
                    dve.wait_ge(x_ready, n - B + 1)
                for s in range(SUB):
                    link(nc.vector.bn_stats(stats[:, s, :], x[:, SUB * b + s, :]))
                    link(nc.vector.bn_aggr(mv[:, s, :], stats[:, s, :]))
                if n >= 1:
                    dve.wait_ge(rstd_ready, n)
                nc.vector.tensor_scalar(var_e[:, :], mv[:, :, 1], 1e-5, None, ALU.add).then_inc(var_ready, 1)
                dve.wait_ge(rstd_ready, n + 1)
                if n >= 3:
                    dve.wait_ge(xt_ps, n - 2)
                for s in range(SUB):
                    i = nc.vector.tensor_scalar(xn[n % 3][:, s, :], x[:, SUB * b + s, :], mv[:, s, 0:1],
                                                rstd[:, s:s + 1], ALU.subtract, ALU.mult)
                i.then_inc(xn_ready, 1)
                dve.wait_ge(xn_ready, n + 1)

            def onorm_rf(n):
                dve.wait_ge(pv_ps, n + 1)
                o4 = bank(7, 0, 288).rearrange("p (g c) -> p g c", c=D + 1)
                rs = rsum[:, :, :].rearrange("p s h -> p (s h)").unsqueeze(2)
                link(nc.vector.reciprocal(rs, o4[:, :, D:D + 1]))
                if n >= 1:
                    dve.wait_ge(ot_ps, n)
                nc.vector.tensor_tensor(o_n[:, :, :].rearrange("p s (h d) -> p (s h) d", d=D), o4[:, :, 0:D],
                                        rs.to_broadcast([P, SUB * H, D]), ALU.mult).then_inc(o_ready, 1)

            def onorm(n):
                dve.wait_ge(or_ps, n - B + 1)
                dve.wait_ge(ot_ps, n)
                for s in range(SUB):
                    o4 = bank(5 - s).rearrange("p (h c) -> p h c", c=VW)
                    link(nc.vector.reciprocal(rsum[:, s, :].unsqueeze(2), o4[:, :, D:D + 1]))
                    i = nc.vector.tensor_tensor(o_n[:, s, :].rearrange("p (h d) -> p h d", d=D), o4[:, :, 0:D],
                                                rsum[:, s, :].unsqueeze(2).to_broadcast([P, H, D]), ALU.mult)
                i.then_inc(o_ready, 1)

            def resid(n):
                b = batch(n)
                dve.wait_ge(y_ps, n + 1)
                nc.vector.tensor_tensor(x[:, SUB * b:SUB * b + SUB, :],
                                        bank(tail_bank(n) + 1, 0, S).rearrange("p (s e) -> p s e", s=SUB),
                                        x[:, SUB * b:SUB * b + SUB, :], ALU.add).then_inc(x_ready, 1)

            def row_max(n, h):
                k = (n - B) * H + h
                dve.wait_ge(rows_ps, k + 1)
                if stage(n) == 2:
                    nc.vector.tensor_reduce(rowmax[n % 2][:, 0, h:h + 1], bank(k % 2, 0, P), AX.X, ALU.max)
                    i = nc.vector.tensor_reduce(rowmax[n % 2][:, 1, h:h + 1], bank(k % 2, P, P + S), AX.X, ALU.max)
                else:
                    i = nc.vector.tensor_reduce(rowmax[n % 2][:, :, h], bank(k % 2).rearrange("p (s n) -> p s n", s=SUB),
                                                AX.X, ALU.max)
                i.then_inc(rows_max, 1)

            def max_parts(n):
                dve.wait_ge(rows_max, (n - B + 1) * H)
                if n - 2 >= B:
                    dve.wait_ge(mt_ps, n - 1 - B)
                mp = mparts[n % 2]
                link(nc.vector.tensor_scalar(negmax[:, :, :], rowmax[n % 2][:, :, :], -1.0, None, ALU.mult))
                link(nc.vector.tensor_copy(mp[:, :, 0, :], negmax[:, :, :]))
                link(nc.vector.tensor_tensor(remax[:, :, :], negmax[:, :, :], mp[:, :, 0, :], ALU.subtract))
                link(nc.vector.tensor_copy(mp[:, :, 1, :], remax[:, :, :]))
                nc.vector.tensor_tensor(mp[:, :, 2, :], remax[:, :, :], mp[:, :, 1, :], ALU.subtract).then_inc(mparts_ready, 1)
                dve.wait_ge(mparts_ready, n - B + 1)

            for i in range(4):
                link(nc.vector.memset(vaug[i][:, :, :, :], 0.0))
                i = nc.vector.memset(vaug[i][:, :, :, D:D + 1], 1.0)
            i.then_inc(vaug_clear, 1)
            norm(0)
            dve.wait_ge(consts, 1)
            dve.wait_ge(in_w, 48)
            split_bias(nc.vector, link, 0, 4 * P)
            nc.vector.tensor_copy(bias_w[:, 0:1], bias_p[:, 0:1]).then_inc(bias_ready, 1)
            nc.vector.tensor_tensor(feat_w[:, :, :], head16[:, :].unsqueeze(2).to_broadcast([P, H, M]),
                                    projb[:, :].unsqueeze(1).to_broadcast([P, H, M]), ALU.mult).then_inc(feat_ready, 1)
            for n in range(B):
                if n + 1 < B:
                    norm(n + 1)
                dve.wait_ge(dd_ps, n + 1)
                if n >= 1:
                    dve.wait_ge(eq_ready, n)
                ddq = psum[:, 0:2 * BANK].rearrange("p (g m) -> p g m", m=M)
                ddk = psum[:, 2 * BANK:4 * BANK].rearrange("p (g m) -> p g m", m=M)
                half_norm = bank(7, 0, 64).rearrange("p (w s h) -> p w (s h)", w=2, s=SUB)
                sv = stab[:, :, :].rearrange("p s h -> p (s h)")
                link(nc.vector.tensor_reduce(sv, ddq, AX.X, ALU.max))
                link(nc.vector.tensor_tensor(sv, half_norm[:, 0, :], sv, ALU.add))
                nc.vector.tensor_tensor(zq.rearrange("p (g m) -> p g m", m=M), ddq,
                                        sv.unsqueeze(2).to_broadcast([P, 2 * H, M]), ALU.subtract).then_inc(zq_ready, 1)
                nc.vector.tensor_reduce(kmax[:, SUB * n:SUB * n + SUB],
                                        psum[:, 2 * BANK:4 * BANK].rearrange("p (s c) -> p s c", s=SUB), AX.X, ALU.max)
                dve.wait_ge(zq_ready, n + 1)
                link(nc.vector.tensor_copy(sv, half_norm[:, 1, :]))
                nc.vector.tensor_tensor(zk[:, SUB * n:SUB * n + SUB, :].rearrange("p s (g m) -> p (s g) m", m=M), ddk,
                                        sv.unsqueeze(2).to_broadcast([P, 2 * H, M]), ALU.subtract).then_inc(zk_ready, 1)
                dve.wait_ge(zk_ready, n + 1)
                dve.wait_ge(qft_ps, n + 1)
                nc.vector.tensor_scalar(qf_t[:, SUB * n:SUB * n + SUB, :, :],
                                        psum[:, 0:2 * BANK].rearrange("p (s g n) -> p s g n", s=SUB, g=HG),
                                        1e-4, None, ALU.add).then_inc(qft_ready, 1)
                if n < B - 1:
                    split_bias(nc.vector, link, (4 + 2 * n) * P, min(6 + 2 * n, 9) * P)
            nc.vector.tensor_copy(bias_w[:, 0:1], bias_p[:, 0:1]).then_inc(bias_ready, 1)
            link(nc.vector.tensor_reduce(kmax1[:, :], kmax[:, :], AX.X, ALU.max))
            nc.vector.tensor_copy(kmax1[:, :], kmax1[:, :]).then_inc(kmax_ready, 1)
            dve.wait_ge(in_ctx, 48)
            nc.vector.tensor_scalar(maskrow[:, :], mask_i, 0.0, None, ALU.not_equal).then_inc(mask_ready, 1)
            dve.wait_ge(kmax_all, 1)
            nc.vector.tensor_scalar(nkmax[:, :], kmaxg[:, :], -1.0, None, ALU.mult).then_inc(nkmax_ready, 1)

            def key_features(n):
                dve.wait_ge(ke_ready, n + 1)
                nc.vector.tensor_scalar(kf[n % 2], kf[n % 2], 1e-4, None, ALU.add).then_inc(kf_ready, 1)

            def own_blocks(n):
                dve.wait_ge(cx_ps, n + 1)
                nc.vector.tensor_tensor(ctx_m[:, :, :], bank(3, 0, 144).rearrange("p (g c) -> p g c", g=HG),
                                        blockm[:, :, :].rearrange("p g c -> p (g c)").unsqueeze(1).to_broadcast([P, HG, 36]),
                                        ALU.mult).then_inc(cx_ready, 1)

            key_features(0)
            own_blocks(0)
            for n in range(B):
                if n + 1 < B:
                    key_features(n + 1)
                onorm_rf(n)
                if n >= 1:
                    resid(n - 1)
                if n + 1 < B:
                    own_blocks(n + 1)
                if 1 <= n < B - 1:
                    norm(B + n - 1)
            resid(B - 1)
            norm(B + 2)

            def run(first, last):
                for h in range(H):
                    row_max(first, h)
                max_parts(first)
                for n in range(first, last + 1):
                    for h in range(H):
                        if n + 1 <= last:
                            for hh in ROWS_AT[h]:
                                row_max(n + 1, hh)
                        if n > first and h == 5:
                            onorm(n - 1)
                        if n > first and h == 11:
                            resid(n - 1)
                        if n + 1 <= last and h == TURN - 2:
                            max_parts(n + 1)
                        if h == 13 and n + 3 <= last:
                            norm(n + 3)
                        if h == 8 and first == B:
                            if n == first:
                                dve.wait_ge(in_tab, 32)
                            j = 9 * P + (n - first) * NODES
                            split_bias(nc.vector, link, j, j + NODES)
                            if n == last:
                                nc.vector.tensor_copy(nbias_w[:, 0:1], bias_p[:, j:j + 1]).then_inc(bias_ready, 1)
                if first == B:
                    ffn_norm(0, 0, 2 * SUB)
                else:
                    peer_norm(0, 0, 2 * SUB)
                onorm(last)
                if first == B:
                    walk_of(0)
                resid(last)

            def moments(src, a, b):
                for t in range(a, b):
                    i = nc.vector.bn_stats(fstats[:, t, :], src[:, t, :])
                link(i)
                for t in range(a, b):
                    i = nc.vector.bn_aggr(fmean[:, t, :], fstats[:, t, :])
                link(i)

            def scale(src, r, a, b):
                for t in range(a, b):
                    i = nc.vector.tensor_scalar(fx[:, t, :], src[:, t, :], fmean[:, t, 0:1], r[:, t:t + 1],
                                                ALU.subtract, ALU.mult)
                return i

            def ffn_norm(part, a, b):
                moments(x, a, b)
                nc.vector.tensor_scalar(fpow[0][:, a:b], fmean[:, a:b, 1], 1e-5, None, ALU.add).then_inc(fv, 1)
                dve.wait_ge(fp, 3 * part + 1)
                link(scale(x, fpow[1], a, b))
                moments(fx, a, b)
                nc.vector.tensor_scalar(fpow[0][:, a:b], fmean[:, a:b, 1], float(E) / (E - 1), None,
                                        ALU.mult).then_inc(fv, 1)
                dve.wait_ge(fp, 3 * part + 2)
                nc.vector.tensor_scalar(fpow[2][:, a:b], fpow[2][:, a:b], 1e-5, None, ALU.add).then_inc(fv, 1)
                dve.wait_ge(fp, 3 * part + 3)
                scale(fx, fpow[3], a, b).then_inc(fx_ready, 1)
                dve.wait_ge(fx_ready, part + 1)

            def route(n, k, numbers, decided, ready):
                d, v = dec[:, 0:n, :], walk[:, 0:n, :]
                logits = psum[:, k * BANK:k * BANK + n * S].rearrange("p (f n) -> p f n", f=n)
                half = LEAVES // 2
                nc.vector.tensor_scalar(d[:, :, 0:half - 1], logits[:, :, 0:half - 1], 0.0, None, ALU.is_gt)
                nc.vector.scalar_tensor_tensor(out=v, in0=logits[:, :, half - 1:NODES], scalar=0.0,
                                               in1=even_ids[:, :].unsqueeze(1).to_broadcast([P, n, half]),
                                               op0=ALU.is_gt, op1=ALU.add).then_inc(*decided[0:2])
                dve.wait_ge(decided[0], decided[2])
                for level in reversed(range(DEPTH - 1)):
                    st = 2 ** (DEPTH - 1 - level)
                    link(nc.vector.copy_predicated(v[:, :, 0:half:st], d[:, :, 2 ** level - 1:2 ** (level + 1) - 1],
                                                   v[:, :, st // 2:half:st]))
                nc.vector.tensor_copy(numbers, v[:, :, 0]).then_inc(*ready[0:2])
                dve.wait_ge(ready[0], ready[2])

            def walk_of(b):
                dve.wait_ge(lg_ps, b + 1)
                route(6, 0, leaf_no[b][:, :], (dec_ready, 1, b + 1), (idx_ready, 1, b + 1))

            def hidden(g):
                b, s, f = ORDER[g]
                src = fy[b][:, s, :] if f == 3 else fx[:, SUB * b + s, :]
                dve.wait_ge(rows1_in[g % RING1], 16 * (g // RING1 + 1))
                if g >= 4:
                    dve.wait_ge(fg_ready, g - 3)
                r = leaf1[g % RING1]
                for l in range(LW):
                    w = r[:, l * E:(l + 1) * E]
                    i = nc.vector.tensor_tensor_reduce(w, w, src, 1.0, r[:, LW * E + l:LW * E + l + 1], ALU.mult, ALU.add,
                                                       hid[g % 4][:, l:l + 1])
                i.then_inc(fh_ready, 1)

            def add_leaf(g):
                b, s, f = ORDER[g]
                dve.wait_ge(leaf_done, g + 1)
                xb = x[:, SUB * b + s, :]
                nc.vector.tensor_tensor(xb, xb, bank(6 + g % 2, 0, P), ALU.add).then_inc(leaf_added, 1)

            def score_max(b):
                dve.wait_ge(fs_ps, b + 1)
                link(nc.vector.tensor_reduce(frow[:, :], bank(5).rearrange("p (s n) -> p s n", s=SUB), AX.X, ALU.max))
                nc.vector.tensor_scalar(fneg[:, :], frow[:, :], -float(E) ** -0.5, None, ALU.mult).then_inc(fmax_ready, 1)

            def attend(b):
                dve.wait_ge(att_ready, SUB * (b + 1))
                link(nc.vector.reciprocal(frec[:, :], fsum[:, :]))
                dve.wait_ge(fy_ps, b + 1)
                for s in range(SUB):
                    i = nc.vector.scalar_tensor_tensor(out=fy[b][:, s, :], in0=bank(3, s * P, s * P + P),
                                                       scalar=frec[:, s:s + 1], in1=fx[:, SUB * b + s, :],
                                                       op0=ALU.mult, op1=ALU.add)
                i.then_inc(fy_ready, 1)
                dve.wait_ge(fy_ready, b + 1)

            def ffn():
                dve.wait_ge(x_ready, 2 * B)
                ffn_norm(1, 2 * SUB, T)
                for what, i in STAGES_V:
                    if what == "next":
                        norm(i)
                    elif what == "leaf":
                        hidden(i)
                        if i >= 2 and last_tree(i - 2):
                            add_leaf(i - 2)
                    elif what == "route":
                        walk_of(i)
                    elif what == "weigh":
                        score_max(i)
                    elif what == "attend":
                        attend(i)
                    elif what == "route_f":
                        dve.wait_ge(lgf_ps, i + 1)
                        route(2, 3, leaf_nof[i][:, :], (decf_ready, 1, i + 1), (idxf_ready, 1, i + 1))
                add_leaf(len(ORDER) - 2)
                norm(NEXT[-1] + 1)
                add_leaf(len(ORDER) - 1)

            def peer_norm(part, a, b):
                moments(x, a, b)
                dve.wait_ge(in_keys, 320)
                nc.vector.tensor_scalar(fpow[0][:, a:b], fmean[:, a:b, 1], 1e-5, None, ALU.add).then_inc(pv2, 1)
                dve.wait_ge(pp2, 2 * part + 1)
                link(scale(x, fpow[1], a, b))
                moments(fx, a, b)
                m, q, n = fmean[:, a:b, 0], fpow[2][:, a:b], fpow[3][:, a:b]
                link(nc.vector.tensor_tensor(q, m, m, ALU.mult))
                link(nc.vector.tensor_tensor(q, q, fmean[:, a:b, 1], ALU.add))
                nc.vector.tensor_scalar(q, q, float(E), None, ALU.mult).then_inc(pv2, 1)
                dve.wait_ge(pp2, 2 * part + 2)
                link(nc.vector.tensor_scalar(n, n, 1e-12, None, ALU.max))
                link(nc.vector.reciprocal(n, n))
                link(nc.vector.tensor_scalar(n, n, float(E) ** 0.5, None, ALU.mult))
                for t in range(a, b):
                    i = nc.vector.scalar_tensor_tensor(out=fx[:, t, :], in0=fx[:, t, :], scalar=fpow[3][:, t:t + 1],
                                                       in1=gamma_sb[:, :], op0=ALU.mult, op1=ALU.mult)
                i.then_inc(px_ready, 1)
                dve.wait_ge(px_ready, part + 1)

            def topk_step(t, j):
                st = sim[:, t, :, :]
                tp = top[t]

                def best8(out, src, n):
                    for g in range(n):
                        i = nc.vector.max(out[g], src[g])
                    link(i)

                if j == 0:
                    dve.wait_ge(sim_ready, t + 1)
                    best8([best[:, g, 0:8] for g in range(16)], [st[:, g, :] for g in range(16)], 16)
                elif j == 1:
                    for g in range(16):
                        i = nc.vector.match_replace(simw[:, g, :], best[:, g, 0:8], st[:, g, :], -3e38)
                    link(i)
                elif j == 2:
                    best8([best[:, g, 8:16] for g in range(16)], [simw[:, g, :] for g in range(16)], 16)
                elif j == 3:
                    off = 0
                    for a in range(8):
                        n = NCAND[a]
                        nc.vector.tensor_tensor(pairs[:, :, off:off + n], best[:, 0:PH, a:a + 1].to_broadcast([P, PH, n]),
                                                best[:, PH:2 * PH, 0:n], ALU.add)
                        off += n
                    link(nc.vector.tensor_tensor(pairs[:, :, off:CAND], best[:, 0:PH, 8:TOPK],
                                                 best[:, PH:2 * PH, 0:1].to_broadcast([P, PH, 8]), ALU.add))
                elif j == 4:
                    best8([tp[:, g, 0:8] for g in range(PH)], [pairs[:, g, :] for g in range(PH)], PH)
                elif j == 5:
                    for g in range(PH):
                        i = nc.vector.match_replace(pairw[:, g, :], tp[:, g, 0:8], pairs[:, g, :], -3e38)
                    link(i)
                else:
                    best8([tp[:, g, 8:16] for g in range(PH)], [pairw[:, g, :] for g in range(PH)], PH)
                    link(nc.vector.tensor_scalar(tneg[:, t, :], tp[:, :, 0], -1.0, None, ALU.mult))
                    nc.vector.tensor_tensor(texp[t], tp, tp[:, :, 0:1].to_broadcast([P, PH, TOPK]),
                                            ALU.subtract).then_inc(tdif_ready, 1)

            def weight_sum(t):
                dve.wait_ge(texp_ready, t + 1)
                if t >= 2:
                    dve.wait_ge(diag_ready, 4 * (t - 1))
                link(nc.vector.tensor_reduce(tsum[:, :], texp[t], AX.X, ALU.add))
                nc.vector.reciprocal(trec[t % 2][:, :], tsum[:, :]).then_inc(trec_ready, 1)

            def peer():
                dve.wait_ge(x_ready, 4 * B)
                peer_norm(1, 2 * SUB, T)
                for i in range(AHEAD):
                    topk_step(i // 7, i % 7)
                weight_sum(0)

                def mix(t):
                    dve.wait_ge(mix_ps, PH * (t + 1))
                    dve.wait_ge(unit_ready, UNITS)
                    if t >= 1:
                        dve.wait_ge(po_ps, t)
                    st = psum[:, (t % 2) * 2 * BANK:((t % 2) * 2 + 2) * BANK].rearrange("p (c n) -> p c n", c=8)
                    nc.vector.tensor_tensor(mixed, st, hg[:, :, t * P:t * P + P], ALU.mult).then_inc(mixed_ready, 1)

                def add(t):
                    dve.wait_ge(po_ps, t + 1)
                    nc.vector.tensor_tensor(x[:, t, :], bank((t % 2) * 2, 0, P), x[:, t, :], ALU.add).then_inc(tile_ready, 1)

                for t in range(T):
                    for h in range(PH):
                        k = t * PH + h
                        dve.wait_ge(e_ready, k + 1)
                        if k == 0:
                            dve.wait_ge(sim_ps, T)
                        if k >= 3:
                            dve.wait_ge(mix_ps, k - 2)
                        nc.vector.scalar_tensor_tensor(out=picked[k % 3], in0=grid[k % 3],
                                                       scalar=top[t][:, h, TOPK - 1:TOPK],
                                                       in1=psum[:, (4 + 2 * (k % 2)) * BANK:(6 + 2 * (k % 2)) * BANK],
                                                       op0=ALU.is_ge, op1=ALU.mult).then_inc(picked_ready, 1)
                        for i in CHOICES.get(k, []):
                            topk_step(i // 7, i % 7)
                        if t + 1 < T and h == 3:
                            weight_sum(t + 1)
                        if t >= 1 and h == 2:
                            mix(t - 1)
                        if t >= 1 and h == 5:
                            add(t - 1)
                mix(T - 1)
                add(T - 1)

            run(*RUNS[0])
            ffn()
            run(*RUNS[1])
            peer()

        @block.tensor
        def _(pe):
            def bias_of(a, b):
                return bias_p[0:3, a:b]

            BIAS = {(0, 0): 0, (0, 1): 1, (0, 2): 2, (0, 3): 3, (1, 0): 4, (1, 1): 5, (1, 2): 6, (1, 3): 7, (3, 3): 8}

            def project(o, lhs, rhs, key, by_row):
                r = BIAS.get(key)
                i = nc.tensor.matmul(o, lhs, rhs, start=True, stop=r is None)
                if r is None:
                    return i
                bias = bias_of(r * P, r * P + P)
                if by_row:
                    return nc.tensor.matmul(o, bias, ones[0:3, :], start=False, stop=True)
                return nc.tensor.matmul(o, ones[0:3, 0:P], bias, start=False, stop=True)

            def pre_x(n):
                pe.wait_ge(xn_ready, n + 1)
                if n >= 1:
                    pe.wait_ge(v_ready, n)
                if tails_ahead(n):
                    pe.wait_ge(ot_ready, tails_ahead(n))
                for s in range(SUB):
                    i = nc.tensor.transpose(bank(4, s * P, s * P + P), xn[n % 3][:, s, :], identf[:, :])
                i.then_inc(xt_ps, 1)

            def kv_of(n):
                return ctx_t[:, batch(n) * S:(batch(n) + 1) * S] if stage(n) in (1, 3) else xn_t[n % 2][:, :]

            def pre_qk(n):
                a = stage(n)
                pe.wait_ge(xt_ready, n + 1)
                if n >= 1:
                    pe.wait_ge(qk_ready, n)
                if tails_ahead(n):
                    pe.wait_ge(x_ready, tails_ahead(n))
                if n >= B and turns_ahead(n) > 0:
                    pe.wait_ge(mt_ready, turns_ahead(n))
                for w, src in ((0, xn_t[n % 2][:, :]), (1, kv_of(n))):
                    i = project(bank(5, w * S, w * S + S), w_sb[:, 4 * a + w, :], src, (a, w), True)
                i.then_inc(qk_ps, 1)

            def pre_v(n):
                a, kv = stage(n), kv_of(n)
                for s in range(SUB):
                    i = project(bank(4, S + s * P, S + s * P + P), kv[:, s * P:s * P + P], w_sb[:, 4 * a + 2, :],
                                (a, 2), False)
                i.then_inc(v_ps, 1)

            def pre(n):
                pre_x(n)
                pre_qk(n)
                pre_v(n)

            def turn_out(n):
                pe.wait_ge(osb_ready, n - B + 1)
                pe.wait_ge(x_ready, n)
                pe.wait_ge(v_ready, pres_ahead(n))
                pe.wait_ge(mt_ready, min(n + 2, run_of(n)[1] + 1) - B)
                pe.wait_ge(qk_ready, min(n + 4, run_of(n)[1] + 1))
                for s in range(SUB):
                    for g in range(H // 4):
                        i = nc.tensor.transpose(bank(5 - s, g * P, g * P + P), o_sb[:, g, s * P:s * P + P], identf[:, :])
                i.then_inc(or_ps, 1)

            def tail_a(n):
                pe.wait_ge(o_ready, n + 1)
                if n < B:
                    pe.wait_ge(v_ready, B)
                    if n >= 1:
                        pe.wait_ge(ot_ready, n)
                for s in range(SUB):
                    i = nc.tensor.transpose(bank(tail_bank(n), s * P, s * P + P), o_n[:, s, :], identf[:, :])
                i.then_inc(ot_ps, 1)

            def tail_b(n):
                pe.wait_ge(ot_ready, n + 1)
                if n >= 1:
                    pe.wait_ge(x_ready, n)
                for s in range(SUB):
                    i = project(bank(tail_bank(n) + 1, s * P, s * P + P), o_t[:, s * P:s * P + P], w_sb[:, 4 * stage(n) + 3, :],
                                (stage(n), 3), False)
                i.then_inc(y_ps, 1)

            def score_rows(n, h):
                k = (n - B) * H + h
                if h == 0:
                    pe.wait_ge(stk_ready[n % 3], 16 * 12 * placed(n))
                if k >= 2:
                    pe.wait_ge(rows_max, k - 1)
                t = stk[n % 3]
                q, kk = t[0:KS, h, 0, :], t[0:KS, h, 1, :]
                if stage(n) == 2:
                    nc.tensor.matmul(bank(k % 2, 0, P), q[:, 0:P], kk[:, 0:P], start=True, stop=False)
                    nc.tensor.matmul(bank(k % 2, 0, P), identb[:, :], causal_q[:, :], start=False, stop=True)
                    nc.tensor.matmul(bank(k % 2, P, P + S), q[:, P:S], kk, start=True, stop=False)
                    i = nc.tensor.matmul(bank(k % 2, S, S + P), identb[:, :], causal_q[:, :], start=False, stop=True)
                else:
                    for s in range(SUB):
                        i = nc.tensor.matmul(bank(k % 2, s * S, s * S + S), q[:, s * P:s * P + P], kk, start=True, stop=True)
                i.then_inc(rows_ps, 1)

            def score_cols(n, h):
                k = (n - B) * H + h
                if h == 0:
                    pe.wait_ge(max_in[n % 3], 16 * placed(n))
                    if n in (B, 2 * B):
                        pe.wait_ge(ones_ready, 16 * 3 * (n // B))
                if k >= 2:
                    pe.wait_ge(probs_ready, k - 1)
                t = stk[n % 3]
                q, kk = t[0:KM, h, 0, :], t[0:KM, h, 1, :]
                causal = stage(n) == 2
                for c in range(SUB):
                    q0 = P if causal and c else 0
                    o = bank(2 + k % 2, c * S, c * S + S - q0)
                    i = nc.tensor.matmul(o, kk[:, c * P:c * P + P], q[:, q0:S], start=True, stop=not causal)
                    if causal:
                        i = nc.tensor.matmul(o[:, 0:P], identb[:, :], causal_k[:, :], start=False, stop=True)
                i.then_inc(cols_ps, 1)

            def values(n, h):
                k = (n - B) * H + h
                pe.wait_ge(probs_ready, k + 1)
                if h == 0:
                    pe.wait_ge(v_ready, n + 1)
                    if n > B:
                        pe.wait_ge(osb_ready, n - B)
                r, col = 32 * (h % 4), (h // 4) * S
                for c in range(SUB):
                    q0 = P if stage(n) == 2 and c else 0
                    o = psum[r:r + VW, 6 * BANK + col + q0:6 * BANK + col + S]
                    i = nc.tensor.matmul(o, vaug[n % 4][:, c, h, :], probs[k % 4][:, c * S:c * S + S - q0],
                                         start=(c == 0), stop=(c == SUB - 1))
                i.then_inc(pv_ps, 1)

            def max_turn(n):
                pe.wait_ge(mparts_ready, n - B + 1)
                first, last = run_of(n)
                pe.wait_ge(qk_ready, min(n + 2, last + 1))
                pe.wait_ge(x_ready, max(n - 1, first))
                for s in range(SUB):
                    i = nc.tensor.transpose(mt_bank[:, s * P:s * P + P],
                                            mparts[n % 2][:, s, :, :].rearrange("p a h -> p (a h)"), identb[:, :])
                i.then_inc(mt_ps, 1)

            pe.wait_ge(consts, 1)
            pe.wait_ge(in_w, 48)
            pre_x(0)
            pe.wait_ge(bias_ready, 1)
            pre_qk(0)
            pre_v(0)
            for n in range(B):
                if n >= 1:
                    pe.wait_ge(qft_ready, n)
                    pe.wait_ge(zk_ready, n)
                else:
                    pe.wait_ge(feat_ready, 1)
                pe.wait_ge(qk_ready, n + 1)
                fw = feat_w[:, :, :].rearrange("p h m -> p (h m)")
                for w in range(2):
                    for s in range(SUB):
                        nc.tensor.matmul(bank(2 * w + s), qk_f[n % 2][:, w, s * P:s * P + P], fw, start=True, stop=True)
                pe.wait_ge(sq_ready, n + 1)
                for w in range(2):
                    for s in range(SUB):
                        j = (w * SUB + s) * H
                        i = nc.tensor.matmul(bank(7, j, j + H), sq[:, w, s * P:s * P + P], half16[:, :], start=True, stop=True)
                i.then_inc(dd_ps, 1)
                if n + 1 < B:
                    pre(n + 1)
                pe.wait_ge(eq_ready, n + 1)
                for s in range(SUB):
                    for g in range(HG):
                        j = (s * HG + g) * P
                        i = nc.tensor.transpose(psum[:, j:j + P], eq[:, j:j + P], identf[:, :])
                i.then_inc(qft_ps, 1)

            def keys_values(n):
                pe.wait_ge(kf_ready, n + 1)
                if n == 0:
                    pe.wait_ge(zk_ready, B)
                    pe.wait_ge(qft_ready, B)
                    pe.wait_ge(v_ready, B)
                else:
                    pe.wait_ge(cx_ready, n)
                for g in range(HG):
                    for s in range(SUB):
                        i = nc.tensor.matmul(bank(3, g * 36, g * 36 + 36), kf[n % 2][:, s, g * P:g * P + P],
                                             vaug[n % 4][:, s, g * HG:g * HG + HG, 0:D + 1],
                                             start=(s == 0), stop=(s == SUB - 1))
                i.then_inc(cx_ps, 1)

            pe.wait_ge(in_ctx, 48)
            pe.wait_ge(zk_ready, B)
            for t in range(T):
                j = (2 + 4 * (t // 4)) * BANK + t % 4 * P
                i = nc.tensor.transpose(psum[:, j:j + P], ctx_rows[:, t, :], identf[:, :])
                if t % 4 == 3:
                    i.then_inc(ctxt_ps, 1)
            keys_values(0)
            for n in range(B):
                pe.wait_ge(cx_ready, n + 1)
                if n >= 1:
                    pe.wait_ge(o_ready, n)
                for s in range(SUB):
                    for g in range(HG):
                        i = nc.tensor.matmul(bank_o(s, g * HG, HG), qf_t[:, SUB * n + s, g, :], ctx_m[:, g, :],
                                             start=True, stop=True)
                i.then_inc(pv_ps, 1)
                if n >= 1:
                    tail_b(n - 1)
                if n + 1 < B:
                    keys_values(n + 1)
                tail_a(n)
                if n == 2:
                    pe.wait_ge(bias_ready, 2)
                    pe.wait_ge(ctxt_ready, 2)
                if n >= 2:
                    pre(B + n - 2)
            tail_b(B - 1)

            def run(first, last):
                for h in range(H):
                    score_rows(first, h)
                max_turn(first)
                for n in range(first, last + 1):
                    if n > first:
                        values(n - 1, H - 2)
                    if n + 2 <= last:
                        pre_x(n + 2)
                    if n > first:
                        values(n - 1, H - 1)
                    for h in range(H):
                        score_cols(n, h)
                        if n + 1 <= last:
                            for hh in ROWS_AT[h]:
                                score_rows(n + 1, hh)
                            if h == TURN:
                                max_turn(n + 1)
                        if n + 2 <= last and h == 1:
                            pre_v(n + 2)
                        if h >= 2:
                            values(n, h - 2)
                        if n + 2 <= last and h == 0:
                            pre_qk(n + 2)
                        if n > first and h == 3:
                            turn_out(n - 1)
                        if n > first and h == 6:
                            tail_a(n - 1)
                        if n > first and h == 9:
                            tail_b(n - 1)
                values(last, H - 2)
                values(last, H - 1)
                if first == B:
                    turn_fx(0)
                else:
                    turn_px(0)
                turn_out(last)
                if first == B:
                    tree_logits(0)
                else:
                    unit(0)
                tail_a(last)
                if first > B:
                    unit(1)
                tail_b(last)

            def logits(s, f, src, o):
                o = o[:, 0:NODES]
                nc.tensor.matmul(o, src[:, s * P:s * P + P], nodes_sb[:, f, :], start=True, stop=False)
                n0 = 9 * P + f * NODES
                return nc.tensor.matmul(o, ones[0:3, 0:P], bias_of(n0, n0 + NODES), start=False, stop=True)

            def turn_fx(b):
                pe.wait_ge(fx_ready, b // 2 + 1)
                if b >= 3:
                    pe.wait_ge(fyt_ready, b - 2)
                for s in range(SUB):
                    j = (4 if b else 3) * BANK + s * P
                    i = nc.tensor.transpose(psum[:, j:j + P], fx[:, SUB * b + s, :], identf[:, :])
                i.then_inc(fxt_ps, 1)

            def tree_logits(b):
                if b == 0:
                    pe.wait_ge(in_tab, 32)
                    pe.wait_ge(bias_ready, 3)
                else:
                    pe.wait_ge(dec_ready, b)
                pe.wait_ge(fxt_ready, b + 1)
                for f in range(3):
                    for s in range(SUB):
                        i = logits(s, f, fx_t, bank(f, s * S, s * S + S))
                i.then_inc(lg_ps, 1)

            def ffn():
                pe.wait_ge(ot_ready, 2 * B)

                def leaf(g):
                    b, s, f = ORDER[g]
                    r = leaf2[g % RING2]
                    o = bank(6 + g % 2, 0, P)
                    if g >= 2:
                        last = last_tree(g - 2)
                        pe.wait_ge(leaf_added if last else leaf_kept, leaves_upto(g - 2, last))
                    for l in range(LW + 1):
                        if l < LW and l % 4 == 0:
                            pe.wait_ge(scaled, 4 * g + l // 4 + 1)
                        w = r[:, l * E:(l + 1) * E]
                        ab = (w, identf[:, :]) if f < 2 else (identf[:, :], w)
                        i = nc.tensor.matmul(o, *ab, start=(l == 0), stop=(l == LW and f < 3))
                    if f == 3:
                        i = nc.tensor.matmul(o, identf[:, :], fy[b][:, s, :], start=False, stop=True)
                    i.then_inc(leaf_done, 1)

                for what, b in STAGES:
                    if what == "turn":
                        turn_fx(b)
                        tree_logits(b)
                    elif what == "next":
                        pre(b)
                    elif what == "leaf":
                        leaf(b)
                    elif what == "score":
                        pe.wait_ge(leaf_kept, 3 * SUB * (b + 1))
                        if b >= 1:
                            pe.wait_ge(at_ready, b)
                        t = fqk_t[b % 2]
                        for s in range(SUB):
                            i = nc.tensor.matmul(bank(5, s * S, s * S + S), t[:, 0, s * P:s * P + P], t[:, 1, :],
                                                 start=True, stop=True)
                        i.then_inc(fs_ps, 1)
                    elif what == "mix":
                        pe.wait_ge(att_ready, SUB * (b + 1))
                        for s in range(SUB):
                            for c in range(SUB):
                                j = (s * SUB + c) * P
                                i = nc.tensor.transpose(bank(5, j, j + P), att[:, s, c * P:c * P + P], identf[:, :])
                        i.then_inc(at_ps, 1)
                        pe.wait_ge(at_ready, b + 1)
                        if b >= 1:
                            pe.wait_ge(decf_ready, b)
                        for s in range(SUB):
                            for c in range(SUB):
                                i = nc.tensor.matmul(bank(3, s * P, s * P + P), att_t[:, s * SUB + c, :],
                                                     fval[b % 2][:, c, :], start=(c == 0), stop=(c == SUB - 1))
                        i.then_inc(fy_ps, 1)
                    elif what == "turn_f":
                        pe.wait_ge(fy_ready, b + 1)
                        if b + 2 < B:
                            pe.wait_ge(fxt_ready, b + 3)
                        for s in range(SUB):
                            i = nc.tensor.transpose(bank(4, s * P, s * P + P), fy[b][:, s, :], identf[:, :])
                        i.then_inc(fyt_ps, 1)
                        pe.wait_ge(fyt_ready, b + 1)
                        for s in range(SUB):
                            i = logits(s, 3, fy_t, bank(3, s * S, s * S + S))
                        i.then_inc(lgf_ps, 1)

            def turn_px(i):
                pe.wait_ge(px_ready, i + 1)
                for t in range(2 * SUB):
                    j = (7 if i else 3) * BANK + t * P
                    j = nc.tensor.transpose(psum[:, j:j + P], fx[:, 2 * SUB * i + t, :], identf[:, :])
                j.then_inc(pxt_ps, 1)

            def unit(u):
                b = u // 2 % B
                if u == 0:
                    pe.wait_ge(in_keys, 320)
                pe.wait_ge(pxt_ready, b // 2 + 1)
                if u >= 2:
                    pe.wait_ge(unit_ready, u - 1)
                w = wq_sb if u < 2 * B else down_sb
                for c in range(4):
                    cc = u % 2 * 4 + c
                    i = nc.tensor.matmul(unit_bank(u)[:, c * S:(c + 1) * S], w[:, cc * P:cc * P + P], px_of(b),
                                         start=True, stop=True)
                i.then_inc(unit_ps, 1)

            def sims(t):
                b, s = t // SUB, t % SUB
                pe.wait_ge(unit_ready, 2 * b + 2)
                if b >= 1:
                    pe.wait_ge(sim_ready, t - SUB + 1)
                for c in range(8):
                    i = nc.tensor.matmul(bank(5 + s, c * 2 * PK, (c + 1) * 2 * PK),
                                         qp_t[b % 2][:, c, s * P:s * P + P], keys_sb[:, c, :], start=True, stop=True)
                i.then_inc(sim_ps, 1)

            def peer():
                pe.wait_ge(ot_ready, 4 * B)
                pe.wait_ge(x_ready, 4 * B)
                for u in range(2, UNITS):
                    if u == 4:
                        turn_px(1)
                    unit(u)
                    if u < T + 2:
                        sims(u - 2)
                pe.wait_ge(unit_ready, UNITS)

                def out_of(t):
                    pe.wait_ge(mixed_ready, t + 1)
                    for c in range(8):
                        i = nc.tensor.matmul(bank((t % 2) * 2, 0, P), mixed[:, c, :], up_sb[:, c, :],
                                             start=(c == 0), stop=(c == 7))
                    i.then_inc(po_ps, 1)

                for t in range(T):
                    if t >= 2:
                        pe.wait_ge(tile_ready, t - 1)
                    for h in range(PH):
                        k = t * PH + h
                        pe.wait_ge(picked_ready, k + 1)
                        pe.wait_ge(diag_ready, 4 * t + h // 2 + 1)
                        for c in range(8):
                            o = ((t % 2) * 2) * BANK + c * P
                            i = nc.tensor.matmul(psum[:, o:o + P], picked[k % 3][:, c * P:c * P + P], diag[t % 2][:, h, :],
                                                 start=(h == 0 and c % 4 == 0), stop=(h == PH - 1),
                                                 skip_group_check=True)
                        i.then_inc(mix_ps, 1)
                        if t >= 1 and h == 3:
                            out_of(t - 1)
                out_of(T - 1)

            pe.wait_ge(consts, 2)
            pe.wait_ge(ot_ready, B)
            pe.wait_ge(x_ready, B)
            run(*RUNS[0])
            ffn()
            run(*RUNS[1])
            peer()


def kernel(**a):
    import numpy as np
    import concourse.bacc as bacc
    from concourse.bass_utils import run_bass_kernel_spmd

    a = {k: np.asarray(v) for k, v in a.items()}

    def by_width(w):
        return w.reshape(w.shape[:-1] + (H, D)).swapaxes(-1, -2).reshape(w.shape)

    ws = []
    for names in (("L0_attn_Wq", "L0_attn_Wk", "L0_attn_Wv", "L0_attn_Wo"),
                  ("L0_xattn_wq", "L0_xattn_wk", "L0_xattn_wv", "L0_xattn_wo"),
                  ("L1_attn_Wq", "L1_attn_Wk", "L1_attn_Wv", "L1_attn_Wo"),
                  ("L1_xattn_Wq", "L1_xattn_Wk", "L1_xattn_Wv", "L1_xattn_Wo")):
        q, k, v, o = (a[n].T for n in names)
        ws += [by_width(q), by_width(k), v, o]
    bias = [by_width(a["L0_attn_bq"]), by_width(a["L0_attn_bk"]), a["L0_attn_bv"], a["L0_attn_bo"],
            by_width(a["L0_xattn_bq"]), by_width(a["L0_xattn_bk"]), a["L0_xattn_bv"], a["L0_xattn_bo"],
            a["L1_xattn_bo"]]
    kinds = "qkvf"

    def first(c):
        w1 = a[f"L0_ffn_{c}_w1"].transpose(0, 2, 1).reshape(LEAVES, LW * E)
        return np.concatenate([w1, a[f"L0_ffn_{c}_b1"]], axis=1)

    def second(c):
        return np.concatenate([a[f"L0_ffn_{c}_w2"].reshape(LEAVES, LW * E), a[f"L0_ffn_{c}_b2"]], axis=1)

    ins = {
        "x_in": a["x"], "ctx_in": a["ctx_1024"], "mask_in": a["mask_BxS_ik0"],
        "attn_w": np.stack(ws), "attn_bias": np.concatenate(bias),
        "proj_t": np.repeat(a["L0_attn_proj"].T, H, axis=0),
        "node_w": np.stack([a[f"L0_ffn_{c}_nw"].T for c in kinds], axis=1),
        "node_b": np.concatenate([a[f"L0_ffn_{c}_nb"] for c in kinds]),
        "tab1_q": first("q"), "tab1_k": first("k"), "tab1_v": first("v"), "tab1_f": first("f"),
        "tab2_q": second("q"), "tab2_k": second("k"), "tab2_v": second("v"), "tab2_f": second("f"),
        "gamma_in": a["L1_ffn_gamma"], "peer_wq": a["L1_ffn_wq"].T,
        "peer_keys": a["L1_ffn_keys"].transpose(2, 0, 3, 1),
        "table_down": a["L1_ffn_table_down"][:EXPERTS].T, "table_up": a["L1_ffn_table_up"][:EXPERTS],
    }
    nc = bacc.Bacc("TRN2", target_bir_lowering=False, num_devices=1)
    arrays, aps = {}, []
    for name, v in ins.items():
        v = np.ascontiguousarray(v)
        arrays[name] = v
        aps.append(nc.dram_tensor(name, v.shape, mybir.dt.from_np(v.dtype), kind="ExternalInput").ap())
    out = nc.dram_tensor("out", (B, S, E), mybir.dt.float32, kind="ExternalOutput").ap()
    decoder_program(nc, *aps, out)
    r = run_bass_kernel_spmd(nc, [arrays], core_ids=[0])
    return r.results[0]["out"]
```
